# Optimizing a Trainium2 kernel written in Bass

```python
import numpy as np
import jax
import jax.numpy as jnp

def _softmax(x, axis=-1):
    return jax.nn.softmax(x, axis=axis)

def _gelu(x):
    return jax.nn.gelu(x, approximate=True)

def _silu(x):
    return jax.nn.silu(x)

def _sigmoid(x):
    return jax.nn.sigmoid(x)

def _layernorm(x, axis=-1, eps=1e-05):
    m = jnp.mean(x, axis=axis, keepdims=True)
    v = jnp.var(x, axis=axis, keepdims=True)
    return (x - m) / jnp.sqrt(v + eps)

def _scatter_add(tgt, idx, src, axis=0):
    return tgt.at[idx].add(src)

def _segment_sum(src, seg, n):
    return jax.ops.segment_sum(src, seg, n)
kernel_name = 'mk_xattn_ffn_d4_seqx_r8_e8678c'

def setup_inputs(seed: int=0):
    np.random.seed(seed)
    _w = jnp.asarray

    def _rec_inputs():
        import jax
        import jax.numpy as jnp
        _rk = jax.random.key(seed)
        x = -0.0002928 + 1 * jax.random.normal(jax.random.fold_in(_rk, 1), (64, 64, 128), jnp.float32)
        _lenS = 64 - jax.random.randint(jax.random.fold_in(_rk, 7), (64,), 0, max(1, 64 // 4) + 1, jnp.int32)
        _lenS2 = 64 - jax.random.randint(jax.random.fold_in(_rk, 8), (64,), 0, max(1, 64 // 4) + 1, jnp.int32)
        _ctx_1024P = jax.random.normal(jax.random.fold_in(_rk, 11), (64, 16, 128), jnp.float32)
        _ctx_1024c = jax.random.dirichlet(jax.random.fold_in(_rk, 511), 0.3 * jnp.ones((16,), jnp.float32), (64, 64))
        _ctx_1024t = jnp.einsum('bsk,bkd->bsd', _ctx_1024c, _ctx_1024P)
        _ctx_1024t = _ctx_1024t * jax.lax.rsqrt(jnp.mean(jnp.square(_ctx_1024t)) + 1e-12) * 0.953939
        ctx_1024 = -1.39393e-06 + 0.999914 * (_ctx_1024t + 0.3 * jax.random.normal(jax.random.fold_in(_rk, 611), (64, 64, 128), jnp.float32))
        return (x, ctx_1024)
    x, ctx_1024 = _rec_inputs()

    def _L0_xattn_setup():
        import jax, jax.numpy as jnp
        import numpy as np
        import math
        CHANNELS = 64
        N_HEADS = 8
        K_CH = CHANNELS // N_HEADS
        ROPE_D = int(K_CH * 0.5)
        BASE = 1250

        def _rope(x):
            d = ROPE_D
            t = x.shape[2]
            theta = 1.0 / BASE ** (jnp.arange(0, d, 2, dtype=jnp.float32) / d)
            ang = jnp.arange(t, dtype=jnp.float32)[:, None] * theta[None, :]
            ang = jnp.concatenate([ang, ang], axis=-1)
            cos = jnp.cos(ang)[None, None, :, :].astype(x.dtype)
            sin = jnp.sin(ang)[None, None, :, :].astype(x.dtype)
            x_rope, x_pass = (x[..., :d], x[..., d:])
            neg_half = jnp.concatenate([-x_rope[..., d // 2:], x_rope[..., :d // 2]], axis=-1)
            return jnp.concatenate([x_rope * cos + neg_half * sin, x_pass], axis=-1)

        def _split_heads(y):
            b, _, t = y.shape
            return y.reshape(b, N_HEADS, K_CH, t).transpose(0, 1, 3, 2)
        key = jax.random.key(seed)
        ks = jax.random.split(key, 10)
        B, T = (8, 128)
        w_scale = 1.0 / math.sqrt(CHANNELS)
        return {'x': jax.random.normal(ks[0], (B, CHANNELS, T), jnp.float32), 'c': jax.random.normal(ks[1], (B, CHANNELS, T), jnp.float32), 'Wq': jax.random.normal(ks[2], (CHANNELS, CHANNELS), jnp.float32) * w_scale, 'bq': jax.random.normal(ks[3], (CHANNELS,), jnp.float32) * 0.02, 'Wk': jax.random.normal(ks[4], (CHANNELS, CHANNELS), jnp.float32) * w_scale, 'bk': jax.random.normal(ks[5], (CHANNELS,), jnp.float32) * 0.02, 'Wv': jax.random.normal(ks[6], (CHANNELS, CHANNELS), jnp.float32) * w_scale, 'bv': jax.random.normal(ks[7], (CHANNELS,), jnp.float32) * 0.02, 'Wo': jax.random.normal(ks[8], (CHANNELS, CHANNELS), jnp.float32) * w_scale, 'bo': jax.random.normal(ks[9], (CHANNELS,), jnp.float32) * 0.02}
    _L0_xattn_all = _L0_xattn_setup()
    _L0_xattn_in = {k: v for k, v in _L0_xattn_all.items() if k in ('Wq', 'bq', 'Wk', 'bk', 'Wv', 'bv', 'Wo', 'bo')}
    del _L0_xattn_all

    def _L0_ffn_setup():
        import jax, jax.numpy as jnp
        import numpy as np
        from functools import partial
        HEADS = 16
        EPS = 1e-12

        def _l2_normalize(z):
            n = jnp.linalg.norm(z, axis=-1, keepdims=True)
            return z / jnp.maximum(n, EPS)
        key = jax.random.key(seed)
        kx, kq, kk, kv, ko, kf = jax.random.split(key, 6)
        B, S, D, L = (2, 256, 128, 128)
        scale = 0.02
        return {'x': jax.random.normal(kx, (B, S, D), dtype=jnp.float32), 'Wq': jax.random.normal(kq, (D, L), dtype=jnp.float32) * scale, 'Wk': jax.random.normal(kk, (D, L), dtype=jnp.float32) * scale, 'Wv': jax.random.normal(kv, (D, L), dtype=jnp.float32) * scale, 'Wo': jax.random.normal(ko, (L, D), dtype=jnp.float32) * scale, 'Wff': jax.random.normal(kf, (D, D), dtype=jnp.float32) * scale}
    _L0_ffn_all = _L0_ffn_setup()
    _L0_ffn_in = {k: v for k, v in _L0_ffn_all.items() if k in ('Wq', 'Wk', 'Wv', 'Wo', 'Wff')}
    del _L0_ffn_all

    def _L1_xattn_setup():
        import jax, jax.numpy as jnp
        import numpy as np
        DIM = 128
        HEADS = 16
        DS = 4
        key = jax.random.key(seed)
        ks = jax.random.split(key, 10)
        B, N, M = (2, 128, 512)
        s = 0.02
        return {'x': jax.random.normal(ks[0], (B, M, DIM), jnp.float32), 'l': jax.random.normal(ks[1], (B, N, DIM), jnp.float32), 'Wq': jax.random.normal(ks[2], (DIM, DIM), jnp.float32) * s, 'bq': jnp.zeros((DIM,), jnp.float32), 'Wk': jax.random.normal(ks[3], (DIM, DIM), jnp.float32) * s, 'bk': jnp.zeros((DIM,), jnp.float32), 'Wv': jax.random.normal(ks[4], (DIM, DIM), jnp.float32) * s, 'bv': jnp.zeros((DIM,), jnp.float32), 'Wo': jax.random.normal(ks[5], (DIM, DIM), jnp.float32) * s, 'bo': jnp.zeros((DIM,), jnp.float32)}
    _L1_xattn_all = _L1_xattn_setup()
    _L1_xattn_in = {k: v for k, v in _L1_xattn_all.items() if k in ('Wq', 'bq', 'Wk', 'bk', 'Wv', 'bv', 'Wo', 'bo')}
    del _L1_xattn_all

    def _L1_ffn_setup():
        import jax, jax.numpy as jnp
        import numpy as np
        TOP_K = 2

        def _route(x2d, gate_w, num_experts, top_k):
            scores = jax.nn.softmax((x2d @ gate_w.T).astype(jnp.float32), axis=1)
            top_scores, sel = jax.lax.top_k(scores, top_k)
            sel_flat = sel.reshape(-1)
            counts = jnp.bincount(sel_flat, length=num_experts)
            order = jnp.argsort(sel_flat, stable=True)
            top_scores_sorted = top_scores.reshape(-1)[order]
            token_idx = order // top_k
            return (top_scores_sorted, token_idx, counts)

        def _grouped_swiglu(xr, w1, w2, w3, eid):
            out = jnp.zeros((xr.shape[0], w2.shape[-1]), dtype=xr.dtype)
            for e in range(w1.shape[0]):
                xe = jnp.where((eid == e)[:, None], xr, 0.0)
                h = jax.nn.silu(xe @ w1[e]) * (xe @ w3[e])
                out = out + h @ w2[e]
            return out
        key = jax.random.key(seed)
        ks = jax.random.split(key, 5)
        bs, slen, dim, hidden, E = (2, 256, 128, 352, 8)
        x = jax.random.normal(ks[0], (bs, slen, dim), dtype=jnp.float32)
        gate_w = jax.random.normal(ks[1], (E, dim), dtype=jnp.float32) * 0.02
        w1 = jax.random.normal(ks[2], (E, dim, hidden), dtype=jnp.float32) * 0.02
        w2 = jax.random.normal(ks[3], (E, hidden, dim), dtype=jnp.float32) * 0.02
        w3 = jax.random.normal(ks[4], (E, dim, hidden), dtype=jnp.float32) * 0.02
        return {'x': x, 'gate_w': gate_w, 'w1': w1, 'w2': w2, 'w3': w3}
    _L1_ffn_all = _L1_ffn_setup()
    _L1_ffn_in = {k: v for k, v in _L1_ffn_all.items() if k in ('gate_w', 'w1', 'w2', 'w3')}
    del _L1_ffn_all

    def _L2_xattn_setup():
        import jax, jax.numpy as jnp
        import numpy as np
        DIM = 128
        NUM_HEADS = 8
        HEAD_DIM = 64
        INNER = NUM_HEADS * HEAD_DIM
        key = jax.random.key(seed)
        ks = jax.random.split(key, 7)
        B, N, M = (8, 64, 512)
        x = jax.random.normal(ks[0], (B, N, DIM), dtype=jnp.float32)
        context = jax.random.normal(ks[1], (B, M, DIM), dtype=jnp.float32)
        s_in = 1.0 / np.sqrt(DIM)
        s_inner = 1.0 / np.sqrt(INNER)
        Wq = jax.random.normal(ks[2], (DIM, INNER), dtype=jnp.float32) * s_in
        Wk = jax.random.normal(ks[3], (DIM, INNER), dtype=jnp.float32) * s_in
        Wv = jax.random.normal(ks[4], (DIM, INNER), dtype=jnp.float32) * s_in
        Wo = jax.random.normal(ks[5], (INNER, DIM), dtype=jnp.float32) * s_inner
        bo = jax.random.normal(ks[6], (DIM,), dtype=jnp.float32) * 0.01
        return {'x': x, 'context': context, 'Wq': Wq, 'Wk': Wk, 'Wv': Wv, 'Wo': Wo, 'bo': bo}
    _L2_xattn_all = _L2_xattn_setup()
    _L2_xattn_in = {k: v for k, v in _L2_xattn_all.items() if k in ('Wq', 'Wk', 'Wv', 'Wo', 'bo')}
    del _L2_xattn_all

    def _L2_ffn_setup():
        import jax, jax.numpy as jnp
        import numpy as np
        E = 8
        K = 2
        CAP_FACTOR = 1.0
        key = jax.random.key(seed)
        ks = jax.random.split(key, 5)
        B, T, C, H = (4, 256, 128, 512)
        x = jax.random.normal(ks[0], (B, T, C), dtype=jnp.float32)
        Wr = jax.random.normal(ks[1], (C, E), dtype=jnp.float32) * 0.02
        br = jnp.zeros((E,), jnp.float32)
        W1 = jax.random.normal(ks[2], (E, C, H), dtype=jnp.float32) * 0.02
        b1 = jnp.zeros((E, H), jnp.float32)
        W2 = jax.random.normal(ks[3], (E, H, C), dtype=jnp.float32) * 0.02
        b2 = jnp.zeros((E, C), jnp.float32)
        return {'x': x, 'Wr': Wr, 'br': br, 'W1': W1, 'b1': b1, 'W2': W2, 'b2': b2}
    _L2_ffn_all = _L2_ffn_setup()
    _L2_ffn_in = {k: v for k, v in _L2_ffn_all.items() if k in ('Wr', 'br', 'W1', 'b1', 'W2', 'b2')}
    del _L2_ffn_all

    def _L3_xattn_setup():
        import jax, jax.numpy as jnp
        import numpy as np
        E = 128
        NUM_HEADS = 16
        DK = E // NUM_HEADS
        EPS = 1e-05
        NEG_INF = -jnp.inf

        def layer_norm(x, g, b):
            mu = jnp.mean(x, axis=-1, keepdims=True)
            var = jnp.var(x, axis=-1, keepdims=True)
            return (x - mu) * jax.lax.rsqrt(var + EPS) * g + b

        def self_attn(x, Wq, Wk, Wv):
            Q, K, V = (x @ Wq, x @ Wk, x @ Wv)
            energy = jnp.einsum('bqd,bkd->bqk', Q, K)
            S = energy.shape[-1]
            lengths = jnp.sum(energy[:, 0] != 0, axis=-1)
            kidx = jnp.arange(S)
            pad = kidx[None, None, :] >= lengths[:, None, None]
            causal = kidx[None, :] < kidx[:, None]
            causal = (kidx[None, :] > kidx[:, None])[None]
            energy = jnp.where(pad | causal, NEG_INF, energy)
            score = jax.nn.softmax(energy / np.sqrt(DK), axis=-1)
            return jnp.einsum('bqk,bkd->bqd', score, V)

        def cross_attn(x, context, Wq, Wk, Wv):
            Q = x @ Wq
            K, V = (context @ Wk, context @ Wv)
            energy = jnp.einsum('bqd,bkd->bqk', Q, K)
            Sk = energy.shape[-1]
            lengths = jnp.sum(energy[:, 0] != 0, axis=-1)
            kidx = jnp.arange(Sk)
            pad = kidx[None, None, :] >= lengths[:, None, None]
            energy = jnp.where(pad, NEG_INF, energy)
            score = jax.nn.softmax(energy / np.sqrt(DK), axis=-1)
            return jnp.einsum('bqk,bkd->bqd', score, V)
        key = jax.random.key(seed)
        ks = jax.random.split(key, 12)
        B, S = (8, 256)
        s = 1.0 / np.sqrt(E)
        inp = {'x': jax.random.normal(ks[0], (B, S, E), jnp.float32), 'context': jax.random.normal(ks[1], (B, S, E), jnp.float32), 'Wq1': jax.random.normal(ks[2], (E, E), jnp.float32) * s, 'Wk1': jax.random.normal(ks[3], (E, E), jnp.float32) * s, 'Wv1': jax.random.normal(ks[4], (E, E), jnp.float32) * s, 'Wq2': jax.random.normal(ks[5], (E, E), jnp.float32) * s, 'Wk2': jax.random.normal(ks[6], (E, E), jnp.float32) * s, 'Wv2': jax.random.normal(ks[7], (E, E), jnp.float32) * s, 'fc1_w': jax.random.normal(ks[8], (E, E), jnp.float32) * s, 'fc1_b': jnp.zeros((E,), jnp.float32), 'fc2_w': jax.random.normal(ks[9], (E, E), jnp.float32) * s, 'fc2_b': jnp.zeros((E,), jnp.float32), 'ln1_g': jnp.ones((E,), jnp.float32), 'ln1_b': jnp.zeros((E,), jnp.float32), 'ln2_g': jnp.ones((E,), jnp.float32), 'ln2_b': jnp.zeros((E,), jnp.float32), 'ln3_g': jnp.ones((E,), jnp.float32), 'ln3_b': jnp.zeros((E,), jnp.float32)}
        return inp
    _L3_xattn_all = _L3_xattn_setup()
    _L3_xattn_in = {k: v for k, v in _L3_xattn_all.items() if k in ('Wq1', 'Wk1', 'Wv1', 'Wq2', 'Wk2', 'Wv2', 'fc1_w', 'fc1_b', 'fc2_w', 'fc2_b', 'ln1_g', 'ln1_b', 'ln2_g', 'ln2_b', 'ln3_g', 'ln3_b')}
    del _L3_xattn_all

    def _L3_ffn_setup():
        import jax, jax.numpy as jnp
        import numpy as np
        DIM = 128

        def _reference_tuple_inner(x, W_r, W_k, W_v, mu_r, mu_k):
            B, T, C = x.shape
            x_prev = jnp.concatenate([jnp.zeros((B, 1, C), x.dtype), x[:, :-1, :]], axis=1)
            xr = mu_r * x + (1.0 - mu_r) * x_prev
            xk = mu_k * x + (1.0 - mu_k) * x_prev
            r = jax.nn.sigmoid(jnp.einsum('btc,dc->btd', xr, W_r))
            k = jnp.einsum('btc,dc->btd', xk, W_k)
            k_act = jnp.square(jax.nn.relu(k))
            out = r * jnp.einsum('btc,dc->btd', k_act, W_v)
            new_state = x[:, -1, :]
            return (out, new_state)
        key = jax.random.key(seed)
        ks = jax.random.split(key, 6)
        B, T, C = (8, 256, DIM)
        x = jax.random.normal(ks[0], (B, T, C), dtype=jnp.float32)
        s = 1.0 / np.sqrt(C)
        W_r = jax.random.uniform(ks[1], (C, C), jnp.float32, -s, s)
        W_k = jax.random.uniform(ks[2], (C, C), jnp.float32, -s, s)
        W_v = jax.random.uniform(ks[3], (C, C), jnp.float32, -s, s)
        mu_r = jax.random.uniform(ks[4], (C,), jnp.float32)
        mu_k = jax.random.uniform(ks[5], (C,), jnp.float32)
        return {'x': x, 'W_r': W_r, 'W_k': W_k, 'W_v': W_v, 'mu_r': mu_r, 'mu_k': mu_k}
    _L3_ffn_all = _L3_ffn_setup()
    _L3_ffn_in = {k: v for k, v in _L3_ffn_all.items() if k in ('W_r', 'W_k', 'W_v', 'mu_r', 'mu_k')}
    del _L3_ffn_all
    return {'x': x, 'ctx_1024': ctx_1024, 'L0_xattn_Wq': _L0_xattn_in['Wq'], 'L0_xattn_bq': _L0_xattn_in['bq'], 'L0_xattn_Wk': _L0_xattn_in['Wk'], 'L0_xattn_bk': _L0_xattn_in['bk'], 'L0_xattn_Wv': _L0_xattn_in['Wv'], 'L0_xattn_bv': _L0_xattn_in['bv'], 'L0_xattn_Wo': _L0_xattn_in['Wo'], 'L0_xattn_bo': _L0_xattn_in['bo'], 'L0_ffn_Wq': _L0_ffn_in['Wq'], 'L0_ffn_Wk': _L0_ffn_in['Wk'], 'L0_ffn_Wv': _L0_ffn_in['Wv'], 'L0_ffn_Wo': _L0_ffn_in['Wo'], 'L0_ffn_Wff': _L0_ffn_in['Wff'], 'L1_xattn_Wq': _L1_xattn_in['Wq'], 'L1_xattn_bq': _L1_xattn_in['bq'], 'L1_xattn_Wk': _L1_xattn_in['Wk'], 'L1_xattn_bk': _L1_xattn_in['bk'], 'L1_xattn_Wv': _L1_xattn_in['Wv'], 'L1_xattn_bv': _L1_xattn_in['bv'], 'L1_xattn_Wo': _L1_xattn_in['Wo'], 'L1_xattn_bo': _L1_xattn_in['bo'], 'L1_ffn_gate_w': _L1_ffn_in['gate_w'], 'L1_ffn_w1': _L1_ffn_in['w1'], 'L1_ffn_w2': _L1_ffn_in['w2'], 'L1_ffn_w3': _L1_ffn_in['w3'], 'L2_xattn_Wq': _L2_xattn_in['Wq'], 'L2_xattn_Wk': _L2_xattn_in['Wk'], 'L2_xattn_Wv': _L2_xattn_in['Wv'], 'L2_xattn_Wo': _L2_xattn_in['Wo'], 'L2_xattn_bo': _L2_xattn_in['bo'], 'L2_ffn_Wr': _L2_ffn_in['Wr'], 'L2_ffn_br': _L2_ffn_in['br'], 'L2_ffn_W1': _L2_ffn_in['W1'], 'L2_ffn_b1': _L2_ffn_in['b1'], 'L2_ffn_W2': _L2_ffn_in['W2'], 'L2_ffn_b2': _L2_ffn_in['b2'], 'L3_xattn_Wq1': _L3_xattn_in['Wq1'], 'L3_xattn_Wk1': _L3_xattn_in['Wk1'], 'L3_xattn_Wv1': _L3_xattn_in['Wv1'], 'L3_xattn_Wq2': _L3_xattn_in['Wq2'], 'L3_xattn_Wk2': _L3_xattn_in['Wk2'], 'L3_xattn_Wv2': _L3_xattn_in['Wv2'], 'L3_xattn_fc1_w': _L3_xattn_in['fc1_w'], 'L3_xattn_fc1_b': _L3_xattn_in['fc1_b'], 'L3_xattn_fc2_w': _L3_xattn_in['fc2_w'], 'L3_xattn_fc2_b': _L3_xattn_in['fc2_b'], 'L3_xattn_ln1_g': _L3_xattn_in['ln1_g'], 'L3_xattn_ln1_b': _L3_xattn_in['ln1_b'], 'L3_xattn_ln2_g': _L3_xattn_in['ln2_g'], 'L3_xattn_ln2_b': _L3_xattn_in['ln2_b'], 'L3_xattn_ln3_g': _L3_xattn_in['ln3_g'], 'L3_xattn_ln3_b': _L3_xattn_in['ln3_b'], 'L3_ffn_W_r': _L3_ffn_in['W_r'], 'L3_ffn_W_k': _L3_ffn_in['W_k'], 'L3_ffn_W_v': _L3_ffn_in['W_v'], 'L3_ffn_mu_r': _L3_ffn_in['mu_r'], 'L3_ffn_mu_k': _L3_ffn_in['mu_k']}

def reference(x, ctx_1024, L0_xattn_Wq, L0_xattn_bq, L0_xattn_Wk, L0_xattn_bk, L0_xattn_Wv, L0_xattn_bv, L0_xattn_Wo, L0_xattn_bo, L0_ffn_Wq, L0_ffn_Wk, L0_ffn_Wv, L0_ffn_Wo, L0_ffn_Wff, L1_xattn_Wq, L1_xattn_bq, L1_xattn_Wk, L1_xattn_bk, L1_xattn_Wv, L1_xattn_bv, L1_xattn_Wo, L1_xattn_bo, L1_ffn_gate_w, L1_ffn_w1, L1_ffn_w2, L1_ffn_w3, L2_xattn_Wq, L2_xattn_Wk, L2_xattn_Wv, L2_xattn_Wo, L2_xattn_bo, L2_ffn_Wr, L2_ffn_br, L2_ffn_W1, L2_ffn_b1, L2_ffn_W2, L2_ffn_b2, L3_xattn_Wq1, L3_xattn_Wk1, L3_xattn_Wv1, L3_xattn_Wq2, L3_xattn_Wk2, L3_xattn_Wv2, L3_xattn_fc1_w, L3_xattn_fc1_b, L3_xattn_fc2_w, L3_xattn_fc2_b, L3_xattn_ln1_g, L3_xattn_ln1_b, L3_xattn_ln2_g, L3_xattn_ln2_b, L3_xattn_ln3_g, L3_xattn_ln3_b, L3_ffn_W_r, L3_ffn_W_k, L3_ffn_W_v, L3_ffn_mu_r, L3_ffn_mu_k):
    import jax
    import jax.numpy as jnp

    def _L0_xattn_ref(x, c, Wq, bq, Wk, bk, Wv, bv, Wo, bo):
        import jax, jax.numpy as jnp
        import numpy as np
        import math
        CHANNELS = 64
        N_HEADS = 8
        K_CH = CHANNELS // N_HEADS
        ROPE_D = int(K_CH * 0.5)
        BASE = 1250

        def _rope(x):
            d = ROPE_D
            t = x.shape[2]
            theta = 1.0 / BASE ** (jnp.arange(0, d, 2, dtype=jnp.float32) / d)
            ang = jnp.arange(t, dtype=jnp.float32)[:, None] * theta[None, :]
            ang = jnp.concatenate([ang, ang], axis=-1)
            cos = jnp.cos(ang)[None, None, :, :].astype(x.dtype)
            sin = jnp.sin(ang)[None, None, :, :].astype(x.dtype)
            x_rope, x_pass = (x[..., :d], x[..., d:])
            neg_half = jnp.concatenate([-x_rope[..., d // 2:], x_rope[..., :d // 2]], axis=-1)
            return jnp.concatenate([x_rope * cos + neg_half * sin, x_pass], axis=-1)

        def _split_heads(y):
            b, _, t = y.shape
            return y.reshape(b, N_HEADS, K_CH, t).transpose(0, 1, 3, 2)
        q = jnp.einsum('oc,bct->bot', Wq, x) + bq[None, :, None]
        k = jnp.einsum('oc,bct->bot', Wk, c) + bk[None, :, None]
        v = jnp.einsum('oc,bct->bot', Wv, c) + bv[None, :, None]
        q = _rope(_split_heads(q))
        k = _rope(_split_heads(k))
        v = _split_heads(v)
        scale = 1.0 / math.sqrt(K_CH)
        scores = jnp.einsum('bhtc,bhsc->bhts', q, k) * scale
        p_attn = jax.nn.softmax(scores, axis=-1)
        out = jnp.einsum('bhts,bhsc->bhtc', p_attn, v)
        b, _, t, _ = out.shape
        out = out.transpose(0, 1, 3, 2).reshape(b, CHANNELS, t)
        return jnp.einsum('oc,bct->bot', Wo, out) + bo[None, :, None]

    def _L0_ffn_ref(x, Wq, Wk, Wv, Wo, Wff):
        import jax, jax.numpy as jnp
        import numpy as np
        from functools import partial
        HEADS = 16
        EPS = 1e-12

        def _l2_normalize(z):
            n = jnp.linalg.norm(z, axis=-1, keepdims=True)
            return z / jnp.maximum(n, EPS)
        B, S, D = x.shape
        H = HEADS
        L = Wq.shape[1]
        dh = L // H

        def split_heads(t):
            return t.reshape(B, S, H, dh).transpose(0, 2, 1, 3).reshape(B * H, S, dh)
        q = split_heads(x @ Wq)
        k = split_heads(x @ Wk)
        v = split_heads(x @ Wv)
        scores = jnp.einsum('bqd,bkd->bkq', q, k) / jnp.sqrt(jnp.asarray(D, x.dtype))
        attn = jax.nn.softmax(scores, axis=-1)
        out = jnp.einsum('bkq,bkv->bqv', attn, v)
        z = out.reshape(B, H, S, dh).transpose(0, 2, 1, 3).reshape(B, S, L)
        z = z @ Wo
        z = _l2_normalize(z)
        z = z @ Wff
        z = _l2_normalize(z)
        z = jax.nn.gelu(z, approximate=False)
        return z

    def _L1_xattn_ref(x, l, Wq, bq, Wk, bk, Wv, bv, Wo, bo):
        import jax, jax.numpy as jnp
        import numpy as np
        DIM = 128
        HEADS = 16
        DS = 4
        B, N, _ = l.shape
        M = x.shape[1]
        d = DIM // HEADS

        def split_heads(t):
            return t.reshape(t.shape[0], t.shape[1], HEADS, d).transpose(0, 2, 1, 3)
        q = split_heads(l @ Wq.T + bq)
        k = split_heads(x @ Wk.T + bk)
        v = split_heads(x @ Wv.T + bv)
        scores = jnp.einsum('bhid,bhjd->bhij', q, k) * d ** (-0.5)
        ii = jnp.arange(N)[:, None]
        jj = jnp.arange(M)[None, :]
        allowed = jj // DS <= ii
        scores = jnp.where(allowed[None, None], scores, -jnp.inf)
        attn = jax.nn.softmax(scores, axis=-1)
        out = jnp.einsum('bhij,bhjd->bhid', attn, v)
        out = out.transpose(0, 2, 1, 3).reshape(B, N, DIM)
        return out @ Wo.T + bo

    def _L1_ffn_ref(x, gate_w, w1, w2, w3):
        import jax, jax.numpy as jnp
        import numpy as np
        TOP_K = 2

        def _route(x2d, gate_w, num_experts, top_k):
            scores = jax.nn.softmax((x2d @ gate_w.T).astype(jnp.float32), axis=1)
            top_scores, sel = jax.lax.top_k(scores, top_k)
            sel_flat = sel.reshape(-1)
            counts = jnp.bincount(sel_flat, length=num_experts)
            order = jnp.argsort(sel_flat, stable=True)
            top_scores_sorted = top_scores.reshape(-1)[order]
            token_idx = order // top_k
            return (top_scores_sorted, token_idx, counts)

        def _grouped_swiglu(xr, w1, w2, w3, eid):
            out = jnp.zeros((xr.shape[0], w2.shape[-1]), dtype=xr.dtype)
            for e in range(w1.shape[0]):
                xe = jnp.where((eid == e)[:, None], xr, 0.0)
                h = jax.nn.silu(xe @ w1[e]) * (xe @ w3[e])
                out = out + h @ w2[e]
            return out
        bs, slen, dim = x.shape
        E, top_k = (gate_w.shape[0], TOP_K)
        x2d = x.reshape(bs * slen, dim)
        top_scores, token_idx, counts = _route(x2d, gate_w, E, top_k)
        routed_in = (x2d[token_idx].astype(jnp.float32) * top_scores[:, None]).astype(x.dtype)
        Tr = bs * slen * top_k
        eid = jnp.repeat(jnp.arange(E), counts, total_repeat_length=Tr)
        routed_out = _grouped_swiglu(routed_in, w1, w2, w3, eid)
        out = jnp.zeros((bs * slen, dim), dtype=x.dtype).at[token_idx].add(routed_out)
        return out.reshape(bs, slen, dim)

    def _L2_xattn_ref(x, context, Wq, Wk, Wv, Wo, bo):
        import jax, jax.numpy as jnp
        import numpy as np
        DIM = 128
        NUM_HEADS = 8
        HEAD_DIM = 64
        INNER = NUM_HEADS * HEAD_DIM
        B, N, _ = x.shape
        M = context.shape[1]
        scale = HEAD_DIM ** (-0.5)
        q = (x @ Wq).reshape(B, N, NUM_HEADS, HEAD_DIM).transpose(0, 2, 1, 3)
        k = (context @ Wk).reshape(B, M, NUM_HEADS, HEAD_DIM).transpose(0, 2, 1, 3)
        v = (context @ Wv).reshape(B, M, NUM_HEADS, HEAD_DIM).transpose(0, 2, 1, 3)
        attn = jax.nn.softmax(jnp.einsum('bhnd,bhmd->bhnm', q, k) * scale, axis=-1)
        out = jnp.einsum('bhnm,bhmd->bhnd', attn, v)
        out = out.transpose(0, 2, 1, 3).reshape(B, N, INNER)
        return out @ Wo + bo

    def _L2_ffn_ref(x, Wr, br, W1, b1, W2, b2):
        import jax, jax.numpy as jnp
        import numpy as np
        E = 8
        K = 2
        CAP_FACTOR = 1.0
        B, T, C = x.shape
        N = B * T
        xf = x.reshape(N, C)
        logits = xf @ Wr + br
        topv, topi = jax.lax.top_k(logits, K)
        gates = jax.nn.softmax(topv, axis=-1)
        rw = jnp.zeros((N, E), xf.dtype).at[jnp.arange(N)[:, None], topi].set(gates)
        cap = int(N * K / E * CAP_FACTOR)
        sel = jax.nn.one_hot(topi, E, dtype=jnp.int32).sum(1)
        rank = jnp.cumsum(sel, axis=0) - sel
        keep = (sel > 0) & (rank < cap)
        tok = jnp.broadcast_to(jnp.arange(N, dtype=jnp.int32)[:, None], (N, E))
        eid = jnp.broadcast_to(jnp.arange(E, dtype=jnp.int32)[None, :], (N, E))
        rank_c = jnp.where(keep, rank, cap)
        buf = jnp.full((E, cap), N, dtype=jnp.int32)
        buf = buf.at[eid, rank_c].set(tok, mode='drop')
        xpad = jnp.concatenate([xf, jnp.zeros((1, C), xf.dtype)], axis=0)
        xg = xpad[buf]
        h = jax.nn.gelu(jnp.einsum('ecd,edh->ech', xg, W1) + b1[:, None, :], approximate=False)
        out = jnp.einsum('ech,ehd->ecd', h, W2) + b2[:, None, :]
        rw_pad = jnp.concatenate([rw, jnp.zeros((1, E), rw.dtype)], axis=0)
        w = rw_pad[buf, jnp.arange(E, dtype=jnp.int32)[:, None]]
        weighted = out * w[..., None]
        final = jnp.zeros((N + 1, C), xf.dtype).at[buf.reshape(-1)].add(weighted.reshape(-1, C))
        return final[:N].reshape(B, T, C)

    def _L3_xattn_ref(x, context, Wq1, Wk1, Wv1, Wq2, Wk2, Wv2, fc1_w, fc1_b, fc2_w, fc2_b, ln1_g, ln1_b, ln2_g, ln2_b, ln3_g, ln3_b):
        import jax, jax.numpy as jnp
        import numpy as np
        E = 128
        NUM_HEADS = 16
        DK = E // NUM_HEADS
        EPS = 1e-05
        NEG_INF = -jnp.inf

        def layer_norm(x, g, b):
            mu = jnp.mean(x, axis=-1, keepdims=True)
            var = jnp.var(x, axis=-1, keepdims=True)
            return (x - mu) * jax.lax.rsqrt(var + EPS) * g + b

        def self_attn(x, Wq, Wk, Wv):
            Q, K, V = (x @ Wq, x @ Wk, x @ Wv)
            energy = jnp.einsum('bqd,bkd->bqk', Q, K)
            S = energy.shape[-1]
            lengths = jnp.sum(energy[:, 0] != 0, axis=-1)
            kidx = jnp.arange(S)
            pad = kidx[None, None, :] >= lengths[:, None, None]
            causal = kidx[None, :] < kidx[:, None]
            causal = (kidx[None, :] > kidx[:, None])[None]
            energy = jnp.where(pad | causal, NEG_INF, energy)
            score = jax.nn.softmax(energy / np.sqrt(DK), axis=-1)
            return jnp.einsum('bqk,bkd->bqd', score, V)

        def cross_attn(x, context, Wq, Wk, Wv):
            Q = x @ Wq
            K, V = (context @ Wk, context @ Wv)
            energy = jnp.einsum('bqd,bkd->bqk', Q, K)
            Sk = energy.shape[-1]
            lengths = jnp.sum(energy[:, 0] != 0, axis=-1)
            kidx = jnp.arange(Sk)
            pad = kidx[None, None, :] >= lengths[:, None, None]
            energy = jnp.where(pad, NEG_INF, energy)
            score = jax.nn.softmax(energy / np.sqrt(DK), axis=-1)
            return jnp.einsum('bqk,bkd->bqd', score, V)
        z = self_attn(x, Wq1, Wk1, Wv1)
        x = layer_norm(x + z, ln1_g, ln1_b)
        z = cross_attn(x, context, Wq2, Wk2, Wv2)
        x = layer_norm(x + z, ln2_g, ln2_b)
        z = jax.nn.relu(x @ fc1_w + fc1_b)
        z = z @ fc2_w + fc2_b
        return layer_norm(x + z, ln3_g, ln3_b)

    def _L3_ffn_ref(x, W_r, W_k, W_v, mu_r, mu_k):
        import jax, jax.numpy as jnp
        import numpy as np
        DIM = 128

        def _reference_tuple_inner(x, W_r, W_k, W_v, mu_r, mu_k):
            B, T, C = x.shape
            x_prev = jnp.concatenate([jnp.zeros((B, 1, C), x.dtype), x[:, :-1, :]], axis=1)
            xr = mu_r * x + (1.0 - mu_r) * x_prev
            xk = mu_k * x + (1.0 - mu_k) * x_prev
            r = jax.nn.sigmoid(jnp.einsum('btc,dc->btd', xr, W_r))
            k = jnp.einsum('btc,dc->btd', xk, W_k)
            k_act = jnp.square(jax.nn.relu(k))
            out = r * jnp.einsum('btc,dc->btd', k_act, W_v)
            new_state = x[:, -1, :]
            return (out, new_state)
        return _reference_tuple_inner(x, W_r, W_k, W_v, mu_r, mu_k)[0]
    x = x + _L0_xattn_ref(_layernorm(x, axis=-1), ctx_1024, L0_xattn_Wq, L0_xattn_bq, L0_xattn_Wk, L0_xattn_bk, L0_xattn_Wv, L0_xattn_bv, L0_xattn_Wo, L0_xattn_bo)
    x = x + _L0_ffn_ref(_layernorm(x, axis=-1), L0_ffn_Wq, L0_ffn_Wk, L0_ffn_Wv, L0_ffn_Wo, L0_ffn_Wff)
    x = x + _L1_xattn_ref(ctx_1024, _layernorm(x, axis=-1), L1_xattn_Wq, L1_xattn_bq, L1_xattn_Wk, L1_xattn_bk, L1_xattn_Wv, L1_xattn_bv, L1_xattn_Wo, L1_xattn_bo)
    x = x + _L1_ffn_ref(_layernorm(x, axis=-1), L1_ffn_gate_w, L1_ffn_w1, L1_ffn_w2, L1_ffn_w3)
    x = x + _L2_xattn_ref(_layernorm(x, axis=-1), ctx_1024, L2_xattn_Wq, L2_xattn_Wk, L2_xattn_Wv, L2_xattn_Wo, L2_xattn_bo)
    x = x + _L2_ffn_ref(_layernorm(x, axis=-1), L2_ffn_Wr, L2_ffn_br, L2_ffn_W1, L2_ffn_b1, L2_ffn_W2, L2_ffn_b2)
    x = x + _L3_xattn_ref(_layernorm(x, axis=-1), ctx_1024, L3_xattn_Wq1, L3_xattn_Wk1, L3_xattn_Wv1, L3_xattn_Wq2, L3_xattn_Wk2, L3_xattn_Wv2, L3_xattn_fc1_w, L3_xattn_fc1_b, L3_xattn_fc2_w, L3_xattn_fc2_b, L3_xattn_ln1_g, L3_xattn_ln1_b, L3_xattn_ln2_g, L3_xattn_ln2_b, L3_xattn_ln3_g, L3_xattn_ln3_b)
    x = x + _L3_ffn_ref(_layernorm(x, axis=-1), L3_ffn_W_r, L3_ffn_W_k, L3_ffn_W_v, L3_ffn_mu_r, L3_ffn_mu_k)
    return x

_drawn_inputs = setup_inputs


def setup_inputs(seed=0):
    import zlib

    import numpy as np

    out = dict(_drawn_inputs(seed))
    spreads = {'L1_xattn_bq': (0.0, 0.8),
     'L1_xattn_bk': (0.0, 2.0),
     'L1_xattn_bv': (0.0, 0.292),
     'L1_xattn_bo': (0.0, 0.1),
     'L2_ffn_br': (0.0, 0.1),
     'L2_ffn_b1': (0.0, 0.497),
     'L2_ffn_b2': (0.0, 0.1),
     'L3_xattn_fc1_b': (0.0, 0.45),
     'L3_xattn_fc2_b': (0.0, 0.321),
     'L3_xattn_ln1_g': (1.0, 0.2),
     'L3_xattn_ln1_b': (0.0, 0.1),
     'L3_xattn_ln2_g': (1.0, 0.2),
     'L3_xattn_ln2_b': (0.0, 0.1),
     'L3_xattn_ln3_g': (1.0, 0.2),
     'L3_xattn_ln3_b': (0.0, 0.1)}
    factors = {'L0_xattn_bq': 8.0,
     'L0_xattn_bk': 8.0,
     'L0_xattn_bv': 5.127,
     'L0_xattn_bo': 5.029,
     'L0_ffn_Wq': 8.0,
     'L0_ffn_Wk': 8.0,
     'L1_xattn_Wq': 8.0,
     'L1_xattn_Wk': 8.0,
     'L1_ffn_gate_w': 8.0,
     'L1_ffn_w1': 8.0,
     'L1_ffn_w2': 8.0,
     'L1_ffn_w3': 8.0,
     'L2_xattn_bo': 4.409,
     'L3_ffn_W_r': 5.128,
     'L3_ffn_mu_r': 27.753,
     'L2_ffn_W1': 3.045,
     'L3_ffn_mu_k': 3.025}
    for name, (base, spread) in spreads.items():
        noise = np.random.default_rng([zlib.crc32(name.encode()), seed]).standard_normal(out[name].shape)
        drawn = base * np.exp(spread * noise) if base else spread * noise
        out[name] = jnp.asarray(drawn.astype(out[name].dtype))
    for name, factor in factors.items():
        out[name] = (out[name] * factor).astype(out[name].dtype)
    return out
```

```python
from contextlib import ExitStack

import numpy as np
import concourse.bass as bass
from concourse import mybir

F32 = mybir.dt.float32
BF16 = mybir.dt.bfloat16
U32 = mybir.dt.uint32
I32 = mybir.dt.int32
ALU = mybir.AluOpType
ACT = mybir.ActivationFunctionType
AX = mybir.AxisListType.X

P = 128
B, T, D = 64, 64, 128
NT = B // 2
NTOK = B * T
E = 8
TOPK = 2
LN_EPS = 1e-5
L2_EPS = 1e-12
NEG = -1e30
CHUNK = 256
CAP = NTOK * TOPK // E
HID1, HID1P = 352, 384
HID2 = 512
NCH1 = (NTOK * TOPK + E * (CHUNK - 1)) // CHUNK
NCH1 += NCH1 % 2
NCH2 = E * CAP // CHUNK


def pipeline(eng, n, steps):
    lags = [lag for lag, _ in steps]
    head = max(lags) + 2
    head += head % 2
    if head >= n:
        head = n

    def static(t):
        for lag, fn in steps:
            if 0 <= t - lag < n:
                fn(t - lag, (t - lag) % 2)

    for t in range(head):
        static(t)
    if head < n:
        with eng.Fori(head // 2, n // 2) as i:
            for p in range(2):
                for lag, fn in steps:
                    fn(2 * i + (p - lag), (p - lag) % 2)
    for t in range(n, n + max(lags)):
        static(t)


def done(eng, sem, u, per=1):
    eng.wait_ge(sem, per * u + per)


def free(eng, sem, u, bufs=2, per=1):
    if isinstance(u, int) and u < bufs:
        return
    eng.wait_ge(sem, per * u + (per - per * bufs))


def landed(eng, sems, u, p):
    eng.wait_ge(sems[p], 8 * u + (16 - 8 * p))


def pack_layout():
    cols = {}
    at = 0
    for name, n in PACK:
        cols[name] = (at, n)
        at += n
    return cols, at


PACK = [
    ("ident", 128), ("maskA", 16), ("maskB", 8), ("cos", 128), ("sin", 128),
    ("a0_wq", 128), ("a0_wqr", 128), ("a0_wk", 128), ("a0_wkr", 128), ("a0_wv", 128), ("a0_wo", 128),
    ("a0_bias", 6),
    ("ones", 128), ("tri", 128), ("sel0", 128), ("iota64", 64), ("causal", 64), ("allow1", 64),
    ("rank8", 8), ("iota8", 8), ("chunk0", NCH1), ("spare", TOPK * NT),
    ("f0_wq", 128), ("f0_wk", 128), ("f0_wv", 128), ("f0_woT", 128), ("f0_wo", 128), ("f0_wff", 128),
    ("a1_wq", 128), ("a1_wk", 128), ("a1_wv", 128), ("a1_wo", 128), ("a1_bq", 2), ("a1_bk", 2),
    ("a1_bv", 1), ("a1_bo", 128),
    ("f1_gate", 8),
    ("a2_wq", 512), ("a2_wk", 512), ("a2_wv", 512), ("a2_wo", 512), ("a2_bo", 128),
    ("f2_wr", 8), ("f2_br", 8),
    ("a3_wq1", 128), ("a3_wk1", 128), ("a3_wv1", 128), ("a3_wq2", 128), ("a3_wk2", 128),
    ("a3_wv2", 128), ("a3_fc1", 128), ("a3_fc2", 128), ("a3_b1", 1), ("a3_b2", 128),
    ("a3_g1", 128), ("a3_c1", 128), ("a3_g2", 128), ("a3_c2", 128), ("a3_g3", 128), ("a3_c3", 128),
    ("f3_wr", 128), ("f3_wk", 128), ("f3_wv", 128), ("f3_mr", 1), ("f3_mk", 1),
]
COLS, PACKW = pack_layout()
FIRST = COLS["ones"][0]
GATHER_PARTS = 4
HEADS = 16
GH = 8


class Net:

    def __init__(self, nc, dram, W, X):
        self.nc, self.dram, self.W, self.X = nc, dram, W, X
        self.stale, self.current = [], []

    def w(self, name, lo=0, hi=None):
        at, n = COLS[name]
        return self.W[:, at + lo:at + (n if hi is None else hi)]


def opener(net, ctx, stage):
    nc = net.nc
    net.stale, net.current = net.current, []

    def sb(name, shape, dt=F32):
        return ctx.enter_context(nc.sbuf_tensor(f"{stage}_{name}", shape, dt))

    def ps(name, shape, dt=F32):
        return ctx.enter_context(nc.psum_tensor(f"{stage}_{name}", shape, dt))

    def sem(name):
        net.current.append(ctx.enter_context(nc.semaphore(f"{stage}_{name}")))
        return net.current[-1]

    return sb, ps, sem


def clear_stale(net, sp):
    for sem in net.stale:
        sp.sem_clear(sem)


class Bank:

    def __init__(self, n, uses):
        self.n, self.uses, self.order = n, uses, list(uses)

    def take(self, pe, name, u):
        at = self.order.index(name)
        lag = self.uses[name][0]
        before = [(m, u + lag - self.uses[m][0] - (k >= at)) for k, m in enumerate(self.order)]
        if isinstance(u, int):
            for m, v in before:
                v = min(v, self.n - 1)
                if v >= 0:
                    self.reader_done(pe, m, v)
        else:
            self.reader_done(pe, *before[at - 1])

    def reader_done(self, pe, m, u):
        _, sem, per, nth = self.uses[m]
        pe.wait_ge(sem, per * u + nth)


class LayerNorm:

    def __init__(self, net, sb, sem, xn, xn_used):
        self.net, self.xn, self.xn_used = net, xn, xn_used
        self.stats = sb("ln_stats", [P, 2, 6])
        self.moments = sb("ln_moments", [P, 2, 2])
        self.rstd = sb("ln_rstd", [P, 2, 2])
        self.half = sb("ln_half", [P, 2])
        self.s_half = sem("ln_half")
        self.s_stats = sem("ln_stats")
        self.s_moments = sem("ln_moments")
        self.s_vareps = sem("ln_vareps")
        self.s_rstd = sem("ln_rstd")
        self.s_xn = sem("xn")

    def setup(self, pool):
        self.net.nc.gpsimd.memset(self.half[:, 0:1], -0.5).then_inc(self.s_half, 1)
        self.net.nc.gpsimd.memset(self.half[:, 1:2], LN_EPS).then_inc(self.s_half, 1)
        pool.wait_ge(self.s_half, 2)

    def vector_stats(self, dve, u, p):
        nc = self.net.nc
        if not isinstance(u, int):
            self.moments_waits(dve, u - 1)
        nc.vector.bn_stats(self.stats[:, p, :], self.net.X[:, u, :]).then_inc(self.s_stats, 1)

    def moments_waits(self, dve, u):
        done(dve, self.s_stats, u)
        free(dve, self.s_rstd, u)
        free(dve, self.s_xn, u)

    def vector_moments(self, dve, u, p):
        if isinstance(u, int):
            self.moments_waits(dve, u)
        self.net.nc.vector.bn_aggr(self.moments[:, p, :], self.stats[:, p, :]).then_inc(self.s_moments, 1)

    def pool_rstd(self, pool, u, p):
        nc = self.net.nc
        done(pool, self.s_moments, u)
        free(pool, self.s_xn, u)
        nc.gpsimd.tensor_tensor(self.rstd[:, p, 0:1], self.moments[:, p, 1:2], self.half[:, 1:2],
                                ALU.add).then_inc(self.s_vareps, 1)
        done(pool, self.s_vareps, u)
        nc.gpsimd.tensor_tensor(self.rstd[:, p, 1:2], self.rstd[:, p, 0:1], self.half[:, 0:1],
                                ALU.pow).then_inc(self.s_rstd, 1)

    def vector_apply(self, dve, u, p):
        done(dve, self.s_moments, u)
        done(dve, self.s_rstd, u)
        free(dve, self.xn_used, u)
        self.net.nc.vector.tensor_scalar(self.xn[:, p, :], self.net.X[:, u, :], self.moments[:, p, 0:1],
                                         self.rstd[:, p, 1:2], ALU.subtract, ALU.mult
                                         ).then_inc(self.s_xn, 1)


def load_stage(net):
    nc = net.nc
    with ExitStack() as ctx:
        _, _, sem = opener(net, ctx, "load")
        s_first, s_zero, s_fill = sem("weights"), sem("zero"), sem("slots_zeroed")
        block = ctx.enter_context(nc.Block())
        slots = net.dram["slots_in"][0:NCH1 * CHUNK, :].rearrange("(n p r) d -> n p (r d)", p=P, r=8)

        @block.vector
        def _(dve):
            nc.vector.memset(net.Y[:, 0:8, :], 0.0).then_inc(s_zero, 1)

        @block.sync
        def _(sp):
            sp.dma_start(net.W[:, 0:FIRST], net.dram["wpack"][:, 0:FIRST]).then_inc(s_first, 16)
            sp.dma_start(net.X[:, :, :], net.dram["x"].rearrange("(i b) t d -> (b t) i d", b=2)
                         ).then_inc(s_first, 16)
            sp.dma_start(net.W[:, FIRST:], net.dram["wpack"][:, FIRST:]).then_inc(s_first, 16)
            sp.wait_ge(s_zero, 1)
            for n in range(slots.shape[0]):
                sp.dma_start(slots[n], net.Y[:, 0:8, :].rearrange("p r d -> p (r d)")).then_inc(s_fill, 16)
            sp.wait_ge(s_first, 48)
            sp.wait_ge(s_fill, 16 * slots.shape[0])


def attention0_stage(net):
    nc, X, w = net.nc, net.X, net.w
    SCALE = 8 ** -0.5
    with ExitStack() as ctx:
        sb, ps, sem = opener(net, ctx, "a0")
        xn = sb("xn", [P, 2, D])
        cx = sb("cx", [P, 2, D])
        qb = sb("qbias", [P, 2, D])
        rot = sb("rot", [P, 2, 2, 2, D])
        qk = sb("qk", [P, 2, 2, D])
        kM = sb("kM", [P, 2, HEADS, D])
        V = sb("V", [P, 2, HEADS, 9])
        Pr = sb("Pr", [P, 2, GH, D])
        PT = sb("PT", [P, 2, GH, D])
        mx = sb("mx", [P, 2, GH])
        rden = sb("rden", [P, 2, GH, 1])
        zn = sb("zn", [P, 2, HEADS, 8])
        zT = sb("zT", [P, 2, D])
        S = ps("S", [P, 2, 1024])
        PTp = ps("PTp", [P, 1024])
        pQ = ps("pQ", [P, 4, D])
        pY = ps("pY", [P, 512])
        pV, pO, pZ, pW = pY[:, 0:128], pY[:, 128:128 + 72], pY[:, 256:384], pY[:, 384:512]

        s_cx = [sem("cx_even"), sem("cx_odd")]
        s_ones, s_qb, s_qb2 = sem("ones"), sem("qbias"), sem("qbias2")
        s_proj, s_v, s_vs = sem("proj"), sem("v"), sem("v_out")
        s_cos, s_sin, s_rot, s_qk = sem("cos"), sem("sin"), sem("rot"), sem("qk")
        s_km = sem("kM")
        s_S, s_mx, s_sub, s_exp = sem("scores"), sem("max"), sem("sub"), sem("exp")
        s_pt, s_pts, s_o, s_rd, s_zn = sem("pt"), sem("pt_out"), sem("o"), sem("rden"), sem("zn")
        s_zt, s_zts, s_y, s_x = sem("zt"), sem("zt_out"), sem("y"), sem("x")
        ln = LayerNorm(net, sb, sem, xn, s_proj)
        block = ctx.enter_context(nc.Block())

        @block.sync
        def _(sp):
            clear_stale(net, sp)
            def load_context(u, p):
                free(sp, s_v, u)
                sp.dma_start(cx[:, p, :], net.dram["ctx"][2 * u:2 * u + 2] if isinstance(u, int)
                             else net.dram["ctx"][bass.ds(2 * u, 2)]).then_inc(s_cx[p], 16)
            pipeline(sp, NT, [(0, load_context)])

        @block.gpsimd
        def _(pool):
            ln.setup(pool)
            nc.gpsimd.memset(V[:, :, :, 8:9], 1.0).then_inc(s_ones, 1)

            def add_parts(u, p):
                done(pool, s_sin, u)
                nc.gpsimd.tensor_tensor(rot[:, p, 0], rot[:, p, 0], rot[:, p, 1],
                                        ALU.add).then_inc(s_rot, 1)
                done(pool, s_rot, u)
                free(pool, s_S, u, per=2)
                free(pool, s_km, u)
                nc.gpsimd.tensor_tensor(qk[:, p], rot[:, p, 0], qb[:, :, :], ALU.add).then_inc(s_qk, 1)

            pool.wait_ge(s_qb2, 2)
            pipeline(pool, NT, [(1, lambda u, p: ln.pool_rstd(pool, u, p)), (3, add_parts)])

        @block.vector
        def _(dve):
            bias = w("a0_bias")
            for n in range(2):
                nc.vector.tensor_scalar(qb[:, n, :], w("cos"), bias[:, 2 * n:2 * n + 1], None,
                                        ALU.mult).then_inc(s_qb, 1)
            dve.wait_ge(s_qb, 2)
            for n in range(2):
                nc.vector.scalar_tensor_tensor(qb[:, n, :], w("sin"), bias[:, 2 * n + 1:2 * n + 2],
                                               qb[:, n, :], ALU.mult, ALU.add).then_inc(s_qb2, 1)
            cos2 = w("cos").unsqueeze(1).broadcast_to([P, 2, D])
            sin2 = w("sin").unsqueeze(1).broadcast_to([P, 2, D])
            head_mask = w("maskA").unsqueeze(2).broadcast_to([P, HEADS, D])

            def rotate(u, p):
                done(dve, s_proj, u)
                free(dve, s_rot, u)
                free(dve, s_qk, u)
                nc.vector.tensor_tensor(rot[:, p, 0], pQ[:, 0:2, :], cos2, ALU.mult).then_inc(s_cos, 1)
                nc.vector.tensor_tensor(rot[:, p, 1], pQ[:, 2:4, :], sin2, ALU.mult).then_inc(s_sin, 1)

            def spread_k(u, p):
                done(dve, s_qk, u)
                free(dve, s_S, u, per=2)
                nc.vector.tensor_tensor(kM[:, p], qk[:, p, 1:2, :].broadcast_to([P, HEADS, D]),
                                        head_mask, ALU.mult).then_inc(s_km, 1)

            def take_v(u, p):
                done(dve, s_v, u)
                free(dve, s_o, u, per=2)
                nc.vector.tensor_copy(V[:, p, :, 0:8], pV.rearrange("p (h c) -> p h c", c=8)
                                      ).then_inc(s_vs, 1)

            def softmax(half):
                def fn(u, p):
                    Sh = S[:, half, :].rearrange("p (h k) -> p h k", k=D)
                    dve.wait_ge(s_S, 2 * u + half + 1)
                    nc.vector.tensor_reduce(mx[:, half, :], Sh, AX, ALU.max).then_inc(s_mx, 1)
                    dve.wait_ge(s_mx, 2 * u + half + 1)
                    free(dve, s_pt, 2 * u + half)
                    nc.vector.tensor_tensor(Pr[:, half], Sh,
                                            mx[:, half, :].unsqueeze(2).broadcast_to([P, GH, D]),
                                            ALU.subtract).then_inc(s_sub, 1)
                return fn

            def normalise(half):
                def fn(u, p):
                    o = pO.rearrange("p (h c) -> p h c", c=9)
                    dve.wait_ge(s_o, 2 * u + half + 1)
                    nc.vector.reciprocal(rden[:, half], o[:, :, 8:9]).then_inc(s_rd, 1)
                    dve.wait_ge(s_rd, 2 * u + half + 1)
                    free(dve, s_zt, u)
                    nc.vector.tensor_tensor(zn[:, p, GH * half:GH * (half + 1), :], o[:, :, 0:8],
                                            rden[:, half].broadcast_to([P, GH, 8]),
                                            ALU.mult).then_inc(s_zn, 1)
                return fn

            def residual(u, p):
                done(dve, s_y, u)
                nc.vector.scalar_tensor_tensor(X[:, u, :], pW, bias[:, 5:6], X[:, u, :], ALU.add,
                                               ALU.add).then_inc(s_x, 1)

            pipeline(dve, NT, [(4, softmax(0)), (2, lambda u, p: ln.vector_apply(dve, u, p)),
                               (0, lambda u, p: ln.vector_stats(dve, u, p)),
                               (1, lambda u, p: ln.vector_moments(dve, u, p)), (5, normalise(0)),
                               (3, rotate), (4, softmax(1)), (5, normalise(1)), (3, take_v),
                               (3, spread_k), (6, residual)])

        @block.scalar
        def _(act):
            def exps(half):
                def fn(u, p):
                    act.wait_ge(s_sub, 2 * u + half + 1)
                    nc.scalar.activation(Pr[:, half], Pr[:, half], ACT.Exp, scale=SCALE
                                         ).then_inc(s_exp, 1)
                return fn

            def take_pt(half):
                def fn(u, p):
                    act.wait_ge(s_pt, 2 * u + half + 1)
                    free(act, s_o, 2 * u + half)
                    nc.scalar.activation(PT[:, half], PTp[:, :].rearrange("p (h k) -> p h k", k=D),
                                         ACT.Copy).then_inc(s_pts, 1)
                return fn

            def take_zt(u, p):
                done(act, s_zt, u)
                free(act, s_y, u)
                nc.scalar.activation(zT[:, p, :], pZ, ACT.Identity, bias=w("a0_bias")[:, 4:5]
                                     ).then_inc(s_zts, 1)

            pipeline(act, NT, [(5, take_pt(0)), (4, exps(0)), (6, take_zt), (5, take_pt(1)),
                               (4, exps(1))])

        small = Bank(NT, {"o0": (5, s_zn, 2, 1), "z": (6, s_zts, 1, 1), "o1": (5, s_zn, 2, 2),
                          "v": (3, s_vs, 1, 1), "y": (6, s_x, 1, 1)})

        @block.tensor
        def _(pe):
            pe.wait_ge(s_ones, 1)

            def project(u, p):
                done(pe, ln.s_xn, u)
                landed(pe, s_cx, u, p)
                free(pe, s_sin, u, bufs=1)
                nc.tensor.matmul(pQ[:, 0, :], w("a0_wq"), xn[:, p, :], start=True, stop=True)
                nc.tensor.matmul(pQ[:, 1, :], w("a0_wk"), cx[:, p, :], start=True, stop=True)
                nc.tensor.matmul(pQ[:, 2, :], w("a0_wqr"), xn[:, p, :], start=True, stop=True)
                nc.tensor.matmul(pQ[:, 3, :], w("a0_wkr"), cx[:, p, :], start=True, stop=True
                                 ).then_inc(s_proj, 1)

            def values(u, p):
                landed(pe, s_cx, u, p)
                small.take(pe, "v", u)
                nc.tensor.matmul(pV, cx[:, p, :], w("a0_wv"), start=True, stop=True).then_inc(s_v, 1)

            def scores(half):
                def fn(u, p):
                    done(pe, s_km, u)
                    if not (isinstance(u, int) and u == 0):
                        pe.wait_ge(s_sub, 2 * u + (half - 1))
                    for n in range(2):
                        k4 = kM[:, p, GH * half + 4 * n:GH * half + 4 * n + 4, :]
                        last = nc.tensor.matmul(S[:, half, 512 * n:512 * n + 512], qk[:, p, 0, :], k4,
                                                start=True, stop=True)
                    last.then_inc(s_S, 1)
                return fn

            def transpose_p(half):
                def fn(u, p):
                    pe.wait_ge(s_exp, 2 * u + half + 1)
                    free(pe, s_pts, 2 * u + half, bufs=1)
                    for h in range(GH):
                        last = nc.tensor.transpose(PTp[:, D * h:D * h + D], Pr[:, half, h, :], w("ident"))
                    last.then_inc(s_pt, 1)
                return fn

            def product_v(half):
                def fn(u, p):
                    pe.wait_ge(s_pts, 2 * u + half + 1)
                    if half == 0:
                        done(pe, s_vs, u)
                    small.take(pe, f"o{half}", u)
                    for h in range(GH):
                        last = nc.tensor.matmul(pO[:, 9 * h:9 * h + 9], PT[:, half, h, :],
                                                V[:, p, GH * half + h, :], start=True, stop=True)
                    last.then_inc(s_o, 1)
                return fn

            def transpose_z(u, p):
                done(pe, s_zn, u, per=2)
                small.take(pe, "z", u)
                nc.tensor.transpose(pZ, zn[:, p].rearrange("p h c -> p (h c)"), w("ident")
                                    ).then_inc(s_zt, 1)

            def output(u, p):
                done(pe, s_zts, u)
                small.take(pe, "y", u)
                nc.tensor.matmul(pW, w("a0_wo"), zT[:, p, :], start=True, stop=True).then_inc(s_y, 1)

            pipeline(pe, NT, [(5, transpose_p(0)), (4, scores(0)), (5, product_v(0)), (6, transpose_z),
                              (2, project), (5, transpose_p(1)), (4, scores(1)), (5, product_v(1)),
                              (3, values), (6, output)])


def heads16_stage(net, cross):
    nc, X, w = net.nc, net.X, net.w
    name = "a1" if cross else "f0"
    SCALE = 8 ** -0.5 if cross else D ** -0.5
    with ExitStack() as ctx:
        sb, ps, sem = opener(net, ctx, name)
        xn = sb("xn", [P, 2, D])
        xT = sb("xT", [P, 2, P])
        blk = sb("blk", [P, 2, 2, P])
        spread = sb("spread", [P, 2, 2, GH, T])
        Pr = sb("Pr", [P, 2, HEADS * T])
        mx = sb("mx", [P, 2, HEADS])
        zn = sb("zn", [P, 2, D])
        zT = sb("zT", [P, 2, P])
        rden = sb("rden", [P, 2, HEADS, 1])
        S = ps("S", [P, 2, 1024])
        pA = ps("pA", [P, 512])
        pB = ps("pB", [P, 512])
        s_ones, s_zero = sem("ones"), sem("zero")
        s_xt, s_xts, s_proj = sem("xt"), sem("xt_out"), sem("proj")
        s_blk, s_spread = sem("blk"), sem("spread")
        s_S, s_mx, s_sub, s_exp = sem("scores"), sem("max"), sem("sub"), sem("exp")
        s_v, s_vs, s_o, s_zn = sem("v"), sem("v_out"), sem("o"), sem("zn")
        s_rd, s_zt, s_zts, s_y, s_x = sem("rden"), sem("zt"), sem("zt_out"), sem("y"), sem("x")
        if cross:
            cT = sb("cT", [P, 2, P])
            V = sb("V", [P, 2, 2, 8, 2, 9])
            PT = sb("PT", [P, 2, 8, P])
            PTp = ps("PTp", [P, 1024])
            allow = sb("allow", [P, T], BF16)
            identb = sb("identb", [P, P], BF16)
            s_cT = [sem("cT_even"), sem("cT_odd")]
            s_pt, s_pts, s_tb, s_add = sem("pt"), sem("pt_out"), sem("tables"), sem("bias_added")
            wblk, wspread = w("a1_wq"), w("a1_wk")
        else:
            V = sb("V", [P, 2, HEADS, 8])
            vraw = sb("vraw", [P, 2, D])
            sums = sb("sums", [P, 2, HEADS])
            junk = sb("junk", [P, D])
            s_sum, s_w, s_sq = sem("sum"), sem("w_out"), sem("squares")
            s_wz, s_wzs = sem("wowff"), sem("wowff_out")
            wow = sb("wow", [P, 2 * D])
            wblk, wspread = w("f0_wk"), w("f0_wq")
        ln = LayerNorm(net, sb, sem, xn, s_xt)
        block = ctx.enter_context(nc.Block())

        if cross:
            @block.sync
            def _(sp):
                clear_stale(net, sp)
                def load_context(u, p):
                    free(sp, s_v, u)
                    sp.dma_start(cT[:, p, :], net.dram["ctxT"][u]).then_inc(s_cT[p], 16)
                pipeline(sp, NT, [(0, load_context)])
        else:
            @block.sync
            def _(sp):
                clear_stale(net, sp)

        @block.gpsimd
        def _(pool):
            ln.setup(pool)
            nc.gpsimd.memset(blk[:, :, :, :], 0.0).then_inc(s_zero, 1)
            if cross:
                nc.gpsimd.memset(V[:, :, :, :, :, :], 0.0).then_inc(s_ones, 1)
                for h in range(2):
                    pool.wait_ge(s_ones, h + 1)
                    nc.gpsimd.memset(V[64 * h:64 * h + 64, :, :, :, h, 8:9], 1.0).then_inc(s_ones, 1)
                pool.wait_ge(s_ones, 3)
            pipeline(pool, NT, [(1, lambda u, p: ln.pool_rstd(pool, u, p))])

        @block.vector
        def _(dve):
            mask = w("maskB").unsqueeze(2).broadcast_to([P, GH, T])
            if cross:
                nc.vector.tensor_copy(allow[:, :], w("allow1")).then_inc(s_tb, 1)
                nc.vector.tensor_copy(identb[:, :], w("ident")).then_inc(s_tb, 1)

            def take_spread(u, p):
                done(dve, s_blk, u)
                free(dve, s_S, u)
                for g in range(2):
                    src = pA[:, 384 + T * g:384 + T * g + T].unsqueeze(1).broadcast_to([P, GH, T])
                    if cross:
                        i = nc.vector.scalar_tensor_tensor(spread[:, p, g], src, w("a1_bk")[:, g:g + 1],
                                                           mask, ALU.add, ALU.mult)
                    else:
                        i = nc.vector.tensor_tensor(spread[:, p, g], src, mask, ALU.mult)
                i.then_inc(s_spread, 1)

            def softmax(u, p):
                Sh = S[:, p, :].rearrange("p (h k) -> p h k", k=T)
                done(dve, s_S, u)
                nc.vector.tensor_reduce(mx[:, p, :], Sh, AX, ALU.max).then_inc(s_mx, 1)
                done(dve, s_mx, u)
                free(dve, s_pt if cross else s_o, u)
                nc.vector.tensor_tensor(Pr[:, p, :].rearrange("p (h k) -> p h k", k=T), Sh,
                                        mx[:, p, :].unsqueeze(2).broadcast_to([P, HEADS, T]),
                                        ALU.subtract).then_inc(s_sub, 1)

            def normalise(u, p):
                o = pB[:, 0:144].rearrange("p (h c) -> p h c", c=9)
                done(dve, s_o, u)
                nc.vector.reciprocal(rden[:, p], o[:, :, 8:9]).then_inc(s_rd, 1)
                done(dve, s_rd, u)
                free(dve, s_zt, u)
                nc.vector.tensor_tensor(zn[:, p, :].rearrange("p (h c) -> p h c", c=8), o[:, :, 0:8],
                                        rden[:, p].broadcast_to([P, HEADS, 8]), ALU.mult
                                        ).then_inc(s_zn, 1)

            def residual(u, p):
                done(dve, s_y, u)
                nc.vector.tensor_tensor(X[:, u, :], pB[:, 384:512], X[:, u, :], ALU.add).then_inc(s_add, 1)
                done(dve, s_add, u)
                nc.vector.tensor_tensor(X[:, u, :], X[:, u, :], w("a1_bo"), ALU.add).then_inc(s_x, 1)

            def divide_v(u, p):
                done(dve, s_exp, u)
                done(dve, s_v, u)
                nc.vector.tensor_reduce(sums[:, p, :], Pr[:, p, :].rearrange("p (h k) -> p h k", k=T),
                                        AX, ALU.add).then_inc(s_sum, 1)
                done(dve, s_sum, u)
                free(dve, s_vs, u)
                nc.vector.reciprocal(rden[:, p, :, 0], sums[:, p, :]).then_inc(s_rd, 1)
                done(dve, s_rd, u)
                free(dve, s_o, u)
                nc.vector.tensor_tensor(V[:, p], vraw[:, p, :].rearrange("p (h c) -> p h c", c=8),
                                        rden[:, p].broadcast_to([P, HEADS, 8]), ALU.mult
                                        ).then_inc(s_vs, 1)

            def keep_w(u, p):
                done(dve, s_y, u)
                nc.vector.tensor_copy(net.Y[:, u, :], pB[:, 384:512]).then_inc(s_w, 1)

            stats = [(2, lambda u, p: ln.vector_apply(dve, u, p)),
                     (0, lambda u, p: ln.vector_stats(dve, u, p)),
                     (1, lambda u, p: ln.vector_moments(dve, u, p))]
            if cross:
                pipeline(dve, NT, [(4, softmax)] + stats + [(3, take_spread), (5, normalise),
                                                            (6, residual)])
            else:
                dve.wait_ge(s_wz, 1)
                nc.vector.tensor_copy(wow[:, D:2 * D], pA[:, 0:D]).then_inc(s_wzs, 1)
                nc.vector.tensor_copy(wow[:, 0:D], w("f0_wo")).then_inc(s_wzs, 1)
                pipeline(dve, NT, [(4, softmax)] + stats + [(5, divide_v), (3, take_spread), (6, keep_w)])

        @block.scalar
        def _(act):
            act.wait_ge(s_zero, 1)
            if cross:
                act.wait_ge(s_ones, 3)

            def take_xt(u, p):
                done(act, s_xt, u)
                free(act, s_proj, u)
                nc.scalar.activation(xT[:, p, :], pA[:, 0:128], ACT.Copy).then_inc(s_xts, 1)

            def take_blk(u, p):
                done(act, s_proj, u)
                free(act, s_S, u)
                if not cross:
                    free(act, s_vs, u)
                    nc.scalar.activation(vraw[:, p, :], pA[:, 128:256], ACT.Copy).then_inc(s_v, 1)
                for b in range(2):
                    r = slice(64 * b, 64 * b + 64)
                    if cross:
                        for g in range(2):
                            i = nc.scalar.activation(blk[r, p, g, 64 * b:64 * b + 64],
                                                     pA[r, 256 + T * g:256 + T * g + T], ACT.Identity,
                                                     bias=w("a1_bq")[r, g:g + 1])
                    else:
                        i = nc.scalar.activation(blk[r, p, :, 64 * b:64 * b + 64],
                                                 pA[r, 256:384].rearrange("p (g t) -> p g t", t=T),
                                                 ACT.Copy)
                i.then_inc(s_blk, 1)

            def exps(u, p):
                done(act, s_sub, u)
                nc.scalar.activation(Pr[:, p, :], Pr[:, p, :], ACT.Exp, scale=SCALE).then_inc(s_exp, 1)

            def take_v(u, p):
                done(act, s_v, u)
                free(act, s_o, u)
                for h in range(2):
                    r = slice(64 * h, 64 * h + 64)
                    i = nc.scalar.activation(
                        V[r, p, :, :, h, 0:8].rearrange("p b j c -> p (b j) c"),
                        pB[r, 256:384].rearrange("p (n c) -> p n c", c=8), ACT.Copy)
                i.then_inc(s_vs, 1)

            def take_pt(u, p):
                done(act, s_pt, u)
                free(act, s_o, u)
                nc.scalar.activation(PT[:, p].rearrange("p j q -> p (j q)"), PTp[:, :], ACT.Copy
                                     ).then_inc(s_pts, 1)

            def take_zt(u, p):
                done(act, s_zt, u)
                free(act, s_y, u)
                if cross:
                    nc.scalar.activation(zT[:, p, :], pB[:, 256:384], ACT.Identity, bias=w("a1_bv")
                                         ).then_inc(s_zts, 1)
                else:
                    nc.scalar.activation(zT[:, p, :], pB[:, 128:256], ACT.Copy).then_inc(s_zts, 1)

            def take_z(u, p):
                done(act, s_o, u)
                free(act, s_zt, u)
                nc.scalar.activation(zn[:, p, :], pB[:, 0:128], ACT.Copy).then_inc(s_zn, 1)

            def squares(u, p):
                done(act, s_w, u)
                nc.scalar.activation(junk[:, :], pB[:, 256:384], ACT.Square,
                                     accum_out=net.norms[:, 0, u:u + 1] if isinstance(u, int)
                                     else net.norms[:, 0, bass.ds(u, 1)]).then_inc(s_sq, 1)

            if cross:
                pipeline(act, NT, [(4, take_v), (5, take_pt), (2, take_xt), (6, take_zt), (3, take_blk),
                                   (4, exps)])
            else:
                pipeline(act, NT, [(2, take_xt), (6, take_zt), (5, take_z), (3, take_blk), (4, exps),
                                   (6, squares)])

        if cross:
            turnsA = Bank(NT, {"xt": (2, s_xts, 1, 1), "qk": (3, s_spread, 1, 1)})
            turnsB = Bank(NT, {"v": (4, s_vs, 1, 1), "z": (6, s_zts, 1, 1), "o": (5, s_zn, 1, 1),
                               "y": (6, s_x, 1, 1)})
        else:
            turnsA = Bank(NT, {"xt": (2, s_xts, 1, 1), "qk": (3, s_spread, 1, 1)})
            turnsB = Bank(NT, {"z": (6, s_zts, 1, 1), "o": (5, s_zn, 1, 1),
                               "y": (6, s_sq, 1, 1)})

        @block.tensor
        def _(pe):
            def transpose_x(u, p):
                done(pe, ln.s_xn, u)
                turnsA.take(pe, "xt", u)
                nc.tensor.transpose(pA[:, 0:128], xn[:, p, :], w("ident")).then_inc(s_xt, 1)

            def project(u, p):
                done(pe, s_xts, u)
                if cross:
                    landed(pe, s_cT, u, p)
                turnsA.take(pe, "qk", u)
                other = cT if cross else xT
                if not cross:
                    nc.tensor.matmul(pA[:, 128:256], xT[:, p, :], w("f0_wv"), start=True, stop=True)
                for b in range(2):
                    r = slice(64 * b, 64 * b + 64)
                    for g in range(2):
                        c = slice(64 * g, 64 * g + 64)
                        nc.tensor.matmul(pA[r, 256 + T * g:256 + T * g + T], wblk[:, c], xT[:, p, r],
                                         start=True, stop=True)
                        i = nc.tensor.matmul(pA[r, 384 + T * g:384 + T * g + T], wspread[:, c],
                                             other[:, p, r], start=True, stop=True)
                i.then_inc(s_proj, 1)

            def scores(u, p):
                done(pe, s_spread, u)
                free(pe, s_sub, u)
                for g in range(2):
                    out = S[:, p, 512 * g:512 * g + 512]
                    if cross:
                        nc.tensor.matmul(out, identb[:, :],
                                         allow[:, :].unsqueeze(1).broadcast_to([P, GH, T]),
                                         start=True, stop=False)
                    i = nc.tensor.matmul(out, blk[:, p, g, :],
                                         spread[:, p, g].rearrange("p h t -> p (h t)"),
                                         start=not cross, stop=True)
                i.then_inc(s_S, 1)

            def transpose_p(u, p):
                done(pe, s_exp, u)
                free(pe, s_pts, u, bufs=1)
                for j in range(8):
                    i = nc.tensor.transpose(PTp[:, P * j:P * j + P], Pr[:, p, P * j:P * j + P], w("ident"))
                i.then_inc(s_pt, 1)

            def values(u, p):
                turnsB.take(pe, "v", u)
                wv = w("a1_wv").rearrange("p (j h c) -> p h j c", h=2, c=8)
                for b in range(2):
                    for h in range(2):
                        i = nc.tensor.matmul(pB[64 * h:64 * h + 64, 256 + 64 * b:256 + 64 * b + 64],
                                             cT[:, p, 64 * b:64 * b + 64], wv[:, h],
                                             start=True, stop=True)
                i.then_inc(s_v, 1)

            def product_v(u, p):
                done(pe, s_vs, u)
                if cross:
                    done(pe, s_pts, u)
                turnsB.take(pe, "o", u)
                if not cross:
                    nc.tensor.matmul(pB[:, 0:2], w("ident"), w("ident", 0, 2), start=True, stop=True)
                for b in range(2):
                    r = slice(64 * b, 64 * b + 64)
                    if cross:
                        for j in range(8):
                            i = nc.tensor.matmul(pB[r, 18 * j:18 * j + 18], PT[:, p, j, r],
                                                 V[:, p, b, j].rearrange("p h c -> p (h c)"),
                                                 start=True, stop=True)
                    else:
                        for h in range(HEADS):
                            i = nc.tensor.matmul(pB[r, 8 * h:8 * h + 8], Pr[r, p, T * h:T * h + T],
                                                 V[r, p, h, :], start=True, stop=True)
                i.then_inc(s_o, 1)

            def transpose_z(u, p):
                done(pe, s_zn, u)
                turnsB.take(pe, "z", u)
                out = pB[:, 256:384] if cross else pB[:, 128:256]
                nc.tensor.transpose(out, zn[:, p, :], w("ident")).then_inc(s_zt, 1)

            def output(u, p):
                done(pe, s_zts, u)
                turnsB.take(pe, "y", u)
                if cross:
                    i = nc.tensor.matmul(pB[:, 384:512], zT[:, p, :], w("a1_wo"), start=True, stop=True)
                else:
                    i = nc.tensor.matmul(pB[:, 256:512], zT[:, p, :], wow[:, :], start=True, stop=True)
                i.then_inc(s_y, 1)

            if cross:
                pe.wait_ge(s_tb, 2)
                pipeline(pe, NT, [(4, scores), (4, values), (5, transpose_p), (2, transpose_x),
                                  (6, transpose_z), (5, product_v), (3, project), (6, output)])
            else:
                nc.tensor.matmul(pA[:, 0:D], w("f0_woT"), w("f0_wff"), start=True, stop=True
                                 ).then_inc(s_wz, 1)
                pe.wait_ge(s_wzs, 2)
                pipeline(pe, NT, [(4, scores), (2, transpose_x), (6, transpose_z),
                                  (5, product_v), (3, project), (6, output)])


def norm_gelu_stage(net):
    nc, X, Y = net.nc, net.X, net.Y
    PART = NT // 4
    with ExitStack() as ctx:
        sb, ps, sem = opener(net, ctx, "n0")
        sq = sb("squares", [P, PART, D])
        root = sb("root", [P, 2, NT])
        inv = sb("inv", [P, 2, NT])
        s_sq, s_ss, s_rt, s_v, s_m, s_g, s_x = [sem(n) for n in (
            "squares", "sums", "root", "factor", "scaled", "gelu", "x")]
        block = ctx.enter_context(nc.Block())

        @block.sync
        def _(sp):
            clear_stale(net, sp)

        def part(t, k):
            return t[:, PART * k:PART * k + PART, :]

        @block.gpsimd
        def _(pool):
            for k in range(4):
                pool.wait_ge(s_ss, k)
                nc.gpsimd.tensor_tensor(sq[:, :, :], part(Y, k), part(Y, k), ALU.mult).then_inc(s_sq, 1)

        @block.vector
        def _(dve):
            for k in range(4):
                dve.wait_ge(s_sq, k + 1)
                nc.vector.tensor_reduce(net.norms[:, 1, PART * k:PART * k + PART], sq[:, :, :], AX,
                                        ALU.add).then_inc(s_ss, 1)
            dve.wait_ge(s_rt, 1)
            nc.vector.tensor_scalar(root[:, 0], root[:, 0], L2_EPS, None, ALU.max).then_inc(s_v, 1)
            dve.wait_ge(s_v, 1)
            nc.vector.reciprocal(inv[:, 0], root[:, 0]).then_inc(s_v, 1)
            dve.wait_ge(s_v, 2)
            nc.vector.tensor_tensor(root[:, 1], root[:, 1], inv[:, 0], ALU.mult).then_inc(s_v, 1)
            dve.wait_ge(s_v, 3)
            nc.vector.tensor_scalar(root[:, 1], root[:, 1], L2_EPS, None, ALU.max).then_inc(s_v, 1)
            dve.wait_ge(s_v, 4)
            nc.vector.reciprocal(inv[:, 1], root[:, 1]).then_inc(s_v, 1)
            dve.wait_ge(s_v, 5)
            nc.vector.tensor_tensor(inv[:, 0], inv[:, 0], inv[:, 1], ALU.mult).then_inc(s_v, 1)
            dve.wait_ge(s_v, 6)
            for k in range(4):
                f = inv[:, 0, PART * k:PART * k + PART].unsqueeze(2).broadcast_to([P, PART, D])
                nc.vector.tensor_tensor(part(Y, k), part(Y, k), f, ALU.mult).then_inc(s_m, 1)
            for k in range(4):
                dve.wait_ge(s_g, k + 1)
                nc.vector.tensor_tensor(part(X, k), part(X, k), part(Y, k), ALU.add).then_inc(s_x, 1)

        @block.scalar
        def _(act):
            act.wait_ge(s_ss, 4)
            nc.scalar.activation(root[:, :, :], net.norms[:, :, :], ACT.Sqrt).then_inc(s_rt, 1)
            for k in range(4):
                act.wait_ge(s_m, k + 1)
                nc.scalar.activation(part(Y, k), part(Y, k), ACT.Gelu).then_inc(s_g, 1)


def attention2_stage(net):
    nc, X, w = net.nc, net.X, net.w
    SCALE = 64 ** -0.5
    with ExitStack() as ctx:
        sb, ps, sem = opener(net, ctx, "a2")
        xn = sb("xn", [P, 2, D])
        xT = sb("xT", [P, 2, P])
        cT = sb("cT", [P, 2, P])
        q = sb("q", [P, 2, 4, P])
        k = sb("k", [P, 2, 4, 2, P])
        V = sb("V", [P, 2, 2, 4, 2, 65])
        Pr = sb("Pr", [P, 2, 512])
        PT = sb("PT", [P, 2, 4, P])
        mx = sb("mx", [P, 2, 8])
        rden = sb("rden", [P, 2, 2, 4, 1])
        zn = sb("zn", [P, 2, 512])
        zT = sb("zT", [P, 2, 4, P])
        S = ps("S", [P, 2, 512])
        pQ, pK, pV, pT = ps("pQ", [P, 512]), ps("pK", [P, 512]), ps("pV", [P, 512]), ps("pT", [P, 512])
        pO = ps("pO", [P, 2, 512])
        s_ones, s_zero = sem("ones"), sem("zero")
        s_cT = [sem("cT_even"), sem("cT_odd")]
        s_xt, s_xts, s_q, s_qs, s_k, s_ks = [sem(n) for n in ("xt", "xt_out", "q", "q_out", "k", "k_out")]
        s_v, s_vs, s_S, s_mx, s_sub, s_exp = [sem(n) for n in ("v", "v_out", "scores", "max", "sub", "exp")]
        s_pt, s_pts, s_o, s_rd, s_zn = [sem(n) for n in ("pt", "pt_out", "o", "rden", "zn")]
        s_zt, s_zts, s_y, s_add, s_x = [sem(n) for n in ("zt", "zt_out", "y", "bias_added", "x")]
        ln = LayerNorm(net, sb, sem, xn, s_xt)
        block = ctx.enter_context(nc.Block())

        @block.sync
        def _(sp):
            clear_stale(net, sp)
            def load_context(u, p):
                free(sp, s_v, u)
                sp.dma_start(cT[:, p, :], net.dram["ctxT"][u]).then_inc(s_cT[p], 16)
            pipeline(sp, NT, [(0, load_context)])

        @block.gpsimd
        def _(pool):
            ln.setup(pool)
            nc.gpsimd.memset(k[:, :, :, :, :], 0.0).then_inc(s_zero, 1)
            nc.gpsimd.memset(V[:, :, :, :, :, :], 0.0).then_inc(s_ones, 1)
            for h in range(2):
                pool.wait_ge(s_ones, h + 1)
                nc.gpsimd.memset(V[64 * h:64 * h + 64, :, :, :, h, 64:65], 1.0).then_inc(s_ones, 1)
            pool.wait_ge(s_ones, 3)
            pipeline(pool, NT, [(1, lambda u, p: ln.pool_rstd(pool, u, p))])

        @block.vector
        def _(dve):
            dve.wait_ge(s_zero, 1)

            def take_k(u, p):
                done(dve, s_k, u)
                free(dve, s_S, u)
                for h in range(2):
                    r = slice(64 * h, 64 * h + 64)
                    i = nc.vector.tensor_copy(k[r, p, :, h, :], pK[r, :].rearrange("p (j t) -> p j t", j=4))
                i.then_inc(s_ks, 1)

            def softmax(u, p):
                Sh = S[:, p, :].rearrange("p (h k) -> p h k", k=T)
                done(dve, s_S, u)
                nc.vector.tensor_reduce(mx[:, p, :], Sh, AX, ALU.max).then_inc(s_mx, 1)
                done(dve, s_mx, u)
                free(dve, s_pt, u)
                nc.vector.tensor_tensor(Pr[:, p, :].rearrange("p (h k) -> p h k", k=T), Sh,
                                        mx[:, p, :].unsqueeze(2).broadcast_to([P, 8, T]),
                                        ALU.subtract).then_inc(s_sub, 1)

            def normalise(u, p):
                o = pO[:, :, 0:260].rearrange("p a (h c) -> p a h c", c=65)
                done(dve, s_o, u)
                nc.vector.reciprocal(rden[:, p], o[:, :, :, 64:65]).then_inc(s_rd, 1)
                done(dve, s_rd, u)
                free(dve, s_zt, u)
                nc.vector.tensor_tensor(zn[:, p, :].rearrange("p (a h c) -> p a h c", a=2, c=64),
                                        o[:, :, :, 0:64], rden[:, p].broadcast_to([P, 2, 4, 64]),
                                        ALU.mult).then_inc(s_zn, 1)

            def residual(u, p):
                done(dve, s_y, u)
                nc.vector.tensor_tensor(X[:, u, :], pK[:, 0:128], X[:, u, :], ALU.add).then_inc(s_add, 1)
                done(dve, s_add, u)
                nc.vector.tensor_tensor(X[:, u, :], X[:, u, :], w("a2_bo"), ALU.add).then_inc(s_x, 1)

            pipeline(dve, NT, [(4, softmax), (2, lambda u, p: ln.vector_apply(dve, u, p)),
                               (0, lambda u, p: ln.vector_stats(dve, u, p)),
                               (1, lambda u, p: ln.vector_moments(dve, u, p)),
                               (3, take_k), (5, normalise), (6, residual)])

        @block.scalar
        def _(act):
            act.wait_ge(s_ones, 3)

            def take_xt(u, p):
                done(act, s_xt, u)
                free(act, s_q, u)
                nc.scalar.activation(xT[:, p, :], pQ[:, 0:128], ACT.Copy).then_inc(s_xts, 1)

            def take_q(u, p):
                done(act, s_q, u)
                free(act, s_S, u)
                nc.scalar.activation(q[:, p].rearrange("p j t -> p (j t)"), pQ[:, :], ACT.Copy
                                     ).then_inc(s_qs, 1)

            def take_v(u, p):
                done(act, s_v, u)
                free(act, s_o, u)
                for h in range(2):
                    r = slice(64 * h, 64 * h + 64)
                    i = nc.scalar.activation(V[r, p, :, :, h, 0:64].rearrange("p b j c -> p (b j) c"),
                                             pV[r, :].rearrange("p (n c) -> p n c", c=64), ACT.Copy)
                i.then_inc(s_vs, 1)

            def exps(u, p):
                done(act, s_sub, u)
                nc.scalar.activation(Pr[:, p, :], Pr[:, p, :], ACT.Exp, scale=SCALE).then_inc(s_exp, 1)

            def take_pt(u, p):
                done(act, s_pt, u)
                free(act, s_o, u)
                nc.scalar.activation(PT[:, p].rearrange("p j t -> p (j t)"), pT[:, :], ACT.Copy
                                     ).then_inc(s_pts, 1)

            def take_zt(u, p):
                done(act, s_zt, u)
                free(act, s_y, u)
                nc.scalar.activation(zT[:, p].rearrange("p j t -> p (j t)"), pT[:, :], ACT.Copy
                                     ).then_inc(s_zts, 1)

            pipeline(act, NT, [(5, take_pt), (2, take_xt), (6, take_zt), (3, take_q), (4, take_v),
                               (4, exps)])

        turnsQ = Bank(NT, {"xt": (2, s_xts, 1, 1), "q": (3, s_qs, 1, 1)})
        turnsK = Bank(NT, {"k": (3, s_ks, 1, 1), "y": (6, s_x, 1, 1)})
        turnsT = Bank(NT, {"pt": (5, s_pts, 1, 1), "zt": (6, s_zts, 1, 1)})

        @block.tensor
        def _(pe):
            def transpose_x(u, p):
                done(pe, ln.s_xn, u)
                turnsQ.take(pe, "xt", u)
                nc.tensor.transpose(pQ[:, 0:128], xn[:, p, :], w("ident")).then_inc(s_xt, 1)

            def project(u, p):
                landed(pe, s_cT, u, p)
                turnsK.take(pe, "k", u)
                for j in range(4):
                    i = nc.tensor.matmul(pK[:, P * j:P * j + P], w("a2_wk", P * j, P * j + P),
                                         cT[:, p, :], start=True, stop=True)
                i.then_inc(s_k, 1)
                done(pe, s_xts, u)
                turnsQ.take(pe, "q", u)
                for j in range(4):
                    i = nc.tensor.matmul(pQ[:, P * j:P * j + P], w("a2_wq", P * j, P * j + P),
                                         xT[:, p, :], start=True, stop=True)
                i.then_inc(s_q, 1)

            def values(u, p):
                free(pe, s_vs, u, bufs=1)
                wv = w("a2_wv").rearrange("p (j h c) -> p h j c", h=2, c=64)
                for b in range(2):
                    for h in range(2):
                        i = nc.tensor.matmul(pV[64 * h:64 * h + 64, 256 * b:256 * b + 256],
                                             cT[:, p, 64 * b:64 * b + 64], wv[:, h],
                                             start=True, stop=True)
                i.then_inc(s_v, 1)

            def scores(u, p):
                done(pe, s_qs, u)
                done(pe, s_ks, u)
                free(pe, s_sub, u)
                for b in range(2):
                    r = slice(64 * b, 64 * b + 64)
                    for j in range(4):
                        i = nc.tensor.matmul(S[r, p, P * j:P * j + P], q[:, p, j, r], k[:, p, j, :, r],
                                             start=True, stop=True)
                i.then_inc(s_S, 1)

            def transpose_p(u, p):
                done(pe, s_exp, u)
                turnsT.take(pe, "pt", u)
                for j in range(4):
                    i = nc.tensor.transpose(pT[:, P * j:P * j + P], Pr[:, p, P * j:P * j + P], w("ident"))
                i.then_inc(s_pt, 1)

            def product_v(u, p):
                done(pe, s_pts, u)
                done(pe, s_vs, u)
                free(pe, s_zn, u, bufs=1)
                for b in range(2):
                    r = slice(64 * b, 64 * b + 64)
                    for j in range(4):
                        i = nc.tensor.matmul(pO[r, j // 2, 130 * (j % 2):130 * (j % 2) + 130],
                                             PT[:, p, j, r], V[:, p, b, j].rearrange("p h c -> p (h c)"),
                                             start=True, stop=True)
                i.then_inc(s_o, 1)

            def transpose_z(u, p):
                done(pe, s_zn, u)
                turnsT.take(pe, "zt", u)
                for j in range(4):
                    i = nc.tensor.transpose(pT[:, P * j:P * j + P], zn[:, p, P * j:P * j + P], w("ident"))
                i.then_inc(s_zt, 1)

            def output(u, p):
                done(pe, s_zts, u)
                turnsK.take(pe, "y", u)
                for j in range(4):
                    i = nc.tensor.matmul(pK[:, 0:128], zT[:, p, j, :], w("a2_wo", P * j, P * j + P),
                                         start=(j == 0), stop=(j == 3))
                i.then_inc(s_y, 1)

            pipeline(pe, NT, [(4, scores), (5, transpose_p), (2, transpose_x), (4, values),
                              (5, product_v), (6, transpose_z), (3, project), (6, output)])


NU = NT // 2


def pair(t, u):
    return t[:, 2 * u:2 * u + 2, :] if isinstance(u, int) else t[:, bass.ds(2 * u, 2), :]


class PairNorm:

    def __init__(self, net, sb, sem, name, used=None):
        self.net, self.used = net, used
        self.stats = sb(name + "_stats", [P, 2, 2, 6])
        self.moments = sb(name + "_moments", [P, 2, 2, 2])
        self.rstd = sb(name + "_rstd", [P, 2, 2, 2])
        self.half = sb(name + "_half", [P, 2])
        self.spare = sb(name + "_spare", [1, 1])
        self.s_half, self.s_stats, self.s_spare = sem(name + "_half"), sem(name + "_stats"), sem(name + "_sp")
        self.s_moments, self.s_vareps = sem(name + "_moments"), sem(name + "_vareps")
        self.s_rstd, self.s_out = sem(name + "_rstd"), sem(name + "_out")

    def setup(self, pool):
        self.net.nc.gpsimd.memset(self.half[:, 0:1], -0.5).then_inc(self.s_half, 1)
        self.net.nc.gpsimd.memset(self.half[:, 1:2], LN_EPS).then_inc(self.s_half, 1)
        pool.wait_ge(self.s_half, 2)

    def vector_moments(self, dve, u, p, src):
        nc = self.net.nc
        for t in range(2):
            i = nc.vector.bn_stats(self.stats[:, p, t, :], src(t))
        i.then_inc(self.s_stats, 1)
        done(dve, self.s_stats, u)
        free(dve, self.s_out, u)
        nc.vector.memset(self.spare[:, :], 0.0).then_inc(self.s_spare, 1)
        for t in range(2):
            i = nc.vector.bn_aggr(self.moments[:, p, t, :], self.stats[:, p, t, :])
        i.then_inc(self.s_moments, 1)

    def pool_rstd(self, pool, u, p):
        nc = self.net.nc
        done(pool, self.s_moments, u)
        nc.gpsimd.tensor_tensor(self.rstd[:, p, :, 0:1], self.moments[:, p, :, 1:2],
                                self.half[:, 1:2].unsqueeze(1).broadcast_to([P, 2, 1]), ALU.add
                                ).then_inc(self.s_vareps, 1)
        done(pool, self.s_vareps, u)
        nc.gpsimd.tensor_tensor(self.rstd[:, p, :, 1:2], self.rstd[:, p, :, 0:1],
                                self.half[:, 0:1].unsqueeze(1).broadcast_to([P, 2, 1]), ALU.pow
                                ).then_inc(self.s_rstd, 1)

    def vector_apply(self, dve, u, p, src, dsts):
        done(dve, self.s_moments, u)
        done(dve, self.s_rstd, u)
        if self.used is not None:
            free(dve, self.used, u)
        for t in range(2):
            for dst in dsts(t):
                i = self.net.nc.vector.tensor_scalar(dst, src(t), self.moments[:, p, t, 0:1],
                                                     self.rstd[:, p, t, 1:2], ALU.subtract, ALU.mult)
        i.then_inc(self.s_out, 1)


def tile_of(t, u, k):
    return t[:, 2 * u + k, :]


def affine(net, dve, u, x, gain, bias, s_gain, s_bias, out):
    nc, w = net.nc, net.w
    nc.vector.tensor_tensor(x, x, w(gain).unsqueeze(1).broadcast_to([P, 2, D]), ALU.mult
                            ).then_inc(s_gain, 1)
    done(dve, s_gain, u)
    return nc.vector.tensor_tensor(out, x, w(bias).unsqueeze(1).broadcast_to([P, 2, D]), ALU.add
                                   ).then_inc(s_bias, 1)


def attention3_stage(net, cross):
    nc, X, Y, R, w = net.nc, net.X, net.Y, net.R, net.w
    SCALE = 8 ** -0.5
    i2 = "2" if cross else "1"
    with ExitStack() as ctx:
        sb, ps, sem = opener(net, ctx, "c3" if cross else "s3")
        xs = sb("xs", [P, 2, 2, D])
        xT = sb("xT", [P, 2, 2 * P])
        cT = sb("cT", [P, 2, 2, P]) if cross else None
        qk = sb("qk", [P, 2, 2, 2 * P])
        V = sb("V", [P, NT, D + 1])
        Se = sb("Se", [P, 2, 2, T])
        nz = sb("nz", [P, 2, 2, T])
        ln_ = sb("lengths", [P, 2, 2])
        pad = sb("pad", [P, 2, 2, T])
        mx = sb("mx", [P, 2, 2])
        Pr = sb("Pr", [P, 2, 2, P])
        PT = sb("PT", [P, 2, 2, P])
        rden = sb("rden", [P, 2, 2, 1])
        y = sb("y", [P, 2, 2, D])
        pX, pQ, pV, pS = [ps(n, [P, 512]) for n in ("pX", "pQ", "pV", "pS")]
        pL, pT, pO = [ps(n, [P, 512]) for n in ("pL", "pT", "pO")]
        s_zero, s_ones = sem("zero"), sem("ones")
        s_xs, s_xt, s_xts, s_qk, s_qks, s_v, s_vs = [sem(n) for n in (
            "xs", "xt", "xt_out", "qk", "qk_out", "v", "v_out")]
        s_S, s_Se, s_nz, s_L, s_len, s_pad, s_e1, s_e2, s_mx, s_sub, s_exp = [sem(n) for n in (
            "scores", "scores_out", "nonzero", "first_row", "lengths", "pad", "masked", "masked2",
            "max", "sub", "exp")]
        s_pt, s_pts, s_o, s_rd, s_y, s_g, s_b = [sem(n) for n in (
            "pt", "pt_out", "o", "rden", "y", "gain", "bias")]
        n_in = None if cross else PairNorm(net, sb, sem, "nin", s_xt)
        n_out = PairNorm(net, sb, sem, "nout")
        s_in = s_xs if cross else n_in.s_out
        s_cT = [sem("cT_even"), sem("cT_odd")]
        block = ctx.enter_context(nc.Block())

        if cross:
            @block.sync
            def _(sp):
                clear_stale(net, sp)
                ctxT = net.dram["ctxT"].rearrange("n d t -> d n t")

                def load_context(u, p):
                    free(sp, s_v, u)
                    sp.dma_start(cT[:, p], ctxT[:, 2 * u:2 * u + 2, :] if isinstance(u, int)
                                 else ctxT[:, bass.ds(2 * u, 2), :]).then_inc(s_cT[p], 16)
                pipeline(sp, NU, [(0, load_context)])
        else:
            @block.sync
            def _(sp):
                clear_stale(net, sp)

        @block.gpsimd
        def _(pool):
            nc.gpsimd.memset(Pr[:, :, :, :], 0.0).then_inc(s_zero, 1)
            nc.gpsimd.memset(V[:, :, D:D + 1], 1.0).then_inc(s_ones, 1)
            n_out.setup(pool)
            steps = [(7, lambda u, p: n_out.pool_rstd(pool, u, p))]
            if not cross:
                n_in.setup(pool)
                steps.append((0, lambda u, p: n_in.pool_rstd(pool, u, p)))
            pipeline(pool, NU, steps)

        @block.vector
        def _(dve):
            def copy_in(u, p):
                free(dve, s_xt, u)
                nc.vector.tensor_copy(xs[:, p], pair(Y, u)).then_inc(s_xs, 1)

            def moments_in(u, p):
                n_in.vector_moments(dve, u, p, lambda t: tile_of(X, u, t))

            def apply_in(u, p):
                n_in.vector_apply(dve, u, p, lambda t: tile_of(X, u, t),
                                  lambda t: (tile_of(R, u, t), xs[:, p, t]))

            def take_v(u, p):
                done(dve, s_v, u)
                nc.vector.tensor_copy(pair(V, u)[:, :, 0:D], pV[:, 0:2 * D].rearrange("p (a d) -> p a d", a=2)
                                      ).then_inc(s_vs, 1)

            def take_scores(u, p):
                done(dve, s_S, u)
                free(dve, s_e1, u)
                nc.vector.tensor_copy(Se[:, p], pS[:, 0:2 * T].rearrange("p (a k) -> p a k", a=2)
                                      ).then_inc(s_Se, 1)
                done(dve, s_Se, u)
                free(dve, s_L, u)
                nc.vector.tensor_scalar(nz[:, p], Se[:, p], 0.0, None, ALU.not_equal).then_inc(s_nz, 1)

            def softmax(u, p):
                done(dve, s_L, u)
                nc.vector.tensor_reduce(ln_[:, p], pL[:, 0:2 * T].rearrange("p (a k) -> p a k", a=2), AX,
                                        ALU.add).then_inc(s_len, 1)
                done(dve, s_len, u)
                nc.vector.tensor_tensor(pad[:, p], w("iota64").unsqueeze(1).broadcast_to([P, 2, T]),
                                        ln_[:, p].unsqueeze(2).broadcast_to([P, 2, T]), ALU.is_ge
                                        ).then_inc(s_pad, 1)
                done(dve, s_pad, u)
                free(dve, s_exp, u)
                nc.vector.scalar_tensor_tensor(pad[:, p], pad[:, p], NEG, Se[:, p], ALU.mult, ALU.add
                                               ).then_inc(s_e1, 1)
                done(dve, s_e1, u)
                if not cross:
                    nc.vector.tensor_tensor(pad[:, p], pad[:, p],
                                            w("causal").unsqueeze(1).broadcast_to([P, 2, T]), ALU.add
                                            ).then_inc(s_e2, 1)
                    done(dve, s_e2, u)
                nc.vector.tensor_reduce(mx[:, p], pad[:, p], AX, ALU.max).then_inc(s_mx, 1)
                done(dve, s_mx, u)
                nc.vector.tensor_tensor(pad[:, p], pad[:, p],
                                        mx[:, p].unsqueeze(2).broadcast_to([P, 2, T]), ALU.subtract
                                        ).then_inc(s_sub, 1)

            def add_z(u, p):
                done(dve, s_o, u)
                o = pO[:, 0:2 * (D + 1)].rearrange("p (a d) -> p a d", a=2)
                nc.vector.reciprocal(rden[:, p], o[:, :, D:D + 1]).then_inc(s_rd, 1)
                done(dve, s_rd, u)
                free(dve, s_b, u)
                for t in range(2):
                    i = nc.vector.scalar_tensor_tensor(y[:, p, t], o[:, t, 0:D], rden[:, p, t],
                                                       tile_of(Y if cross else R, u, t), ALU.mult, ALU.add)
                i.then_inc(s_y, 1)
                done(dve, s_y, u)
                n_out.vector_moments(dve, u, p, lambda t: y[:, p, t])

            def finish(u, p):
                n_out.vector_apply(dve, u, p, lambda t: y[:, p, t], lambda t: (y[:, p, t],))
                done(dve, n_out.s_out, u)
                affine(net, dve, u, y[:, p], "a3_g" + i2, "a3_c" + i2, s_g, s_b, pair(Y, u))

            tail = [(2, take_v), (3, take_scores), (4, softmax), (7, add_z), (8, finish)]
            if cross:
                pipeline(dve, NU, [(1, copy_in)] + tail)
            else:
                pipeline(dve, NU, [(0, moments_in), (1, apply_in)] + tail)

        @block.scalar
        def _(act):
            act.wait_ge(s_zero, 1)

            def take_xt(u, p):
                done(act, s_xt, u)
                free(act, s_v, u)
                nc.scalar.activation(xT[:, p, :], pX[:, 0:2 * P], ACT.Copy).then_inc(s_xts, 1)

            def take_qk(u, p):
                done(act, s_qk, u)
                free(act, s_S, u)
                nc.scalar.activation(qk[:, p].rearrange("p a t -> p (a t)"), pQ[:, :], ACT.Copy
                                     ).then_inc(s_qks, 1)

            def exps(u, p):
                done(act, s_sub, u)
                free(act, s_pt, u)
                for b in range(2):
                    r = slice(64 * b, 64 * b + 64)
                    i = nc.scalar.activation(Pr[r, p, :, r], pad[r, p], ACT.Exp, scale=SCALE)
                i.then_inc(s_exp, 1)

            def take_pt(u, p):
                done(act, s_pt, u)
                free(act, s_o, u)
                nc.scalar.activation(PT[:, p].rearrange("p a t -> p (a t)"), pT[:, 0:2 * P], ACT.Copy
                                     ).then_inc(s_pts, 1)

            pipeline(act, NU, [(1, take_xt), (2, take_qk), (6, take_pt), (5, exps)])

        @block.tensor
        def _(pe):
            pe.wait_ge(s_ones, 1)

            def transpose_x(u, p):
                done(pe, s_in, u)
                free(pe, s_xts, u, bufs=1)
                for t in range(2):
                    i = nc.tensor.transpose(pX[:, P * t:P * t + P], xs[:, p, t], w("ident"))
                i.then_inc(s_xt, 1)

            def project(u, p):
                done(pe, s_xts, u)
                free(pe, s_qks, u, bufs=1)
                if cross:
                    landed(pe, s_cT, u, p)
                    other = cT[:, p].rearrange("p a t -> p (a t)")
                else:
                    other = xT[:, p, :]
                nc.tensor.matmul(pQ[:, 0:2 * P], w("a3_wq" + i2), xT[:, p, :], start=True, stop=True)
                nc.tensor.matmul(pQ[:, 2 * P:4 * P], w("a3_wk" + i2), other, start=True, stop=True
                                 ).then_inc(s_qk, 1)
                free(pe, s_vs, u, bufs=1)
                for t in range(2):
                    i = nc.tensor.matmul(pV[:, P * t:P * t + P], other[:, P * t:P * t + P],
                                         w("a3_wv" + i2), start=True, stop=True)
                i.then_inc(s_v, 1)

            def scores(u, p):
                done(pe, s_qks, u)
                free(pe, s_Se, u, bufs=1)
                for t in range(2):
                    for b in range(2):
                        c = slice(P * t + T * b, P * t + T * b + T)
                        i = nc.tensor.matmul(pS[T * b:T * b + T, T * t:T * t + T], qk[:, p, 0, c],
                                             qk[:, p, 1, c], start=True, stop=True)
                i.then_inc(s_S, 1)

            def first_rows(u, p):
                done(pe, s_nz, u)
                free(pe, s_len, u, bufs=1)
                nc.tensor.matmul(pL[:, 0:2 * T], w("sel0"), nz[:, p].rearrange("p a k -> p (a k)"),
                                 start=True, stop=True).then_inc(s_L, 1)

            def transpose_p(u, p):
                done(pe, s_exp, u)
                free(pe, s_pts, u, bufs=1)
                for t in range(2):
                    i = nc.tensor.transpose(pT[:, P * t:P * t + P], Pr[:, p, t], w("ident"))
                i.then_inc(s_pt, 1)

            def product_v(u, p):
                done(pe, s_pts, u)
                done(pe, s_vs, u)
                free(pe, s_y, u, bufs=1)
                for t in range(2):
                    i = nc.tensor.matmul(pO[:, (D + 1) * t:(D + 1) * (t + 1)], PT[:, p, t], tile_of(V, u, t),
                                         start=True, stop=True)
                i.then_inc(s_o, 1)

            pipeline(pe, NU, [(7, product_v), (6, transpose_p), (4, first_rows), (3, scores),
                              (1, transpose_x), (2, project)])


def mlp3_stage(net):
    nc, X, Y, w = net.nc, net.X, net.Y, net.w
    with ExitStack() as ctx:
        sb, ps, sem = opener(net, ctx, "m3")
        xs, xT, h, y = sb("xs", [P, 2, 2, D]), sb("xT", [P, 2, 2 * P]), sb("h", [P, 2, 2 * P]), sb("y", [P, 2, 2, D])
        pX, pH, pO = ps("pX", [P, 512]), ps("pH", [P, 512]), ps("pO", [P, 512])
        s_xs, s_xt, s_xts, s_h, s_hs, s_o, s_y1, s_y, s_g, s_b, s_x = [sem(n) for n in (
            "xs", "xt", "xt_out", "h", "h_out", "o", "y1", "y", "gain", "bias", "x")]
        norm = PairNorm(net, sb, sem, "norm")
        block = ctx.enter_context(nc.Block())

        @block.sync
        def _(sp):
            clear_stale(net, sp)

        @block.gpsimd
        def _(pool):
            norm.setup(pool)
            pipeline(pool, NU, [(3, lambda u, p: norm.pool_rstd(pool, u, p))])

        @block.vector
        def _(dve):
            def copy_in(u, p):
                free(dve, s_xt, u)
                nc.vector.tensor_copy(xs[:, p], pair(Y, u)).then_inc(s_xs, 1)

            def add_h(u, p):
                done(dve, s_o, u)
                free(dve, s_x, u)
                nc.vector.tensor_tensor(y[:, p], pO[:, 0:2 * D].rearrange("p (a d) -> p a d", a=2),
                                        pair(Y, u), ALU.add).then_inc(s_y1, 1)
                done(dve, s_y1, u)
                nc.vector.tensor_tensor(y[:, p], y[:, p], w("a3_b2").unsqueeze(1).broadcast_to([P, 2, D]),
                                        ALU.add).then_inc(s_y, 1)
                done(dve, s_y, u)
                norm.vector_moments(dve, u, p, lambda t: y[:, p, t])

            def finish(u, p):
                norm.vector_apply(dve, u, p, lambda t: y[:, p, t], lambda t: (y[:, p, t],))
                done(dve, norm.s_out, u)
                affine(net, dve, u, y[:, p], "a3_g3", "a3_c3", s_g, s_b, y[:, p])
                done(dve, s_b, u)
                nc.vector.tensor_tensor(pair(X, u), pair(X, u), y[:, p], ALU.add).then_inc(s_x, 1)

            pipeline(dve, NU, [(0, copy_in), (3, add_h), (4, finish)])

        @block.scalar
        def _(act):
            def take_xt(u, p):
                done(act, s_xt, u)
                free(act, s_h, u)
                nc.scalar.activation(xT[:, p, :], pX[:, 0:2 * P], ACT.Copy).then_inc(s_xts, 1)

            def relu(u, p):
                done(act, s_h, u)
                free(act, s_o, u)
                nc.scalar.activation(h[:, p, :], pH[:, 0:2 * P], ACT.Relu, bias=w("a3_b1")).then_inc(s_hs, 1)

            pipeline(act, NU, [(1, take_xt), (2, relu)])

        @block.tensor
        def _(pe):
            def transpose_x(u, p):
                done(pe, s_xs, u)
                free(pe, s_xts, u, bufs=1)
                for t in range(2):
                    i = nc.tensor.transpose(pX[:, P * t:P * t + P], xs[:, p, t], w("ident"))
                i.then_inc(s_xt, 1)

            def hidden(u, p):
                done(pe, s_xts, u)
                free(pe, s_hs, u, bufs=1)
                nc.tensor.matmul(pH[:, 0:2 * P], w("a3_fc1"), xT[:, p, :], start=True, stop=True
                                 ).then_inc(s_h, 1)

            def output(u, p):
                done(pe, s_hs, u)
                free(pe, s_y1, u, bufs=1)
                for t in range(2):
                    i = nc.tensor.matmul(pO[:, D * t:D * t + D], h[:, p, P * t:P * t + P], w("a3_fc2"),
                                         start=True, stop=True)
                i.then_inc(s_o, 1)

            pipeline(pe, NU, [(1, transpose_x), (2, hidden), (3, output)])


def shift3_stage(net):
    nc, X, w = net.nc, net.X, net.w
    with ExitStack() as ctx:
        sb, ps, sem = opener(net, ctx, "f3")
        xs = sb("xs", [P, 2, 2, D])
        xT = sb("xT", [P, 2, 4, T + 1])
        mu = sb("mu", [P, 4])
        part = sb("part", [P, 2, 2, 4, T])
        mix = sb("mix", [P, 2, 2, 4, T])
        r, k1, k2, o = [sb(n, [P, 2, 2 * D]) for n in ("r", "k1", "k2", "o")]
        pX, pR, pK, pW = [ps(n, [P, 512]) for n in ("pX", "pR", "pK", "pW")]
        s_mu, s_zero, s_xt, s_xts, s_part, s_mix, s_r, s_rs, s_k, s_k1, s_k2, s_w, s_o, s_x = [
            sem(n) for n in ("mu", "zero", "xt", "xt_out", "part", "mix", "r", "r_out", "k", "k1", "k2",
                             "w", "o", "x")]
        norm = PairNorm(net, sb, sem, "norm", s_xt)
        block = ctx.enter_context(nc.Block())

        @block.sync
        def _(sp):
            clear_stale(net, sp)

        @block.gpsimd
        def _(pool):
            nc.gpsimd.memset(xT[:, :, :, 0:1], 0.0).then_inc(s_zero, 1)
            norm.setup(pool)
            pipeline(pool, NU, [(0, lambda u, p: norm.pool_rstd(pool, u, p))])

        @block.vector
        def _(dve):
            for n, m in enumerate(("f3_mr", "f3_mk")):
                nc.vector.tensor_copy(mu[:, n:n + 1], w(m))
                nc.vector.tensor_scalar(mu[:, n + 2:n + 3], w(m), -1.0, 1.0, ALU.mult, ALU.add
                                        ).then_inc(s_mu, 1)
            dve.wait_ge(s_mu, 2)
            dve.wait_ge(s_zero, 1)

            def mixes(u, p):
                done(dve, s_xts, u)
                free(dve, s_k, u)
                for n in range(2):
                    i = nc.vector.tensor_scalar(part[:, p, n], xT[:, p, :, 0:T], mu[:, n + 2:n + 3], None,
                                                ALU.mult)
                i.then_inc(s_part, 1)
                done(dve, s_part, u)
                for n in range(2):
                    i = nc.vector.scalar_tensor_tensor(mix[:, p, n], xT[:, p, :, 1:T + 1], mu[:, n:n + 1],
                                                       part[:, p, n], ALU.mult, ALU.add)
                i.then_inc(s_mix, 1)

            def finish(u, p):
                done(dve, s_w, u)
                done(dve, s_rs, u)
                nc.vector.tensor_tensor(o[:, p, :], pW[:, 0:2 * D], r[:, p, :], ALU.mult).then_inc(s_o, 1)
                done(dve, s_o, u)
                nc.vector.tensor_tensor(pair(X, u), pair(X, u), o[:, p, :].rearrange("p (a d) -> p a d", a=2),
                                        ALU.add).then_inc(s_x, 1)

            pipeline(dve, NU, [
                (0, lambda u, p: norm.vector_moments(dve, u, p, lambda t: tile_of(X, u, t))),
                (1, lambda u, p: norm.vector_apply(dve, u, p, lambda t: tile_of(X, u, t),
                                                   lambda t: (xs[:, p, t],))),
                (2, mixes), (5, finish)])

        @block.scalar
        def _(act):
            def take_xt(u, p):
                done(act, s_xt, u)
                free(act, s_mix, u)
                nc.scalar.activation(xT[:, p, :, 1:T + 1], pX[:, 0:2 * P].rearrange("p (b t) -> p b t", t=T),
                                     ACT.Copy).then_inc(s_xts, 1)

            def gates(u, p):
                done(act, s_r, u)
                free(act, s_o, u)
                nc.scalar.activation(r[:, p, :], pR[:, 0:2 * D], ACT.Sigmoid).then_inc(s_rs, 1)
                done(act, s_k, u)
                free(act, s_w, u)
                nc.scalar.activation(k1[:, p, :], pK[:, 0:2 * D], ACT.Relu).then_inc(s_k1, 1)
                done(act, s_k1, u)
                nc.scalar.activation(k2[:, p, :], k1[:, p, :], ACT.Square).then_inc(s_k2, 1)

            pipeline(act, NU, [(1, take_xt), (3, gates)])

        @block.tensor
        def _(pe):
            def transpose_x(u, p):
                done(pe, norm.s_out, u)
                free(pe, s_xts, u, bufs=1)
                for t in range(2):
                    i = nc.tensor.transpose(pX[:, P * t:P * t + P], xs[:, p, t], w("ident"))
                i.then_inc(s_xt, 1)

            def project(u, p):
                done(pe, s_mix, u)
                free(pe, s_rs, u, bufs=1)
                m = mix[:, p].rearrange("p n b t -> p n (b t)")
                for t in range(2):
                    i = nc.tensor.matmul(pR[:, D * t:D * t + D], m[:, 0, P * t:P * t + P], w("f3_wr"),
                                         start=True, stop=True)
                i.then_inc(s_r, 1)
                free(pe, s_k1, u, bufs=1)
                nc.tensor.matmul(pK[:, 0:2 * P], w("f3_wk"), m[:, 1, :], start=True, stop=True
                                 ).then_inc(s_k, 1)

            def output(u, p):
                done(pe, s_k2, u)
                free(pe, s_o, u, bufs=1)
                for t in range(2):
                    i = nc.tensor.matmul(pW[:, D * t:D * t + D], k2[:, p, P * t:P * t + P], w("f3_wv"),
                                         start=True, stop=True)
                i.then_inc(s_w, 1)

            pipeline(pe, NU, [(1, transpose_x), (4, output), (3, project)])


class Routing:

    def __init__(self, ctx, net, first):
        nc = net.nc
        name = "r1" if first else "r2"

        def sb(n, shape, dt=F32):
            return ctx.enter_context(nc.sbuf_tensor(f"{name}_{n}", shape, dt))
        self.first = first

        self.s_put = net.software_sems.pop()
        self.s_got = [net.software_sems.pop() for _ in range(GATHER_PARTS)]
        self.logits = sb("logits", [P, NT, E])
        self.weight = sb("weight", [P, TOPK, NT])
        self.put = sb("put", [P, TOPK, NT], U32)
        self.get = self.put if first else sb("get", [P, TOPK, NT], U32)
        self.expert = sb("expert", [P, NCH1], I32) if first else None


def logits_stage(net, rt):
    nc, R, w = net.nc, net.R, net.w
    with ExitStack() as ctx:
        sb, ps, sem = opener(net, ctx, "g1" if rt.first else "g2")
        xn, xT = sb("xn", [P, 2, D]), sb("xT", [P, 2, P])
        pX, pL = ps("pX", [P, 512]), ps("pL", [P, 512])
        s_xt, s_xts, s_l, s_ls, s_r = [sem(n) for n in ("xt", "xt_out", "logits", "logits_out", "kept")]
        ln = LayerNorm(net, sb, sem, xn, s_xt)
        block = ctx.enter_context(nc.Block())

        @block.sync
        def _(sp):
            clear_stale(net, sp)

        @block.gpsimd
        def _(pool):
            ln.setup(pool)
            pipeline(pool, NT, [(1, lambda u, p: ln.pool_rstd(pool, u, p))])

        @block.vector
        def _(dve):
            def keep(u, p):
                done(dve, ln.s_xn, u)
                nc.vector.tensor_copy(R[:, u, :], xn[:, p, :]).then_inc(s_r, 1)

            def apply(u, p):
                free(dve, s_r, u)
                ln.vector_apply(dve, u, p)

            def take_logits(u, p):
                done(dve, s_l, u)
                if rt.first:
                    i = nc.vector.tensor_copy(rt.logits[:, u, :], pL[:, 0:E])
                else:
                    i = nc.vector.tensor_tensor(rt.logits[:, u, :], pL[:, 0:E], w("f2_br"), ALU.add)
                i.then_inc(s_ls, 1)

            pipeline(dve, NT, [(2, apply), (0, lambda u, p: ln.vector_stats(dve, u, p)),
                               (1, lambda u, p: ln.vector_moments(dve, u, p)), (3, keep),
                               (4, take_logits)])

        @block.scalar
        def _(act):
            def take_xt(u, p):
                done(act, s_xt, u)
                free(act, s_l, u)
                nc.scalar.activation(xT[:, p, :], pX[:, 0:P], ACT.Copy).then_inc(s_xts, 1)
            pipeline(act, NT, [(2, take_xt)])

        @block.tensor
        def _(pe):
            def transpose_x(u, p):
                done(pe, ln.s_xn, u)
                free(pe, s_xts, u, bufs=1)
                nc.tensor.transpose(pX[:, 0:P], xn[:, p, :], w("ident")).then_inc(s_xt, 1)

            def gate(u, p):
                done(pe, s_xts, u)
                free(pe, s_ls, u, bufs=1)
                nc.tensor.matmul(pL[:, 0:E], xT[:, p, :], w("f1_gate" if rt.first else "f2_wr"),
                                 start=True, stop=True).then_inc(s_l, 1)

            pipeline(pe, NT, [(2, transpose_x), (3, gate)])


def route_stage(net, rt):
    nc, R, Y, w = net.nc, net.R, net.Y, net.w
    first = rt.first
    xg = net.dram["slots_in"]
    NE = NT * E
    with ExitStack() as ctx:
        sb, ps, sem = opener(net, ctx, "t1" if first else "t2")
        L = rt.logits
        m = [sb(f"m{k}", [P, NT, 1]) for k in range(2)]
        pos, pm = sb("pos", [P, NT, E]), sb("pm", [P, NT, 1])
        sel = [sb(f"sel{k}", [P, NT, E]) for k in range(2)]
        both = sb("both", [P, NT, E])
        less = sb("less", [P, NT, E])
        scan = [sb(f"scan{k}", [P, NT, E]) for k in range(2)]
        tot = sb("tot", [P, NT, E])
        rank = sb("rank", [P, NT, E])
        keep = sb("keep", [P, NT, E])
        t3 = sb("t3", [P, NT, E])
        ex = sb("ex", [P, NT, E])
        den = sb("den", [P, NT, 1])
        inv = sb("inv", [P, NT, 1])
        gap = sb("gap", [P, NT, 1])
        egap = sb("egap", [P, NT, 1])
        slotf = sb("slotf", [P, TOPK, NT, 1])
        keptf = sb("keptf", [P, TOPK, NT, 1])
        dumpf = sb("dumpf", [P, TOPK, NT, 1])
        ends = [sb(f"ends{k}", [P, 1, E]) for k in range(2)]
        padded = sb("padded", [P, 1, E])
        base = sb("base", [P, 1, E])
        passed = sb("passed", [P, NCH1, E])
        expf = sb("expf", [P, NCH1, 1])
        pP, pT = ps("pP", [P, 512]), ps("pT", [P, 512])
        s_v = sem("vector")
        s_sel, s_cnt, s_arg, s_exp, s_idx, s_rows = [sem(n) for n in (
            "selected", "counted", "exp_args", "exps", "indices", "rows")]
        s_put = rt.s_put
        block = ctx.enter_context(nc.Block())

        @block.sync
        def _(sp):
            clear_stale(net, sp)
        wide = [P, NT, E]

        @block.vector
        def _(dve):
            count = [0]

            def then(i):
                i.then_inc(s_v, 1)
                count[0] += 1
                dve.wait_ge(s_v, count[0])

            v = nc.vector
            ranks8 = w("rank8").unsqueeze(1).broadcast_to(wide)
            src = L
            for k in range(2):
                then(v.tensor_reduce(m[k][:, :, 0], src[:, :, :], AX, ALU.max))
                then(v.tensor_tensor(pos[:, :, :], src[:, :, :], m[k][:, :, :].broadcast_to(wide), ALU.is_equal))
                then(v.tensor_tensor(pos[:, :, :], pos[:, :, :], ranks8, ALU.mult))
                then(v.tensor_reduce(pm[:, :, 0], pos[:, :, :], AX, ALU.max))
                then(v.tensor_tensor(sel[k][:, :, :], pos[:, :, :], pm[:, :, :].broadcast_to(wide), ALU.is_equal))
                if k == 0:
                    then(v.scalar_tensor_tensor(less[:, :, :], sel[0][:, :, :], -3e38, L[:, :, :],
                                                ALU.mult, ALU.add))
                    src = less
            v.tensor_tensor(both[:, :, :], sel[0][:, :, :], sel[1][:, :, :], ALU.add).then_inc(s_sel, 1)
            if first:
                then(v.tensor_tensor(ex[:, :, :], L[:, :, :], m[0][:, :, :].broadcast_to(wide), ALU.subtract))
            v.tensor_tensor(gap[:, :, :], m[1][:, :, :], m[0][:, :, :], ALU.subtract).then_inc(s_arg, 1)

            dve.wait_ge(s_cnt, 1)
            then(v.tensor_copy(tot[:, :, :], pT[:, 0:NE].rearrange("p (n e) -> p n e", e=E)))
            a = tot
            for n, d in enumerate((1, 2, 4, 8, 16)):
                b = scan[n % 2]
                v.tensor_copy(b[:, 0:d], a[:, 0:d])
                then(v.tensor_tensor(b[:, d:], a[:, d:], a[:, 0:NT - d], ALU.add))
                a = b
            then(v.tensor_tensor(t3[:, :, :], a[:, :, :], tot[:, :, :], ALU.subtract))
            then(v.tensor_tensor(rank[:, :, :], pP[:, 0:NE].rearrange("p (n e) -> p n e", e=E), t3[:, :, :],
                                 ALU.add))
            if first:
                counts = a[:, NT - 1:NT, :]
                then(v.tensor_scalar(padded[:, :, :], counts, 1.0 / CHUNK,
                                     (CHUNK - 1.0) / CHUNK - 0.5 + 0.5 / CHUNK, ALU.mult, ALU.add))
                then(v.tensor_scalar(padded[:, :, :], padded[:, :, :], 8388608.0, -8388608.0, ALU.add, ALU.add))
                then(v.tensor_scalar(padded[:, :, :], padded[:, :, :], float(CHUNK), None, ALU.mult))
                a = padded
                for n, d in enumerate((1, 2, 4)):
                    b = ends[n % 2]
                    v.tensor_copy(b[:, :, 0:d], a[:, :, 0:d])
                    then(v.tensor_tensor(b[:, :, d:], a[:, :, d:], a[:, :, 0:E - d], ALU.add))
                    a = b
                then(v.tensor_tensor(base[:, :, :], a[:, :, :], padded[:, :, :], ALU.subtract))
                then(v.tensor_tensor(passed[:, :, :], w("chunk0").unsqueeze(2).broadcast_to([P, NCH1, E]),
                                     a[:, :, :].broadcast_to([P, NCH1, E]), ALU.is_ge))
                then(v.tensor_reduce(expf[:, :, 0], passed[:, :, :], AX, ALU.add))
                then(v.tensor_scalar(rt.expert[:, :], expf[:, :, 0], float(E - 1), None, ALU.min))
                then(v.tensor_tensor(rank[:, :, :], rank[:, :, :], base[:, :, :].broadcast_to(wide), ALU.add))
            else:
                then(v.tensor_scalar(keep[:, :, :], rank[:, :, :], float(CAP), None, ALU.is_lt))
                then(v.tensor_scalar(base[:, 0, :], w("iota8"), float(CAP), None, ALU.mult))
                then(v.tensor_tensor(rank[:, :, :], rank[:, :, :], base[:, :, :].broadcast_to(wide), ALU.add))
            for k in range(2):
                then(v.tensor_tensor(t3[:, :, :], sel[k][:, :, :], rank[:, :, :], ALU.mult))
                then(v.tensor_reduce(slotf[:, k, :, 0], t3[:, :, :], AX, ALU.add))
                if not first:
                    then(v.tensor_tensor(t3[:, :, :], sel[k][:, :, :], keep[:, :, :], ALU.mult))
                    then(v.tensor_reduce(keptf[:, k, :, 0], t3[:, :, :], AX, ALU.add))
            if not first:
                then(v.tensor_tensor(slotf[:, :, :, :], slotf[:, :, :, :], keptf[:, :, :, :], ALU.mult))
                then(v.tensor_copy(rt.get[:, :, :], slotf[:, :, :, 0]))
                then(v.tensor_scalar(dumpf[:, :, :, :], keptf[:, :, :, :], -1.0, 1.0, ALU.mult, ALU.add))
                spare = w("spare").rearrange("p (k n) -> p k n", k=TOPK).unsqueeze(3)
                then(v.tensor_tensor(dumpf[:, :, :, :], dumpf[:, :, :, :], spare, ALU.mult))
                then(v.tensor_tensor(slotf[:, :, :, :], slotf[:, :, :, :], dumpf[:, :, :, :], ALU.add))
            v.tensor_copy(rt.put[:, :, :], slotf[:, :, :, 0]).then_inc(s_idx, 1)

            dve.wait_ge(s_exp, 1)
            if first:
                then(v.tensor_reduce(den[:, :, 0], ex[:, :, :], AX, ALU.add))
            else:
                then(v.tensor_scalar(den[:, :, :], egap[:, :, :], 1.0, None, ALU.add))
            then(v.reciprocal(inv[:, :, :], den[:, :, :]))
            wt = rt.weight
            v.tensor_copy(wt[:, 0, :], inv[:, :, 0])
            then(v.tensor_tensor(wt[:, 1, :], egap[:, :, 0], inv[:, :, 0], ALU.mult))
            if first:
                then(v.tensor_tensor(Y[:, :, :], R[:, :, :], wt[:, 0, :].unsqueeze(2).broadcast_to([P, NT, D]),
                                     ALU.mult))
                v.tensor_tensor(R[:, :, :], R[:, :, :], wt[:, 1, :].unsqueeze(2).broadcast_to([P, NT, D]),
                                ALU.mult).then_inc(s_rows, 1)
            else:
                v.tensor_tensor(wt[:, :, :], wt[:, :, :], keptf[:, :, :, 0], ALU.mult).then_inc(s_rows, 1)

        @block.scalar
        def _(act):
            act.wait_ge(s_arg, 1)
            if first:
                nc.scalar.activation(ex[:, :, :], ex[:, :, :], ACT.Exp)
            nc.scalar.activation(egap[:, :, :], gap[:, :, :], ACT.Exp).then_inc(s_exp, 1)

        @block.tensor
        def _(pe):
            pe.wait_ge(s_sel, 1)
            flat = both[:, :, :].rearrange("p n e -> p (n e)")
            nc.tensor.matmul(pP[:, 0:NE], w("tri"), flat, start=True, stop=True)
            nc.tensor.matmul(pT[:, 0:NE], w("ones"), flat, start=True, stop=True).then_inc(s_cnt, 1)

        @block.gpsimd
        def _(pool):
            pool.wait_ge(s_idx, 1)
            pool.wait_ge(s_rows, 1)
            for n in range(NT):
                for k in range(TOPK):
                    rows = (Y if k == 0 else R) if first else R
                    nc.gpsimd.indirect_dma_start(
                        xg[:, :], bass.IndirectOffsetOnAxis(ap=rt.put[:, k, n:n + 1], axis=0),
                        rows[:, n, :], None).then_inc(s_put, 16)
            pool.wait_ge(s_put, 16 * TOPK * NT)


def experts_stage(net, rt):
    nc, w = net.nc, net.w
    first = rt.first
    n = NCH1 if first else NCH2
    HC = (HID1P if first else HID2) // P
    UP = 2 * HID1P if first else HID2
    WB = UP + HC * D + (0 if first else HC + D)
    banks = HC if first else HC // 2
    xg, yg = net.dram["slots_in"], net.dram["slots_out"]
    weights = net.dram["f1" if first else "f2"]
    NSL = CHUNK // P
    with ExitStack() as ctx:
        sb, ps, sem = opener(net, ctx, "e1" if first else "e2")
        wt = sb("w", [P, 2, WB])
        rows = sb("rows", [P, 2, NSL, D])
        xT = sb("xT", [P, 2, CHUNK])
        act_out = sb("silu", [P, 2, HC, CHUNK]) if first else None
        h = sb("h", [P, 2, HC, CHUNK])
        y = sb("y", [P, 2, NSL, D])
        H = ps("H", [P, 2 * banks, 512])
        pX, pY = ps("pX", [P, 512]), ps("pY", [P, 512])
        s_w, s_r = [sem("w_even"), sem("w_odd")], [sem("rows_even"), sem("rows_odd")]
        s_out = [sem("out_even"), sem("out_odd")]
        s_xt, s_xts, s_h, s_a, s_hs, s_y, s_ys = [sem(m) for m in (
            "xt", "xt_out", "hidden", "silu", "hidden_out", "y", "y_out")]
        block = ctx.enter_context(nc.Block())

        @block.sync
        def _(sp):
            clear_stale(net, sp)
            def chunk_rows(t, u):
                r = t[0:n * CHUNK, :].rearrange("(c s p) d -> c p s d", s=NSL, p=P)
                return r[u]

            def load_rows(u, p):
                free(sp, s_xt, u)
                sp.dma_start(rows[:, p], chunk_rows(xg, u)).then_inc(s_r[p], 16)

            def load_weights(u, p):
                if first:
                    col = rt.expert[0:1, u:u + 1] if isinstance(u, int) else rt.expert[0:1, bass.ds(u, 1)]
                    e = sp.value_load(col, min_val=0, max_val=E - 1)
                    src = weights[bass.ds(e, 1)].rearrange("a p n -> p (a n)")
                else:
                    src = weights[bass.ds(u // (CAP // CHUNK), 1)].rearrange("a p n -> p (a n)")
                free(sp, s_y if first else s_ys, u)
                sp.dma_start(wt[:, p, :], src).then_inc(s_w[p], 16)

            def store(u, p):
                done(sp, s_ys, u)
                sp.dma_start(chunk_rows(yg, u), y[:, p]).then_inc(s_out[p], 16)

            pipeline(sp, n, [(0, load_rows), (1, load_weights), (4, store)])
            for p in range(2):
                sp.wait_ge(s_out[p], 16 * (n // 2))

        @block.vector
        def _(dve):
            def take_xt(u, p):
                done(dve, s_xt, u)
                free(dve, s_h, u, per=banks)
                nc.vector.tensor_copy(xT[:, p, :], pX[:, 0:CHUNK]).then_inc(s_xts, 1)

            def gate(u, p):
                for b in range(banks):
                    dve.wait_ge(s_a, banks * u + (b + 1))
                    if b == 0:
                        free(dve, s_y, u)
                    nc.vector.tensor_tensor(h[:, p, b, :], act_out[:, p, b, :],
                                            H[:, banks * p + b, CHUNK:2 * CHUNK], ALU.mult
                                            ).then_inc(s_hs, 1)

            def take_y(u, p):
                done(dve, s_y, u)
                if not first:
                    landed(dve, s_w, u, p)
                stored = s_out[p]
                if not (isinstance(u, int) and u < 2):
                    dve.wait_ge(stored, 8 * u - 8 * p)
                src = pY[:, 0:NSL * D].rearrange("p (s d) -> p s d", d=D)
                if first:
                    i = nc.vector.tensor_copy(y[:, p], src)
                else:
                    b2 = wt[:, p, WB - D:WB].unsqueeze(1).broadcast_to([P, NSL, D])
                    i = nc.vector.tensor_tensor(y[:, p], src, b2, ALU.add)
                i.then_inc(s_ys, 1)

            pipeline(dve, n, [(1, take_xt)] + ([(2, gate)] if first else []) + [(3, take_y)])

        @block.scalar
        def _(act):
            def silu(u, p):
                for b in range(banks):
                    act.wait_ge(s_h, banks * u + (b + 1))
                    if b == 0:
                        free(act, s_hs, u, per=banks)
                    nc.scalar.activation(act_out[:, p, b, :], H[:, banks * p + b, 0:CHUNK], ACT.Silu
                                         ).then_inc(s_a, 1)

            def gelu(u, p):
                landed(act, s_w, u, p)
                for b in range(banks):
                    act.wait_ge(s_h, banks * u + (b + 1))
                    if b == 0:
                        free(act, s_y, u)
                    for c in range(2):
                        hc = 2 * b + c
                        i = nc.scalar.activation(h[:, p, hc, :], H[:, banks * p + b, CHUNK * c:CHUNK * (c + 1)],
                                                 ACT.Gelu, bias=wt[:, p, UP + HC * D + hc:UP + HC * D + hc + 1])
                    i.then_inc(s_hs, 1)

            pipeline(act, n, [(2, silu if first else gelu)])

        @block.tensor
        def _(pe):
            def transpose_x(u, p):
                landed(pe, s_r, u, p)
                free(pe, s_xts, u, bufs=1)
                for s in range(NSL):
                    i = nc.tensor.transpose(pX[:, P * s:P * s + P], rows[:, p, s, :], w("ident"))
                i.then_inc(s_xt, 1)

            def hidden(u, p):
                done(pe, s_xts, u)
                landed(pe, s_w, u, p)
                free(pe, s_hs, u, per=banks)
                for b in range(banks):
                    for c in range(2):
                        at = HID1P * c + P * b if first else P * (2 * b + c)
                        i = nc.tensor.matmul(H[:, banks * p + b, CHUNK * c:CHUNK * (c + 1)],
                                             wt[:, p, at:at + P], xT[:, p, :], start=True, stop=True)
                    i.then_inc(s_h, 1)

            def output(u, p):
                done(pe, s_hs, u, per=banks)
                free(pe, s_ys, u, bufs=1)
                for s in range(NSL):
                    for c in range(HC):
                        i = nc.tensor.matmul(pY[:, D * s:D * s + D], h[:, p, c, P * s:P * s + P],
                                             wt[:, p, UP + D * c:UP + D * (c + 1)],
                                             start=(c == 0), stop=(c == HC - 1))
                i.then_inc(s_y, 1)

            pipeline(pe, n, [(3, output), (1, transpose_x), (2, hidden)])


def combine_stage(net, rt):
    nc, X, Y, R = net.nc, net.X, net.Y, net.R
    yg = net.dram["slots_out"][0:(NCH1 if rt.first else NCH2) * CHUNK]
    PARTS = GATHER_PARTS
    n = NT // PARTS
    with ExitStack() as ctx:
        sb, ps, sem = opener(net, ctx, "x1" if rt.first else "x2")
        s_got = rt.s_got
        s_m, s_x = sem("weighted"), sem("x")
        block = ctx.enter_context(nc.Block())

        @block.sync
        def _(sp):
            clear_stale(net, sp)

        @block.gpsimd
        def _(pool):
            for t in range(NT):
                for k, rows in enumerate((Y, R)):
                    nc.gpsimd.indirect_dma_start(
                        rows[:, t, :], None, yg[:, :],
                        bass.IndirectOffsetOnAxis(ap=rt.get[:, k, t:t + 1], axis=0)
                    ).then_inc(s_got[t // n], 16)

        @block.vector
        def _(dve):
            v = nc.vector
            for k in range(PARTS):
                dve.wait_ge(s_got[k], 16 * TOPK * n)
                part = [t[:, n * k:n * k + n, :] for t in (X, Y, R)]
                x, y, r = part
                if not rt.first:
                    for c, t in enumerate((y, r)):
                        wt = rt.weight[:, c, n * k:n * k + n].unsqueeze(2).broadcast_to([P, n, D])
                        v.tensor_tensor(t, t, wt, ALU.mult).then_inc(s_m, 1)
                    dve.wait_ge(s_m, 2 * k + 2)
                v.tensor_tensor(x, x, y, ALU.add).then_inc(s_x, 1)
                dve.wait_ge(s_x, 2 * k + 1)
                v.tensor_tensor(x, x, r, ALU.add).then_inc(s_x, 1)


def mixture(net, first):
    with ExitStack() as ctx:
        rt = Routing(ctx, net, first)
        logits_stage(net, rt)
        route_stage(net, rt)
        experts_stage(net, rt)
        combine_stage(net, rt)


def store_stage(net):
    nc = net.nc
    with ExitStack() as ctx:
        _, _, sem = opener(net, ctx, "out")
        s_out = sem("stored")
        block = ctx.enter_context(nc.Block())

        @block.sync
        def _(sp):
            clear_stale(net, sp)
            sp.dma_start(net.dram["out"].rearrange("(i b) t d -> (b t) i d", b=2), net.X[:, :, :]
                         ).then_inc(s_out, 16)
            sp.wait_ge(s_out, 16)


def feed_forward0(net):
    heads16_stage(net, cross=False)
    norm_gelu_stage(net)


def attention1(net):
    heads16_stage(net, cross=True)


def feed_forward1(net):
    mixture(net, first=True)


def feed_forward2(net):
    mixture(net, first=False)


def attention3(net):
    attention3_stage(net, cross=False)
    attention3_stage(net, cross=True)
    mlp3_stage(net)


LAYERS = (attention0_stage, feed_forward0, attention1, feed_forward1, attention2_stage, feed_forward2,
          attention3, shift3_stage)


def build(nc, dram):
    with ExitStack() as ctx:
        W = ctx.enter_context(nc.sbuf_tensor("W", [P, PACKW], F32))
        X = ctx.enter_context(nc.sbuf_tensor("X", [P, NT, D], F32))
        net = Net(nc, dram, W, X)
        net.software_sems = [ctx.enter_context(nc.semaphore(f"software_dma{k}"))
                             for k in range(2 * (1 + GATHER_PARTS))]
        net.Y = ctx.enter_context(nc.sbuf_tensor("Y", [P, NT, D], F32))
        net.R = ctx.enter_context(nc.sbuf_tensor("R", [P, NT, D], F32))
        net.norms = ctx.enter_context(nc.sbuf_tensor("norms", [P, 2, NT], F32))
        load_stage(net)
        for layer in LAYERS:
            layer(net)
        store_stage(net)


def constants():
    p = np.arange(P)
    one = np.float32
    c = {"ident": np.eye(P, dtype=one), "ones": np.ones((P, P), one)}
    c["maskA"] = (p[:, None] // 8 == np.arange(16)).astype(one)
    c["maskB"] = ((p[:, None] % 64) // 8 == np.arange(8)).astype(one)
    d = p % 8
    theta = (one(1.0) / one(1250) ** (np.arange(0, 4, 2, dtype=one) / one(4))).astype(one)
    ang = np.arange(D, dtype=one)[None, :] * theta[d % 2][:, None]
    rotates = (d < 4)[:, None]
    c["cos"] = np.where(rotates, np.cos(ang), 1).astype(one)
    c["sin"] = np.where(rotates, np.where((d < 2)[:, None], -np.sin(ang), np.sin(ang)), 0).astype(one)
    c["tri"] = (p[:, None] < p[None, :]).astype(one)
    c["sel0"] = (p[:, None] == 64 * (p[None, :] // 64)).astype(one)
    k = np.arange(64)
    c["iota64"] = np.broadcast_to(k, (P, 64)).astype(one)
    q = (p % 64)[:, None]
    c["causal"] = np.where(k[None, :] > q, one(NEG), one(0)).astype(one)
    c["allow1"] = np.where(k[None, :] // 4 <= q, one(0), one(NEG)).astype(one)
    c["rank8"] = np.broadcast_to(8 - np.arange(8), (P, 8)).astype(one)
    c["iota8"] = np.broadcast_to(np.arange(8), (P, 8)).astype(one)
    c["chunk0"] = np.broadcast_to(np.arange(NCH1) * CHUNK, (P, NCH1)).astype(one)
    n = np.arange(TOPK * NT)
    c["spare"] = (NTOK * TOPK + P * n[None, :] + p[:, None]).astype(one)
    return c


def lay_out(inp):
    c = constants()

    def bd(w):
        z = np.zeros((P, P), np.float32)
        z[:64, :64] = w
        z[64:, 64:] = w
        return z

    def rows(v):
        return np.broadcast_to(v[None, :], (P, v.size))

    def col(v):
        return v.reshape(-1, 1)

    turn = np.arange(64).reshape(8, 8)[:, [2, 3, 0, 1, 4, 5, 6, 7]].reshape(-1)
    g = {k: np.asarray(v) for k, v in inp.items()}
    wq, wk = g["L0_xattn_Wq"], g["L0_xattn_Wk"]
    c["a0_wq"], c["a0_wqr"] = bd(wq.T), bd(wq[turn].T)
    c["a0_wk"], c["a0_wkr"] = bd(wk.T), bd(wk[turn].T)
    c["a0_wv"], c["a0_wo"] = bd(g["L0_xattn_Wv"].T), bd(g["L0_xattn_Wo"].T)
    b = [g["L0_xattn_bq"], g["L0_xattn_bq"][turn], g["L0_xattn_bk"], g["L0_xattn_bk"][turn],
         g["L0_xattn_bv"], g["L0_xattn_bo"]]
    c["a0_bias"] = np.stack([np.concatenate([v, v]) for v in b], 1)
    c["f0_wq"], c["f0_wk"], c["f0_wv"] = g["L0_ffn_Wq"], g["L0_ffn_Wk"], g["L0_ffn_Wv"]
    c["f0_woT"], c["f0_wo"], c["f0_wff"] = g["L0_ffn_Wo"].T, g["L0_ffn_Wo"], g["L0_ffn_Wff"]
    for n, m in (("a1_wq", "Wq"), ("a1_wk", "Wk"), ("a1_wv", "Wv"), ("a1_wo", "Wo")):
        c[n] = g["L1_xattn_" + m].T
    for n, m in (("a1_bq", "bq"), ("a1_bk", "bk")):
        v = g["L1_xattn_" + m].reshape(2, 64).T
        c[n] = np.concatenate([v, v], 0)
    c["a1_bv"], c["a1_bo"] = col(g["L1_xattn_bv"]), rows(g["L1_xattn_bo"])
    c["f1_gate"] = g["L1_ffn_gate_w"].T
    c["a2_wq"], c["a2_wk"], c["a2_wv"] = g["L2_xattn_Wq"], g["L2_xattn_Wk"], g["L2_xattn_Wv"]
    c["a2_wo"] = g["L2_xattn_Wo"].reshape(4, P, D).transpose(1, 0, 2).reshape(P, 512)
    c["a2_bo"] = rows(g["L2_xattn_bo"])
    c["f2_wr"], c["f2_br"] = g["L2_ffn_Wr"], rows(g["L2_ffn_br"])
    for m in ("Wq1", "Wk1", "Wv1", "Wq2", "Wk2", "Wv2"):
        c["a3_" + m.lower()] = g["L3_xattn_" + m]
    c["a3_fc1"], c["a3_fc2"] = g["L3_xattn_fc1_w"], g["L3_xattn_fc2_w"]
    c["a3_b1"], c["a3_b2"] = col(g["L3_xattn_fc1_b"]), rows(g["L3_xattn_fc2_b"])
    for i in "123":
        c["a3_g" + i], c["a3_c" + i] = rows(g[f"L3_xattn_ln{i}_g"]), rows(g[f"L3_xattn_ln{i}_b"])
    c["f3_wr"], c["f3_wk"], c["f3_wv"] = g["L3_ffn_W_r"].T, g["L3_ffn_W_k"].T, g["L3_ffn_W_v"].T
    c["f3_mr"], c["f3_mk"] = col(g["L3_ffn_mu_r"]), col(g["L3_ffn_mu_k"])
    wpack = np.ascontiguousarray(np.concatenate([c[n] for n, _ in PACK], 1))
    assert wpack.shape == (P, PACKW), wpack.shape

    ctx = np.ascontiguousarray(g["ctx_1024"])
    f1w = np.zeros((E, P, 2, HID1P), np.float32)
    f1w[:, :, 0, :HID1], f1w[:, :, 1, :HID1] = g["L1_ffn_w1"], g["L1_ffn_w3"]
    f1d = np.zeros((E, HID1P, D), np.float32)
    f1d[:, :HID1] = g["L1_ffn_w2"]
    f1d = f1d.reshape(E, HID1P // P, P, D).transpose(0, 2, 1, 3)
    f2d = g["L2_ffn_W2"].reshape(E, HID2 // P, P, D).transpose(0, 2, 1, 3)
    f1 = np.concatenate([f1w.reshape(E, P, -1), f1d.reshape(E, P, -1)], 2)
    b1 = g["L2_ffn_b1"].reshape(E, HID2 // P, P).transpose(0, 2, 1)
    b2 = np.broadcast_to(g["L2_ffn_b2"][:, None, :], (E, P, D))
    f2 = np.concatenate([g["L2_ffn_W1"], f2d.reshape(E, P, -1), b1, b2], 2)
    return {
        "x": np.ascontiguousarray(g["x"]), "ctx": ctx, "wpack": wpack,
        "ctxT": np.ascontiguousarray(ctx.reshape(NT, P, D).transpose(0, 2, 1)),
        "f1": np.ascontiguousarray(f1), "f2": np.ascontiguousarray(f2),
    }


def kernel(**inputs):
    import concourse.bacc as bacc
    from concourse.bass_utils import run_bass_kernel_spmd

    nc = bacc.Bacc("TRN2", target_bir_lowering=False, num_devices=1)
    arrays = {f"in_{n}_dram": a for n, a in lay_out(inputs).items()}
    dram = {n[3:-5]: nc.dram_tensor(n, a.shape, mybir.dt.from_np(a.dtype), kind="ExternalInput").ap()
            for n, a in arrays.items()}
    dram["out"] = nc.dram_tensor("out_0_dram", (B, T, D), F32, kind="ExternalOutput").ap()
    dram["slots_in"] = nc.dram_tensor("slots_in", (2 * NTOK * TOPK, D), F32).ap()
    dram["slots_out"] = nc.dram_tensor("slots_out", (NCH1 * CHUNK, D), F32).ap()
    build(nc, dram)
    r = run_bass_kernel_spmd(nc, [arrays], core_ids=[0])
    return r.results[0]["out_0_dram"]
```

```python
from contextlib import ExitStack

import numpy as np
import concourse.bass as bass
from concourse import mybir

F32 = mybir.dt.float32
BF16 = mybir.dt.bfloat16
U32 = mybir.dt.uint32
I32 = mybir.dt.int32
ALU = mybir.AluOpType
ACT = mybir.ActivationFunctionType
AX = mybir.AxisListType.X

P = 128
B, T, D = 64, 64, 128
NT = B // 2
NTOK = B * T
E = 8
TOPK = 2
LN_EPS = 1e-5
L2_EPS = 1e-12
NEG = -1e30
CHUNK = 256
CAP = NTOK * TOPK // E
HID1, HID1P = 352, 384
HID2 = 512
NCH1 = (NTOK * TOPK + E * (CHUNK - 1)) // CHUNK
NCH1 += NCH1 % 2
NCH2 = E * CAP // CHUNK
FILL_P = 64
FILL_ROWS = NCH1 * CHUNK // (NT * FILL_P)


def pipeline(eng, n, steps, straight=False):
    lags = [lag for lag, _ in steps]
    head = max(lags) + 2
    head += head % 2
    if straight or head >= n:
        head = n

    def static(t):
        for lag, fn in steps:
            if 0 <= t - lag < n:
                fn(t - lag, (t - lag) % 2)

    for t in range(head):
        static(t)
    if head < n:
        with eng.Fori(head // 2, n // 2) as i:
            for p in range(2):
                for lag, fn in steps:
                    fn(2 * i + (p - lag), (p - lag) % 2)
    for t in range(n, n + max(lags)):
        static(t)


def done(eng, sem, u, per=1):
    eng.wait_ge(sem, per * u + per)


def free(eng, sem, u, bufs=2, per=1):
    if isinstance(u, int) and u < bufs:
        return
    eng.wait_ge(sem, per * u + (per - per * bufs))


def landed(eng, sems, u, p):
    eng.wait_ge(sems[p], 8 * u + (16 - 8 * p))


def pack_layout():
    cols = {}
    at = 0
    for name, n in PACK:
        cols[name] = (at, n)
        at += n
    return cols, at


PACK = [
    ("ident", 128), ("maskA", 16), ("maskB", 8), ("cos", 128), ("sin", 128),
    ("a0_wq", 128), ("a0_wqr", 128), ("a0_wk", 128), ("a0_wkr", 128), ("a0_wv", 128), ("a0_wo", 128),
    ("a0_bias", 6),
    ("ones", 128), ("tri", 128), ("sel0", 128), ("iota64", 64), ("causal", 64), ("allow1", 64),
    ("rank8", 8), ("iota8", 8), ("chunk0", NCH1), ("spare", TOPK * NT),
    ("f0_wq", 128), ("f0_wk", 128), ("f0_wv", 128), ("f0_woT2", 256), ("f0_wo2", 256), ("f0_wff", 128),
    ("a1_wq", 128), ("a1_wk", 128), ("a1_wv", 128), ("a1_wo", 128), ("a1_bq", 2), ("a1_bk", 2),
    ("a1_bv", 1), ("a1_bo", 128),
    ("f1_gate", 8),
    ("a2_wq", 512), ("a2_wk", 512), ("a2_wv", 512), ("a2_wo", 512), ("a2_bo", 128),
    ("f2_wr", 8), ("f2_br", 8),
    ("a3_wq1", 128), ("a3_wk1", 128), ("a3_wv1", 128), ("a3_wq2", 128), ("a3_wk2", 128),
    ("a3_wv2", 128), ("a3_fc1", 128), ("a3_fc2", 128), ("a3_b1", 1), ("a3_b2", 128),
    ("a3_g1", 128), ("a3_c1", 128), ("a3_g2", 128), ("a3_c2", 128), ("a3_g3", 128), ("a3_c3", 128),
    ("f3_wr", 128), ("f3_wk", 128), ("f3_wv", 128), ("f3_mr", 1), ("f3_mk", 1),
]
COLS, PACKW = pack_layout()
FIRST = COLS["ones"][0]
IN_FLIGHT = 4
HEADS = 16
GH = 8


class Net:

    def __init__(self, nc, dram, W, X):
        self.nc, self.dram, self.W, self.X = nc, dram, W, X
        self.stale, self.current = [], []

    def w(self, name, lo=0, hi=None):
        at, n = COLS[name]
        return self.W[:, at + lo:at + (n if hi is None else hi)]


def opener(net, ctx, stage):
    nc = net.nc
    net.stale, net.current = net.current, []

    def sb(name, shape, dt=F32):
        return ctx.enter_context(nc.sbuf_tensor(f"{stage}_{name}", shape, dt))

    def ps(name, shape, dt=F32):
        return ctx.enter_context(nc.psum_tensor(f"{stage}_{name}", shape, dt))

    def sem(name):
        net.current.append(ctx.enter_context(nc.semaphore(f"{stage}_{name}")))
        return net.current[-1]

    return sb, ps, sem


def clear_stale(net, sp):
    for sem in net.stale:
        sp.sem_clear(sem)


class Bank:

    def __init__(self, n, uses):
        self.n, self.uses, self.order = n, uses, list(uses)

    def take(self, pe, name, u):
        at = self.order.index(name)
        lag = self.uses[name][0]
        before = [(m, u + lag - self.uses[m][0] - (k >= at)) for k, m in enumerate(self.order)]
        if isinstance(u, int):
            for m, v in before:
                v = min(v, self.n - 1)
                if v >= 0:
                    self.reader_done(pe, m, v)
        else:
            self.reader_done(pe, *before[at - 1])

    def reader_done(self, pe, m, u):
        _, sem, per, nth = self.uses[m]
        pe.wait_ge(sem, per * u + nth)


class LayerNorm:

    def __init__(self, net, sb, sem, xn, xn_used, ready=None):
        self.net, self.xn, self.xn_used = net, xn, xn_used
        self.ready = ready
        self.stats = sb("ln_stats", [P, 2, 6])
        self.moments = sb("ln_moments", [P, 2, 2])
        self.rstd = sb("ln_rstd", [P, 2, 2])
        self.half = sb("ln_half", [P, 2])
        self.s_half = sem("ln_half")
        self.s_stats = sem("ln_stats")
        self.s_moments = sem("ln_moments")
        self.s_vareps = sem("ln_vareps")
        self.s_rstd = sem("ln_rstd")
        self.s_xn = sem("xn")

    def setup(self, pool):
        self.net.nc.gpsimd.memset(self.half[:, 0:1], -0.5).then_inc(self.s_half, 1)
        self.net.nc.gpsimd.memset(self.half[:, 1:2], LN_EPS).then_inc(self.s_half, 1)
        pool.wait_ge(self.s_half, 2)

    def vector_stats(self, dve, u, p):
        nc = self.net.nc
        if self.ready:
            done(dve, self.ready, u)
        free(dve, self.s_moments, u)
        if not isinstance(u, int):
            self.moments_waits(dve, u - 1)
        nc.vector.bn_stats(self.stats[:, p, :], self.net.X[:, u, :]).then_inc(self.s_stats, 1)

    def moments_waits(self, dve, u):
        done(dve, self.s_stats, u)
        free(dve, self.s_rstd, u)
        free(dve, self.s_xn, u)

    def vector_moments(self, dve, u, p):
        if isinstance(u, int):
            self.moments_waits(dve, u)
        self.net.nc.vector.bn_aggr(self.moments[:, p, :], self.stats[:, p, :]).then_inc(self.s_moments, 1)

    def pool_rstd(self, pool, u, p):
        nc = self.net.nc
        done(pool, self.s_moments, u)
        free(pool, self.s_xn, u)
        nc.gpsimd.tensor_tensor(self.rstd[:, p, 0:1], self.moments[:, p, 1:2], self.half[:, 1:2],
                                ALU.add).then_inc(self.s_vareps, 1)
        done(pool, self.s_vareps, u)
        nc.gpsimd.tensor_tensor(self.rstd[:, p, 1:2], self.rstd[:, p, 0:1], self.half[:, 0:1],
                                ALU.pow).then_inc(self.s_rstd, 1)

    def vector_apply(self, dve, u, p):
        done(dve, self.s_moments, u)
        done(dve, self.s_rstd, u)
        free(dve, self.xn_used, u)
        self.net.nc.vector.tensor_scalar(self.xn[:, p, :], self.net.X[:, u, :], self.moments[:, p, 0:1],
                                         self.rstd[:, p, 1:2], ALU.subtract, ALU.mult
                                         ).then_inc(self.s_xn, 1)


def load_stage(net):
    nc = net.nc
    with ExitStack() as ctx:
        _, _, sem = opener(net, ctx, "load")
        s_first, s_zero = sem("weights"), sem("zero")
        block = ctx.enter_context(nc.Block())

        @block.vector
        def _(dve):
            nc.vector.memset(net.Y[:, 0:FILL_ROWS, :], 0.0).then_inc(s_zero, 1)

        @block.sync
        def _(sp):
            sp.dma_start(net.W[:, 0:FIRST], net.dram["wpack"][:, 0:FIRST]).then_inc(s_first, 16)
            sp.dma_start(net.X[:, :, :], net.dram["x"].rearrange("(i b) t d -> (b t) i d", b=2)
                         ).then_inc(s_first, 16)
            sp.wait_ge(s_zero, 1)
            sp.wait_ge(s_first, 32)


def load_more(net, sp, u):
    if isinstance(u, int) and u == 0:
        sp.dma_start(net.W[:, FIRST:], net.dram["wpack"][:, FIRST:]).then_inc(net.s_rest, 16)
    slots = net.dram["slots_in"][0:NCH1 * CHUNK, :].rearrange("(n p r) d -> n p (r d)", n=NT, p=FILL_P)
    sp.dma_start(slots[u], net.Y[0:FILL_P, 0:FILL_ROWS, :].rearrange("p r d -> p (r d)")
                 ).then_inc(net.s_fill, 16)


def loads_done(net, sp):
    sp.wait_ge(net.s_rest, 16)
    sp.wait_ge(net.s_fill, 16 * NT)


def attention0_stage(net):
    nc, X, w = net.nc, net.X, net.w
    SCALE = 8 ** -0.5
    with ExitStack() as ctx:
        sb, ps, sem = opener(net, ctx, "a0")
        xn = sb("xn", [P, 2, D])
        cK = sb("cK", [P, 2, D])
        cV = sb("cV", [P, 2, D])
        qb = sb("qbias", [P, 2, D])
        rot = sb("rot", [P, 2, 2, 2, D])
        qk = sb("qk", [P, 2, 2, D])
        kM = sb("kM", [P, 2, HEADS, D])
        V = sb("V", [P, 2, HEADS, 9])
        Pr = sb("Pr", [P, 2, HEADS, D])
        PT = sb("PT", [P, 2, HEADS, D])
        mx = sb("mx", [P, 2, HEADS])
        rden = sb("rden", [P, 2, HEADS, 1])
        zn = sb("zn", [P, 2, HEADS, 8])
        zT = sb("zT", [P, 2, D])
        S = ps("S", [P, 2, 1024])
        PTp = ps("PTp", [P, 512])
        pQ = ps("pQ", [P, 4, D])
        pO = ps("pO", [P, 512])
        pY = ps("pY", [P, 512])
        pV, pZ, pW = pY[:, 0:128], pY[:, 256:384], pY[:, 384:512]

        s_cK = [sem("cK_even"), sem("cK_odd")]
        s_cV = [sem("cV_even"), sem("cV_odd")]
        s_ones, s_qb, s_qb2 = sem("ones"), sem("qbias"), sem("qbias2")
        s_proj, s_v, s_vs = sem("proj"), sem("v"), sem("v_out")
        s_cos, s_sin, s_rot, s_qk = sem("cos"), sem("sin"), sem("rot"), sem("qk")
        s_km = sem("kM")
        s_S, s_mx, s_sub, s_exp = sem("scores"), sem("max"), sem("sub"), sem("exp")
        s_pt, s_pts, s_o, s_rd, s_zn = sem("pt"), sem("pt_out"), sem("o"), sem("rden"), sem("zn")
        s_zt, s_zts, s_y, s_x = sem("zt"), sem("zt_out"), sem("y"), sem("x")
        ln = LayerNorm(net, sb, sem, xn, s_proj)
        block = ctx.enter_context(nc.Block())

        @block.sync
        def _(sp):
            clear_stale(net, sp)

            def load_for(tile, sems, reader):
                def fn(u, p):
                    free(sp, reader, u)
                    sp.dma_start(tile[:, p, :], net.dram["ctx"][2 * u:2 * u + 2] if isinstance(u, int)
                                 else net.dram["ctx"][bass.ds(2 * u, 2)]).then_inc(sems[p], 16)
                return fn
            pipeline(sp, NT, [(2, load_for(cK, s_cK, s_proj)), (6, load_for(cV, s_cV, s_v)),
                              (7, lambda u, p: load_more(net, sp, u))])
            loads_done(net, sp)

        @block.gpsimd
        def _(pool):
            ln.setup(pool)
            nc.gpsimd.memset(V[:, :, :, 8:9], 1.0).then_inc(s_ones, 1)

            def add_parts(u, p):
                done(pool, s_sin, u)
                nc.gpsimd.tensor_tensor(rot[:, p, 0], rot[:, p, 0], rot[:, p, 1],
                                        ALU.add).then_inc(s_rot, 1)
                done(pool, s_rot, u)
                free(pool, s_S, u, per=2)
                free(pool, s_km, u)
                nc.gpsimd.tensor_tensor(qk[:, p], rot[:, p, 0], qb[:, :, :], ALU.add).then_inc(s_qk, 1)

            head_mask = w("maskA").unsqueeze(2).broadcast_to([P, HEADS, D])

            def spread_k(u, p):
                done(pool, s_qk, u)
                free(pool, s_S, u, per=2)
                nc.gpsimd.tensor_tensor(kM[:, p], qk[:, p, 1:2, :].broadcast_to([P, HEADS, D]),
                                        head_mask, ALU.mult).then_inc(s_km, 1)

            pool.wait_ge(s_qb2, 2)
            pipeline(pool, NT, [(5, add_parts), (2, lambda u, p: ln.pool_rstd(pool, u, p)),
                                (5, spread_k)])

        @block.vector
        def _(dve):
            bias = w("a0_bias")
            for n in range(2):
                nc.vector.tensor_scalar(qb[:, n, :], w("cos"), bias[:, 2 * n:2 * n + 1], None,
                                        ALU.mult).then_inc(s_qb, 1)
            dve.wait_ge(s_qb, 2)
            for n in range(2):
                nc.vector.scalar_tensor_tensor(qb[:, n, :], w("sin"), bias[:, 2 * n + 1:2 * n + 2],
                                               qb[:, n, :], ALU.mult, ALU.add).then_inc(s_qb2, 1)
            cos2 = w("cos").unsqueeze(1).broadcast_to([P, 2, D])
            sin2 = w("sin").unsqueeze(1).broadcast_to([P, 2, D])

            def rotate(u, p):
                done(dve, s_proj, u)
                free(dve, s_rot, u)
                free(dve, s_qk, u)
                nc.vector.tensor_tensor(rot[:, p, 0], pQ[:, 0:2, :], cos2, ALU.mult).then_inc(s_cos, 1)
                nc.vector.tensor_tensor(rot[:, p, 1], pQ[:, 2:4, :], sin2, ALU.mult).then_inc(s_sin, 1)

            def softmax(half):
                def fn(u, p):
                    hs = slice(GH * half, GH * half + GH)
                    Sh = S[:, half, :].rearrange("p (h k) -> p h k", k=D)
                    dve.wait_ge(s_S, 2 * u + half + 1)
                    nc.vector.tensor_reduce(mx[:, p, hs], Sh, AX, ALU.max).then_inc(s_mx, 1)
                    dve.wait_ge(s_mx, 2 * u + half + 1)
                    free(dve, s_pt, u, per=4)
                    nc.vector.tensor_tensor(Pr[:, p, hs], Sh,
                                            mx[:, p, hs].unsqueeze(2).broadcast_to([P, GH, D]),
                                            ALU.subtract).then_inc(s_sub, 1)
                return fn

            def normalise(u, p):
                o = pO[:, 0:144].rearrange("p (h c) -> p h c", c=9)
                done(dve, s_o, u)
                nc.vector.reciprocal(rden[:, p], o[:, :, 8:9]).then_inc(s_rd, 1)
                done(dve, s_rd, u)
                free(dve, s_zt, u)
                nc.vector.tensor_tensor(zn[:, p], o[:, :, 0:8], rden[:, p].broadcast_to([P, HEADS, 8]),
                                        ALU.mult).then_inc(s_zn, 1)

            def residual(u, p):
                done(dve, s_y, u)
                nc.vector.scalar_tensor_tensor(X[:, u, :], pW, bias[:, 5:6], X[:, u, :], ALU.add,
                                               ALU.add).then_inc(s_x, 1)

            pipeline(dve, NT, [(6, softmax(0)), (9, normalise),
                               (3, lambda u, p: ln.vector_apply(dve, u, p)), (4, rotate), (10, residual),
                               (6, softmax(1)), (0, lambda u, p: ln.vector_stats(dve, u, p)),
                               (1, lambda u, p: ln.vector_moments(dve, u, p))])

        @block.scalar
        def _(act):
            act.wait_ge(s_ones, 1)

            def exps(half):
                def fn(u, p):
                    act.wait_ge(s_sub, 2 * u + half + 1)
                    hs = slice(GH * half, GH * half + GH)
                    nc.scalar.activation(Pr[:, p, hs], Pr[:, p, hs], ACT.Exp, scale=SCALE
                                         ).then_inc(s_exp, 1)
                return fn

            def take_pt(quarter):
                def fn(u, p):
                    act.wait_ge(s_pt, 4 * u + quarter + 1)
                    free(act, s_o, u)
                    nc.scalar.activation(PT[:, p, 4 * quarter:4 * quarter + 4],
                                         PTp[:, :].rearrange("p (h k) -> p h k", k=D),
                                         ACT.Copy).then_inc(s_pts, 1)
                return fn

            def take_v(u, p):
                done(act, s_v, u)
                free(act, s_o, u)
                nc.scalar.activation(V[:, p, :, 0:8], pV.rearrange("p (h c) -> p h c", c=8), ACT.Copy
                                     ).then_inc(s_vs, 1)

            def take_zt(u, p):
                done(act, s_zt, u)
                free(act, s_y, u)
                nc.scalar.activation(zT[:, p, :], pZ, ACT.Identity, bias=w("a0_bias")[:, 4:5]
                                     ).then_inc(s_zts, 1)

            pipeline(act, NT, [(7, take_pt(0)), (6, exps(0)), (7, take_pt(1)), (9, take_zt), (7, take_v),
                               (7, take_pt(2)), (6, exps(1)), (7, take_pt(3))])

        small = Bank(NT, {"y": (10, s_x, 1, 1), "z": (9, s_zts, 1, 1), "v": (7, s_vs, 1, 1)})

        @block.tensor
        def _(pe):
            pe.wait_ge(s_ones, 1)

            def project(u, p):
                done(pe, ln.s_xn, u)
                landed(pe, s_cK, u, p)
                free(pe, s_sin, u, bufs=1)
                nc.tensor.matmul(pQ[:, 0, :], w("a0_wq"), xn[:, p, :], start=True, stop=True)
                nc.tensor.matmul(pQ[:, 1, :], w("a0_wk"), cK[:, p, :], start=True, stop=True)
                nc.tensor.matmul(pQ[:, 2, :], w("a0_wqr"), xn[:, p, :], start=True, stop=True)
                nc.tensor.matmul(pQ[:, 3, :], w("a0_wkr"), cK[:, p, :], start=True, stop=True
                                 ).then_inc(s_proj, 1)

            def values(u, p):
                landed(pe, s_cV, u, p)
                small.take(pe, "v", u)
                nc.tensor.matmul(pV, cV[:, p, :], w("a0_wv"), start=True, stop=True).then_inc(s_v, 1)

            def scores(half):
                def fn(u, p):
                    done(pe, s_km, u)
                    if not (isinstance(u, int) and u == 0):
                        pe.wait_ge(s_sub, 2 * u + (half - 1))
                    for n in range(2):
                        k4 = kM[:, p, GH * half + 4 * n:GH * half + 4 * n + 4, :]
                        last = nc.tensor.matmul(S[:, half, 512 * n:512 * n + 512], qk[:, p, 0, :], k4,
                                                start=True, stop=True)
                    last.then_inc(s_S, 1)
                return fn

            def transpose_p(quarter):
                def fn(u, p):
                    pe.wait_ge(s_exp, 2 * u + quarter // 2 + 1)
                    if not (isinstance(u, int) and 4 * u + quarter == 0):
                        pe.wait_ge(s_pts, 4 * u + quarter)
                    for h in range(4):
                        last = nc.tensor.transpose(PTp[:, D * h:D * h + D],
                                                   Pr[:, p, 4 * quarter + h, :], w("ident"))
                    last.then_inc(s_pt, 1)
                return fn

            def product_v(quarter):
                def fn(u, p):
                    pe.wait_ge(s_pts, 4 * u + quarter + 1)
                    if quarter == 0:
                        done(pe, s_vs, u)
                        free(pe, s_zn, u, bufs=1)
                    for h in range(4 * quarter, 4 * quarter + 4):
                        last = nc.tensor.matmul(pO[:, 9 * h:9 * h + 9], PT[:, p, h, :], V[:, p, h, :],
                                                start=True, stop=True)
                    if quarter == 3:
                        last.then_inc(s_o, 1)
                return fn

            def transpose_z(u, p):
                done(pe, s_zn, u)
                small.take(pe, "z", u)
                nc.tensor.transpose(pZ, zn[:, p].rearrange("p h c -> p (h c)"), w("ident")
                                    ).then_inc(s_zt, 1)

            def output(u, p):
                done(pe, s_zts, u)
                small.take(pe, "y", u)
                nc.tensor.matmul(pW, w("a0_wo"), zT[:, p, :], start=True, stop=True).then_inc(s_y, 1)

            pipeline(pe, NT, [(10, output), (7, transpose_p(0)), (8, product_v(0)), (9, transpose_z),
                              (7, transpose_p(1)), (8, product_v(1)), (7, transpose_p(2)), (7, values),
                              (8, product_v(2)), (5, scores(0)), (8, product_v(3)), (7, transpose_p(3)),
                              (3, project), (5, scores(1))])


def key_attention0_stage(net):
    nc, X, w = net.nc, net.X, net.w
    SCALE = D ** -0.5
    RUN = P + 8
    with ExitStack() as ctx:
        sb, ps, sem = opener(net, ctx, "f0")
        xn = sb("xn", [P, 2, D])
        xT = sb("xT", [P, 2, P])
        blk = sb("blk", [P, 2, 2, P])
        spread = sb("spread", [P, 2, 2, GH, T])
        Pr = sb("Pr", [P, 2, HEADS, T])
        mx = sb("mx", [P, 2, HEADS])
        sums = sb("sums", [P, 2, HEADS])
        rden = sb("rden", [P, 2, 2, GH, 1])
        vsp = sb("vsp", [P, 2, 2, GH * RUN])
        zT = sb("zT", [P, 2, 2, P])
        wow = sb("wow", [P, 2, 2 * D])
        junk = sb("junk", [P, D])
        vraw = net.R
        S = ps("S", [P, 2, 1024])
        pX, pA, pZ, pY = [ps(n, [P, 512]) for n in ("pX", "pA", "pZ", "pY")]
        s_zero = sem("zero")
        s_xt, s_xts, s_proj, s_v = sem("xt"), sem("xt_out"), sem("proj"), sem("v")
        s_blk, s_spread = sem("blk"), sem("spread")
        s_S, s_mx, s_sub, s_exp, s_sum = sem("scores"), sem("max"), sem("sub"), sem("exp"), sem("sum")
        s_rd, s_vs, s_z, s_zt, s_y = sem("rden"), sem("v_out"), sem("z"), sem("zt"), sem("y")
        s_w, s_sq, s_wz, s_wzs = sem("w_out"), sem("squares"), sem("wowff"), sem("wowff_out")
        ln = LayerNorm(net, sb, sem, xn, s_xt)
        block = ctx.enter_context(nc.Block())

        @block.sync
        def _(sp):
            clear_stale(net, sp)

        @block.gpsimd
        def _(pool):
            ln.setup(pool)
            for t in (blk, vsp, zT):
                nc.gpsimd.memset(t[:], 0.0).then_inc(s_zero, 1)
            pipeline(pool, NT, [(1, lambda u, p: ln.pool_rstd(pool, u, p))])

        @block.vector
        def _(dve):
            mask = w("maskB").unsqueeze(2).broadcast_to([P, GH, T])

            def take_spread(u, p):
                done(dve, s_v, u)
                free(dve, s_S, u, per=2)
                for g in range(2):
                    src = pA[:, 384 + T * g:384 + T * g + T].unsqueeze(1).broadcast_to([P, GH, T])
                    i = nc.vector.tensor_tensor(spread[:, p, g], src, mask, ALU.mult)
                i.then_inc(s_spread, 1)

            def softmax(g):
                def fn(u, p):
                    hs = slice(GH * g, GH * g + GH)
                    Sg = S[:, p, 512 * g:512 * g + 512].rearrange("p (h k) -> p h k", k=T)
                    dve.wait_ge(s_S, 2 * u + g + 1)
                    nc.vector.tensor_reduce(mx[:, p, hs], Sg, AX, ALU.max).then_inc(s_mx, 1)
                    dve.wait_ge(s_mx, 2 * u + g + 1)
                    free(dve, s_z, u)
                    nc.vector.tensor_tensor(Pr[:, p, hs], Sg,
                                            mx[:, p, hs].unsqueeze(2).broadcast_to([P, GH, T]),
                                            ALU.subtract).then_inc(s_sub, 1)
                return fn

            def divide_v(u, p):
                done(dve, s_exp, u)
                nc.vector.tensor_reduce(sums[:, p, :], Pr[:, p], AX, ALU.add).then_inc(s_sum, 1)
                done(dve, s_sum, u)
                free(dve, s_vs, u)
                nc.vector.reciprocal(rden[:, p].rearrange("p g h c -> p (g h c)"), sums[:, p, :]
                                     ).then_inc(s_rd, 1)
                done(dve, s_rd, u)
                free(dve, s_z, u)
                for b in range(2):
                    r = slice(64 * b, 64 * b + 64)
                    out = vsp[r, p].rearrange("p g (h x) -> p g h x", x=RUN)[:, :, :, 64 * b:64 * b + 8]
                    i = nc.vector.tensor_tensor(
                        out, vraw[r, u, :].rearrange("p (g h c) -> p g h c", g=2, c=8),
                        rden[r, p].broadcast_to([64, 2, GH, 8]), ALU.mult)
                i.then_inc(s_vs, 1)

            def keep_w(u, p):
                done(dve, s_y, u)
                nc.vector.tensor_copy(net.Y[:, u, :], pY[:, 128:256]).then_inc(s_w, 1)

            dve.wait_ge(s_zero, 3)
            dve.wait_ge(s_wz, 1)
            nc.vector.tensor_copy(wow[:, :, D:2 * D], pA[:, 0:2 * D].rearrange("p (g d) -> p g d", g=2)
                                  ).then_inc(s_wzs, 1)
            nc.vector.tensor_copy(wow[:, :, 0:D], w("f0_wo2").rearrange("p (g d) -> p g d", g=2)
                                  ).then_inc(s_wzs, 1)
            pipeline(dve, NT, [(4, take_spread), (9, keep_w),
                               (2, lambda u, p: ln.vector_apply(dve, u, p)),
                               (0, lambda u, p: ln.vector_stats(dve, u, p)),
                               (1, lambda u, p: ln.vector_moments(dve, u, p)), (6, divide_v),
                               (5, softmax(0)), (5, softmax(1))])

        @block.scalar
        def _(act):
            act.wait_ge(s_zero, 3)

            def take_xt(u, p):
                done(act, s_xt, u)
                free(act, s_proj, u)
                nc.scalar.activation(xT[:, p, :], pX[:, 0:128], ACT.Copy).then_inc(s_xts, 1)

            def take_blk(u, p):
                done(act, s_proj, u)
                free(act, s_S, u, per=2)
                for b in range(2):
                    r = slice(64 * b, 64 * b + 64)
                    i = nc.scalar.activation(blk[r, p, :, 64 * b:64 * b + 64],
                                             pA[r, 256:384].rearrange("p (g t) -> p g t", t=T), ACT.Copy)
                i.then_inc(s_blk, 1)
                nc.scalar.activation(vraw[:, u, :], pA[:, 128:256], ACT.Copy).then_inc(s_v, 1)

            def exps(u, p):
                done(act, s_sub, u, per=2)
                nc.scalar.activation(Pr[:, p], Pr[:, p], ACT.Exp, scale=SCALE).then_inc(s_exp, 1)

            def take_z(u, p):
                done(act, s_z, u)
                free(act, s_y, u)
                for b in range(2):
                    r = slice(64 * b, 64 * b + 64)
                    i = nc.scalar.activation(zT[r, p, :, 64 * b:64 * b + 64],
                                             pZ[r, 0:128].rearrange("p (g t) -> p g t", t=T), ACT.Copy)
                i.then_inc(s_zt, 1)

            def squares(u, p):
                done(act, s_w, u)
                nc.scalar.activation(junk[:, :], pY[:, 0:128], ACT.Square,
                                     accum_out=net.norms[:, 0, u:u + 1] if isinstance(u, int)
                                     else net.norms[:, 0, bass.ds(u, 1)]).then_inc(s_sq, 1)

            pipeline(act, NT, [(9, squares), (7, take_z), (3, take_blk), (5, exps), (2, take_xt)])

        @block.tensor
        def _(pe):
            for g in range(2):
                i = nc.tensor.matmul(pA[:, D * g:D * g + D], w("f0_woT2", D * g, D * g + D), w("f0_wff"),
                                     start=True, stop=True)
            i.then_inc(s_wz, 1)

            def transpose_x(u, p):
                done(pe, ln.s_xn, u)
                free(pe, s_xts, u, bufs=1)
                nc.tensor.transpose(pX[:, 0:128], xn[:, p, :], w("ident")).then_inc(s_xt, 1)

            def project(u, p):
                done(pe, s_xts, u)
                free(pe, s_spread, u, bufs=1)
                nc.tensor.matmul(pA[:, 128:256], xT[:, p, :], w("f0_wv"), start=True, stop=True)
                for b in range(2):
                    r = slice(64 * b, 64 * b + 64)
                    for g in range(2):
                        c = slice(64 * g, 64 * g + 64)
                        nc.tensor.matmul(pA[r, 256 + T * g:256 + T * g + T], w("f0_wk")[:, c],
                                         xT[:, p, r], start=True, stop=True)
                        i = nc.tensor.matmul(pA[r, 384 + T * g:384 + T * g + T], w("f0_wq")[:, c],
                                             xT[:, p, r], start=True, stop=True)
                i.then_inc(s_proj, 1)

            def scores(g):
                def fn(u, p):
                    done(pe, s_spread, u)
                    done(pe, s_blk, u)
                    free(pe, s_sub, u, per=2)
                    nc.tensor.matmul(S[:, p, 512 * g:512 * g + 512], blk[:, p, g, :],
                                     spread[:, p, g].rearrange("p h t -> p (h t)"),
                                     start=True, stop=True).then_inc(s_S, 1)
                return fn

            def product_v(g):
                def fn(u, p):
                    if g == 0:
                        done(pe, s_vs, u)
                        free(pe, s_zt, u, bufs=1)
                    for h in range(GH):
                        i = nc.tensor.matmul(pZ[:, T * g:T * g + T], vsp[:, p, g, P * h:P * h + P],
                                             Pr[:, p, GH * g + h, :], start=h == 0, stop=h == GH - 1)
                    if g == 1:
                        i.then_inc(s_z, 1)
                return fn

            def output(u, p):
                done(pe, s_zt, u)
                free(pe, s_sq, u, bufs=1)
                for g in range(2):
                    i = nc.tensor.matmul(pY[:, 0:256], zT[:, p, g, :], wow[:, g, :],
                                         start=g == 0, stop=g == 1)
                i.then_inc(s_y, 1)

            pe.wait_ge(s_wzs, 2)
            pipeline(pe, NT, [(5, scores(0)), (5, scores(1)), (9, output), (7, product_v(0)),
                              (7, product_v(1)), (3, project), (2, transpose_x)])


def norm_gelu_stage(net):
    nc, X, Y = net.nc, net.X, net.Y
    PART = NT // 4
    with ExitStack() as ctx:
        sb, ps, sem = opener(net, ctx, "n0")
        sq = sb("squares", [P, PART, D])
        root = sb("root", [P, 2, NT])
        inv = sb("inv", [P, 2, NT])
        s_sq, s_ss, s_rt, s_v, s_m, s_g, s_x = [sem(n) for n in (
            "squares", "sums", "root", "factor", "scaled", "gelu", "x")]
        block = ctx.enter_context(nc.Block())

        @block.sync
        def _(sp):
            clear_stale(net, sp)

        def part(t, k):
            return t[:, PART * k:PART * k + PART, :]

        @block.gpsimd
        def _(pool):
            for k in range(4):
                pool.wait_ge(s_ss, k)
                nc.gpsimd.tensor_tensor(sq[:, :, :], part(Y, k), part(Y, k), ALU.mult).then_inc(s_sq, 1)

        @block.vector
        def _(dve):
            for k in range(4):
                dve.wait_ge(s_sq, k + 1)
                nc.vector.tensor_reduce(net.norms[:, 1, PART * k:PART * k + PART], sq[:, :, :], AX,
                                        ALU.add).then_inc(s_ss, 1)
            dve.wait_ge(s_rt, 1)
            nc.vector.tensor_scalar(root[:, 0], root[:, 0], L2_EPS, None, ALU.max).then_inc(s_v, 1)
            dve.wait_ge(s_v, 1)
            nc.vector.reciprocal(inv[:, 0], root[:, 0]).then_inc(s_v, 1)
            dve.wait_ge(s_v, 2)
            nc.vector.tensor_tensor(root[:, 1], root[:, 1], inv[:, 0], ALU.mult).then_inc(s_v, 1)
            dve.wait_ge(s_v, 3)
            nc.vector.tensor_scalar(root[:, 1], root[:, 1], L2_EPS, None, ALU.max).then_inc(s_v, 1)
            dve.wait_ge(s_v, 4)
            nc.vector.reciprocal(inv[:, 1], root[:, 1]).then_inc(s_v, 1)
            dve.wait_ge(s_v, 5)
            nc.vector.tensor_tensor(inv[:, 0], inv[:, 0], inv[:, 1], ALU.mult).then_inc(s_v, 1)
            dve.wait_ge(s_v, 6)
            for k in range(4):
                f = inv[:, 0, PART * k:PART * k + PART].unsqueeze(2).broadcast_to([P, PART, D])
                nc.vector.tensor_tensor(part(Y, k), part(Y, k), f, ALU.mult).then_inc(s_m, 1)
            for k in range(4):
                dve.wait_ge(s_g, k + 1)
                nc.vector.tensor_tensor(part(X, k), part(X, k), part(Y, k), ALU.add).then_inc(s_x, 1)

        @block.scalar
        def _(act):
            act.wait_ge(s_ss, 4)
            nc.scalar.activation(root[:, :, :], net.norms[:, :, :], ACT.Sqrt).then_inc(s_rt, 1)
            for k in range(4):
                act.wait_ge(s_m, k + 1)
                nc.scalar.activation(part(Y, k), part(Y, k), ACT.Gelu).then_inc(s_g, 1)


def attention1_stage(net):
    nc, X, w = net.nc, net.X, net.w
    SCALE = 8 ** -0.5
    with ExitStack() as ctx:
        sb, ps, sem = opener(net, ctx, "a1")
        xn = sb("xn", [P, 2, D])
        xT = sb("xT", [P, 2, P])
        cK = sb("cK", [P, 2, P])
        cV = sb("cV", [P, 2, P])
        blk = sb("blk", [P, 2, 2, P])
        spread = sb("spread", [P, 2, 2, GH, T])
        Pr = sb("Pr", [P, 2, 2, GH * T])
        mx = sb("mx", [P, 2, 2, GH])
        V = sb("V", [P, 2, 2, 8, 2, 9])
        PT = sb("PT", [P, 2, 8, P])
        zn = sb("zn", [P, 2, D])
        zT = sb("zT", [P, 2, P])
        rden = sb("rden", [P, 2, HEADS, 1])
        allow = sb("allow", [P, T], BF16)
        identb = sb("identb", [P, P], BF16)
        S = ps("S", [P, 2, 512])
        PTp = ps("PTp", [P, 2, 512])
        pXY, pA, pVZ, pO = [ps(n, [P, 512]) for n in ("pXY", "pA", "pVZ", "pO")]
        pX, pY, pV, pZ = pXY[:, 0:128], pXY[:, 128:256], pVZ[:, 0:128], pVZ[:, 128:256]
        s_ones, s_zero, s_tb = sem("ones"), sem("zero"), sem("tables")
        s_cK = [sem("cK_even"), sem("cK_odd")]
        s_cV = [sem("cV_even"), sem("cV_odd")]
        s_xt, s_xts, s_proj = sem("xt"), sem("xt_out"), sem("proj")
        s_blk, s_spread = sem("blk"), sem("spread")
        s_S, s_mx, s_sub, s_exp = sem("scores"), sem("max"), sem("sub"), sem("exp")
        s_pt, s_pts, s_v, s_vs = sem("pt"), sem("pt_out"), sem("v"), sem("v_out")
        s_o, s_rd, s_zn, s_zt, s_zts = sem("o"), sem("rden"), sem("zn"), sem("zt"), sem("zt_out")
        s_y, s_add, s_x = sem("y"), sem("added"), sem("x")
        ln = LayerNorm(net, sb, sem, xn, s_xt)
        block = ctx.enter_context(nc.Block())

        @block.sync
        def _(sp):
            clear_stale(net, sp)

            def load_for(tile, sems, reader):
                def fn(u, p):
                    free(sp, reader, u)
                    sp.dma_start(tile[:, p, :], net.dram["ctxT"][u]).then_inc(sems[p], 16)
                return fn
            pipeline(sp, NT, [(2, load_for(cK, s_cK, s_proj)), (4, load_for(cV, s_cV, s_v))])

        @block.gpsimd
        def _(pool):
            ln.setup(pool)
            nc.gpsimd.memset(blk[:, :, :, :], 0.0).then_inc(s_zero, 1)
            nc.gpsimd.memset(V[:, :, :, :, :, :], 0.0).then_inc(s_ones, 1)
            for h in range(2):
                pool.wait_ge(s_ones, h + 1)
                nc.gpsimd.memset(V[64 * h:64 * h + 64, :, :, :, h, 8:9], 1.0).then_inc(s_ones, 1)
            pool.wait_ge(s_ones, 3)
            pipeline(pool, NT, [(1, lambda u, p: ln.pool_rstd(pool, u, p))])

        @block.vector
        def _(dve):
            mask = w("maskB").unsqueeze(2).broadcast_to([P, GH, T])
            nc.vector.tensor_copy(allow[:, :], w("allow1")).then_inc(s_tb, 1)
            nc.vector.tensor_copy(identb[:, :], w("ident")).then_inc(s_tb, 1)

            def take_spread(u, p):
                done(dve, s_blk, u)
                free(dve, s_S, u, per=2)
                for g in range(2):
                    src = pA[:, 384 + T * g:384 + T * g + T].unsqueeze(1).broadcast_to([P, GH, T])
                    i = nc.vector.scalar_tensor_tensor(spread[:, p, g], src, w("a1_bk")[:, g:g + 1],
                                                       mask, ALU.add, ALU.mult)
                i.then_inc(s_spread, 1)

            def softmax(g):
                def fn(u, p):
                    Sg = S[:, g, :].rearrange("p (h k) -> p h k", k=T)
                    dve.wait_ge(s_S, 2 * u + g + 1)
                    nc.vector.tensor_reduce(mx[:, p, g, :], Sg, AX, ALU.max).then_inc(s_mx, 1)
                    dve.wait_ge(s_mx, 2 * u + g + 1)
                    free(dve, s_pt, u, per=2)
                    nc.vector.tensor_tensor(Pr[:, p, g, :].rearrange("p (h k) -> p h k", k=T), Sg,
                                            mx[:, p, g, :].unsqueeze(2).broadcast_to([P, GH, T]),
                                            ALU.subtract).then_inc(s_sub, 1)
                return fn

            def normalise(u, p):
                o = pO[:, 0:144].rearrange("p (h c) -> p h c", c=9)
                done(dve, s_o, u)
                nc.vector.reciprocal(rden[:, p], o[:, :, 8:9]).then_inc(s_rd, 1)
                done(dve, s_rd, u)
                free(dve, s_zt, u)
                nc.vector.tensor_tensor(zn[:, p, :].rearrange("p (h c) -> p h c", c=8), o[:, :, 0:8],
                                        rden[:, p].broadcast_to([P, HEADS, 8]), ALU.mult
                                        ).then_inc(s_zn, 1)

            def residual(u, p):
                done(dve, s_y, u)
                nc.vector.tensor_tensor(X[:, u, :], pY, X[:, u, :], ALU.add).then_inc(s_add, 1)
                done(dve, s_add, u)
                nc.vector.tensor_tensor(X[:, u, :], X[:, u, :], w("a1_bo"), ALU.add).then_inc(s_x, 1)

            pipeline(dve, NT, [(0, lambda u, p: ln.vector_stats(dve, u, p)),
                               (1, lambda u, p: ln.vector_moments(dve, u, p)), (10, normalise),
                               (2, lambda u, p: ln.vector_apply(dve, u, p)), (7, softmax(0)),
                               (11, residual), (7, softmax(1)), (5, take_spread)])

        @block.scalar
        def _(act):
            act.wait_ge(s_zero, 1)
            act.wait_ge(s_ones, 3)

            def take_xt(u, p):
                done(act, s_xt, u)
                free(act, s_proj, u)
                nc.scalar.activation(xT[:, p, :], pX, ACT.Copy).then_inc(s_xts, 1)

            def take_blk(u, p):
                done(act, s_proj, u)
                free(act, s_S, u, per=2)
                for b in range(2):
                    r = slice(64 * b, 64 * b + 64)
                    for g in range(2):
                        i = nc.scalar.activation(blk[r, p, g, 64 * b:64 * b + 64],
                                                 pA[r, 256 + T * g:256 + T * g + T], ACT.Identity,
                                                 bias=w("a1_bq")[r, g:g + 1])
                i.then_inc(s_blk, 1)

            def exps(g):
                def fn(u, p):
                    act.wait_ge(s_sub, 2 * u + g + 1)
                    nc.scalar.activation(Pr[:, p, g, :], Pr[:, p, g, :], ACT.Exp, scale=SCALE
                                         ).then_inc(s_exp, 1)
                return fn

            def take_v(u, p):
                done(act, s_v, u)
                free(act, s_o, u)
                for h in range(2):
                    r = slice(64 * h, 64 * h + 64)
                    i = nc.scalar.activation(
                        V[r, p, :, :, h, 0:8].rearrange("p b j c -> p (b j) c"),
                        pV[r, :].rearrange("p (n c) -> p n c", c=8), ACT.Copy)
                i.then_inc(s_vs, 1)

            def take_pt(g):
                def fn(u, p):
                    free(act, s_o, u)
                    act.wait_ge(s_pt, 2 * u + g + 1)
                    nc.scalar.activation(PT[:, p, 4 * g:4 * g + 4].rearrange("p j q -> p (j q)"),
                                         PTp[:, g, :], ACT.Copy).then_inc(s_pts, 1)
                return fn

            def take_zt(u, p):
                done(act, s_zt, u)
                free(act, s_y, u)
                nc.scalar.activation(zT[:, p, :], pZ, ACT.Identity, bias=w("a1_bv")).then_inc(s_zts, 1)

            pipeline(act, NT, [(10, take_zt), (8, take_v), (3, take_xt), (8, take_pt(0)),
                               (8, take_pt(1)), (7, exps(0)), (7, exps(1)), (4, take_blk)])

        turnsXY = Bank(NT, {"y": (11, s_x, 1, 1), "xt": (3, s_xts, 1, 1)})
        turnsVZ = Bank(NT, {"z": (10, s_zts, 1, 1), "v": (8, s_vs, 1, 1)})

        @block.tensor
        def _(pe):
            def transpose_x(u, p):
                done(pe, ln.s_xn, u)
                turnsXY.take(pe, "xt", u)
                nc.tensor.transpose(pX, xn[:, p, :], w("ident")).then_inc(s_xt, 1)

            def project(u, p):
                done(pe, s_xts, u)
                landed(pe, s_cK, u, p)
                free(pe, s_spread, u, bufs=1)
                for b in range(2):
                    r = slice(64 * b, 64 * b + 64)
                    for g in range(2):
                        c = slice(64 * g, 64 * g + 64)
                        nc.tensor.matmul(pA[r, 256 + T * g:256 + T * g + T], w("a1_wq")[:, c],
                                         xT[:, p, r], start=True, stop=True)
                        i = nc.tensor.matmul(pA[r, 384 + T * g:384 + T * g + T], w("a1_wk")[:, c],
                                             cK[:, p, r], start=True, stop=True)
                i.then_inc(s_proj, 1)

            def scores(g):
                def fn(u, p):
                    done(pe, s_spread, u)
                    if not (isinstance(u, int) and u == 0):
                        pe.wait_ge(s_sub, 2 * u + (g - 1))
                    nc.tensor.matmul(S[:, g, :], identb[:, :],
                                     allow[:, :].unsqueeze(1).broadcast_to([P, GH, T]),
                                     start=True, stop=False)
                    nc.tensor.matmul(S[:, g, :], blk[:, p, g, :],
                                     spread[:, p, g].rearrange("p h t -> p (h t)"),
                                     start=False, stop=True).then_inc(s_S, 1)
                return fn

            def transpose_p(g):
                def fn(u, p):
                    pe.wait_ge(s_exp, 2 * u + g + 1)
                    if not (isinstance(u, int) and u == 0):
                        pe.wait_ge(s_pts, 2 * u + (g - 1))
                    for j in range(4):
                        i = nc.tensor.transpose(PTp[:, g, P * j:P * j + P],
                                                Pr[:, p, g, P * j:P * j + P], w("ident"))
                    i.then_inc(s_pt, 1)
                return fn

            def values(u, p):
                landed(pe, s_cV, u, p)
                turnsVZ.take(pe, "v", u)
                wv = w("a1_wv").rearrange("p (j h c) -> p h j c", h=2, c=8)
                for b in range(2):
                    for h in range(2):
                        i = nc.tensor.matmul(pV[64 * h:64 * h + 64, 64 * b:64 * b + 64],
                                             cV[:, p, 64 * b:64 * b + 64], wv[:, h],
                                             start=True, stop=True)
                i.then_inc(s_v, 1)

            def product_v(g):
                def fn(u, p):
                    pe.wait_ge(s_pts, 2 * u + g + 1)
                    if g == 0:
                        done(pe, s_vs, u)
                        free(pe, s_zn, u, bufs=1)
                    for b in range(2):
                        r = slice(64 * b, 64 * b + 64)
                        for j in range(4 * g, 4 * g + 4):
                            i = nc.tensor.matmul(pO[r, 18 * j:18 * j + 18], PT[:, p, j, r],
                                                 V[:, p, b, j].rearrange("p h c -> p (h c)"),
                                                 start=True, stop=True)
                    if g == 1:
                        i.then_inc(s_o, 1)
                return fn

            def transpose_z(u, p):
                done(pe, s_zn, u)
                turnsVZ.take(pe, "z", u)
                nc.tensor.transpose(pZ, zn[:, p, :], w("ident")).then_inc(s_zt, 1)

            def output(u, p):
                done(pe, s_zts, u)
                turnsXY.take(pe, "y", u)
                nc.tensor.matmul(pY, zT[:, p, :], w("a1_wo"), start=True, stop=True).then_inc(s_y, 1)

            pe.wait_ge(s_tb, 2)
            pipeline(pe, NT, [(10, transpose_z), (11, output), (9, product_v(0)), (9, product_v(1)),
                              (8, values), (8, transpose_p(0)), (8, transpose_p(1)), (3, transpose_x),
                              (6, scores(0)), (6, scores(1)), (4, project)])


def attention2_stage(net):
    nc, X, w = net.nc, net.X, net.w
    SCALE = 64 ** -0.5
    with ExitStack() as ctx:
        sb, ps, sem = opener(net, ctx, "a2")
        xn = sb("xn", [P, 2, D])
        xT = sb("xT", [P, 2, P])
        cK = sb("cK", [P, 2, P])
        cV = sb("cV", [P, 2, P])
        q = sb("q", [P, 2, 4, P])
        k = sb("k", [P, 2, 4, 2, P])
        V = sb("V", [P, 2, 2, 4, 2, 65])
        Pr = sb("Pr", [P, 2, 512])
        PT = sb("PT", [P, 2, 4, P])
        mx = sb("mx", [P, 2, 8])
        rden = sb("rden", [P, 2, 2, 4, 1])
        zn = sb("zn", [P, 2, 512])
        zT = sb("zT", [P, 2, 4, P])
        S, pQ, pK, pV, pT, pZ = [ps(n, [P, 512]) for n in ("S", "pQ", "pK", "pV", "pT", "pZ")]
        pO = ps("pO", [P, 2, 512])
        s_ones, s_zero = sem("ones"), sem("zero")
        s_cK = [sem("cK_even"), sem("cK_odd")]
        s_cV = [sem("cV_even"), sem("cV_odd")]
        s_xt, s_xts, s_q, s_qs, s_k, s_ks = [sem(n) for n in ("xt", "xt_out", "q", "q_out", "k", "k_out")]
        s_v, s_vs, s_S, s_mx, s_sub, s_exp = [sem(n) for n in ("v", "v_out", "scores", "max", "sub", "exp")]
        s_pt, s_pts, s_o, s_rd, s_zn = [sem(n) for n in ("pt", "pt_out", "o", "rden", "zn")]
        s_zt, s_zts, s_y, s_add, s_x = [sem(n) for n in ("zt", "zt_out", "y", "bias_added", "x")]
        combine = Combine(net, net.routing, sem)
        ln = LayerNorm(net, sb, sem, xn, s_xt, combine.s_x)
        block = ctx.enter_context(nc.Block())

        @block.sync
        def _(sp):
            clear_stale(net, sp)

            def load_for(tile, sems, reader):
                def fn(u, p):
                    free(sp, reader, u)
                    sp.dma_start(tile[:, p, :], net.dram["ctxT"][u]).then_inc(sems[p], 16)
                return fn
            pipeline(sp, NT, [(1, load_for(cK, s_cK, s_k)), (3, load_for(cV, s_cV, s_v))])

        @block.gpsimd
        def _(pool):
            ln.setup(pool)
            nc.gpsimd.memset(k[:, :, :, :, :], 0.0).then_inc(s_zero, 1)
            nc.gpsimd.memset(V[:, :, :, :, :, :], 0.0).then_inc(s_ones, 1)
            for h in range(2):
                pool.wait_ge(s_ones, h + 1)
                nc.gpsimd.memset(V[64 * h:64 * h + 64, :, :, :, h, 64:65], 1.0).then_inc(s_ones, 1)
            pool.wait_ge(s_ones, 3)
            pipeline(pool, NT, [(IN_FLIGHT, lambda u, p: combine.add(pool, u)),
                                (IN_FLIGHT + 1, lambda u, p: ln.pool_rstd(pool, u, p)),
                                (0, lambda u, p: combine.gather(u))], straight=True)

        @block.vector
        def _(dve):
            dve.wait_ge(s_zero, 1)

            def take_k(u, p):
                done(dve, s_k, u)
                free(dve, s_S, u)
                for h in range(2):
                    r = slice(64 * h, 64 * h + 64)
                    i = nc.vector.tensor_copy(k[r, p, :, h, :], pK[r, :].rearrange("p (j t) -> p j t", j=4))
                i.then_inc(s_ks, 1)

            def softmax(u, p):
                Sh = S[:, :].rearrange("p (h k) -> p h k", k=T)
                done(dve, s_S, u)
                nc.vector.tensor_reduce(mx[:, p, :], Sh, AX, ALU.max).then_inc(s_mx, 1)
                done(dve, s_mx, u)
                free(dve, s_pt, u)
                nc.vector.tensor_tensor(Pr[:, p, :].rearrange("p (h k) -> p h k", k=T), Sh,
                                        mx[:, p, :].unsqueeze(2).broadcast_to([P, 8, T]),
                                        ALU.subtract).then_inc(s_sub, 1)

            def normalise(u, p):
                o = pO[:, :, 0:260].rearrange("p a (h c) -> p a h c", c=65)
                done(dve, s_o, u)
                nc.vector.reciprocal(rden[:, p], o[:, :, :, 64:65]).then_inc(s_rd, 1)
                done(dve, s_rd, u)
                free(dve, s_zt, u)
                nc.vector.tensor_tensor(zn[:, p, :].rearrange("p (a h c) -> p a h c", a=2, c=64),
                                        o[:, :, :, 0:64], rden[:, p].broadcast_to([P, 2, 4, 64]),
                                        ALU.mult).then_inc(s_zn, 1)

            def residual(u, p):
                done(dve, s_y, u)
                nc.vector.tensor_tensor(X[:, u, :], pV[:, 0:128], X[:, u, :], ALU.add).then_inc(s_add, 1)
                done(dve, s_add, u)
                nc.vector.tensor_tensor(X[:, u, :], X[:, u, :], w("a2_bo"), ALU.add).then_inc(s_x, 1)

            pipeline(dve, NT, [(10, normalise), (7, softmax), (5, take_k),
                               (0, lambda u, p: ln.vector_stats(dve, u, p)),
                               (1, lambda u, p: ln.vector_moments(dve, u, p)),
                               (2, lambda u, p: ln.vector_apply(dve, u, p)), (11, residual)])

        @block.scalar
        def _(act):
            act.wait_ge(s_ones, 3)

            def take_xt(u, p):
                done(act, s_xt, u)
                free(act, s_q, u)
                nc.scalar.activation(xT[:, p, :], pQ[:, 0:128], ACT.Copy).then_inc(s_xts, 1)

            def take_q(u, p):
                done(act, s_q, u)
                free(act, s_S, u)
                nc.scalar.activation(q[:, p].rearrange("p j t -> p (j t)"), pQ[:, :], ACT.Copy
                                     ).then_inc(s_qs, 1)

            def take_v(u, p):
                done(act, s_v, u)
                free(act, s_o, u)
                for h in range(2):
                    r = slice(64 * h, 64 * h + 64)
                    i = nc.scalar.activation(V[r, p, :, :, h, 0:64].rearrange("p b j c -> p (b j) c"),
                                             pV[r, :].rearrange("p (n c) -> p n c", c=64), ACT.Copy)
                i.then_inc(s_vs, 1)

            def exps(u, p):
                done(act, s_sub, u)
                nc.scalar.activation(Pr[:, p, :], Pr[:, p, :], ACT.Exp, scale=SCALE).then_inc(s_exp, 1)

            def take_pt(u, p):
                done(act, s_pt, u)
                free(act, s_o, u)
                nc.scalar.activation(PT[:, p].rearrange("p j t -> p (j t)"), pT[:, :], ACT.Copy
                                     ).then_inc(s_pts, 1)

            def take_zt(u, p):
                done(act, s_zt, u)
                free(act, s_y, u)
                nc.scalar.activation(zT[:, p].rearrange("p j t -> p (j t)"), pZ[:, :], ACT.Copy
                                     ).then_inc(s_zts, 1)

            pipeline(act, NT, [(8, take_pt), (7, exps), (10, take_zt), (3, take_xt), (8, take_v),
                               (4, take_q)])

        turnsQ = Bank(NT, {"xt": (3, s_xts, 1, 1), "q": (4, s_qs, 1, 1)})
        turnsV = Bank(NT, {"y": (11, s_x, 1, 1), "v": (8, s_vs, 1, 1)})

        @block.tensor
        def _(pe):
            def transpose_x(u, p):
                done(pe, ln.s_xn, u)
                turnsQ.take(pe, "xt", u)
                nc.tensor.transpose(pQ[:, 0:128], xn[:, p, :], w("ident")).then_inc(s_xt, 1)

            def project(u, p):
                landed(pe, s_cK, u, p)
                free(pe, s_ks, u, bufs=1)
                for j in range(4):
                    i = nc.tensor.matmul(pK[:, P * j:P * j + P], w("a2_wk", P * j, P * j + P),
                                         cK[:, p, :], start=True, stop=True)
                i.then_inc(s_k, 1)
                done(pe, s_xts, u)
                turnsQ.take(pe, "q", u)
                for j in range(4):
                    i = nc.tensor.matmul(pQ[:, P * j:P * j + P], w("a2_wq", P * j, P * j + P),
                                         xT[:, p, :], start=True, stop=True)
                i.then_inc(s_q, 1)

            def values(u, p):
                landed(pe, s_cV, u, p)
                turnsV.take(pe, "v", u)
                wv = w("a2_wv").rearrange("p (j h c) -> p h j c", h=2, c=64)
                for b in range(2):
                    for h in range(2):
                        i = nc.tensor.matmul(pV[64 * h:64 * h + 64, 256 * b:256 * b + 256],
                                             cV[:, p, 64 * b:64 * b + 64], wv[:, h],
                                             start=True, stop=True)
                i.then_inc(s_v, 1)

            def scores(u, p):
                done(pe, s_qs, u)
                done(pe, s_ks, u)
                free(pe, s_sub, u, bufs=1)
                for b in range(2):
                    r = slice(64 * b, 64 * b + 64)
                    for j in range(4):
                        i = nc.tensor.matmul(S[r, P * j:P * j + P], q[:, p, j, r], k[:, p, j, :, r],
                                             start=True, stop=True)
                i.then_inc(s_S, 1)

            def transpose_p(u, p):
                done(pe, s_exp, u)
                free(pe, s_pts, u, bufs=1)
                for j in range(4):
                    i = nc.tensor.transpose(pT[:, P * j:P * j + P], Pr[:, p, P * j:P * j + P], w("ident"))
                i.then_inc(s_pt, 1)

            def product_v(u, p):
                done(pe, s_pts, u)
                done(pe, s_vs, u)
                free(pe, s_zn, u, bufs=1)
                for b in range(2):
                    r = slice(64 * b, 64 * b + 64)
                    for j in range(4):
                        i = nc.tensor.matmul(pO[r, j // 2, 130 * (j % 2):130 * (j % 2) + 130],
                                             PT[:, p, j, r], V[:, p, b, j].rearrange("p h c -> p (h c)"),
                                             start=True, stop=True)
                i.then_inc(s_o, 1)

            def transpose_z(u, p):
                done(pe, s_zn, u)
                free(pe, s_zts, u, bufs=1)
                for j in range(4):
                    i = nc.tensor.transpose(pZ[:, P * j:P * j + P], zn[:, p, P * j:P * j + P], w("ident"))
                i.then_inc(s_zt, 1)

            def output(u, p):
                done(pe, s_zts, u)
                turnsV.take(pe, "y", u)
                for j in range(4):
                    i = nc.tensor.matmul(pV[:, 0:128], zT[:, p, j, :], w("a2_wo", P * j, P * j + P),
                                         start=(j == 0), stop=(j == 3))
                i.then_inc(s_y, 1)

            pipeline(pe, NT, [(10, transpose_z), (11, output), (8, transpose_p), (9, product_v),
                              (8, values), (6, scores), (3, transpose_x), (4, project)])


NU = NT // 2


def pair(t, u):
    return t[:, 2 * u:2 * u + 2, :] if isinstance(u, int) else t[:, bass.ds(2 * u, 2), :]


class PairNorm:

    def __init__(self, net, sb, sem, name, used=None):
        self.net, self.used = net, used
        self.stats = sb(name + "_stats", [P, 2, 2, 6])
        self.moments = sb(name + "_moments", [P, 2, 2, 2])
        self.rstd = sb(name + "_rstd", [P, 2, 2, 2])
        self.half = sb(name + "_half", [P, 2])
        self.spare = sb(name + "_spare", [1, 1])
        self.s_half, self.s_stats, self.s_spare = sem(name + "_half"), sem(name + "_stats"), sem(name + "_sp")
        self.s_moments, self.s_vareps = sem(name + "_moments"), sem(name + "_vareps")
        self.s_rstd, self.s_out = sem(name + "_rstd"), sem(name + "_out")

    def setup(self, pool):
        self.net.nc.gpsimd.memset(self.half[:, 0:1], -0.5).then_inc(self.s_half, 1)
        self.net.nc.gpsimd.memset(self.half[:, 1:2], LN_EPS).then_inc(self.s_half, 1)
        pool.wait_ge(self.s_half, 2)

    def vector_moments(self, dve, u, p, src):
        nc = self.net.nc
        for t in range(2):
            i = nc.vector.bn_stats(self.stats[:, p, t, :], src(t))
        i.then_inc(self.s_stats, 1)
        done(dve, self.s_stats, u)
        free(dve, self.s_out, u)
        nc.vector.memset(self.spare[:, :], 0.0).then_inc(self.s_spare, 1)
        for t in range(2):
            i = nc.vector.bn_aggr(self.moments[:, p, t, :], self.stats[:, p, t, :])
        i.then_inc(self.s_moments, 1)

    def pool_rstd(self, pool, u, p):
        nc = self.net.nc
        done(pool, self.s_moments, u)
        nc.gpsimd.tensor_tensor(self.rstd[:, p, :, 0:1], self.moments[:, p, :, 1:2],
                                self.half[:, 1:2].unsqueeze(1).broadcast_to([P, 2, 1]), ALU.add
                                ).then_inc(self.s_vareps, 1)
        done(pool, self.s_vareps, u)
        nc.gpsimd.tensor_tensor(self.rstd[:, p, :, 1:2], self.rstd[:, p, :, 0:1],
                                self.half[:, 0:1].unsqueeze(1).broadcast_to([P, 2, 1]), ALU.pow
                                ).then_inc(self.s_rstd, 1)

    def vector_apply(self, dve, u, p, src, dsts):
        done(dve, self.s_moments, u)
        done(dve, self.s_rstd, u)
        if self.used is not None:
            free(dve, self.used, u)
        for t in range(2):
            for dst in dsts(t):
                i = self.net.nc.vector.tensor_scalar(dst, src(t), self.moments[:, p, t, 0:1],
                                                     self.rstd[:, p, t, 1:2], ALU.subtract, ALU.mult)
        i.then_inc(self.s_out, 1)


def tile_of(t, u, k):
    return t[:, 2 * u + k, :]


def affine(net, dve, u, x, gain, bias, s_gain, s_bias, out):
    nc, w = net.nc, net.w
    nc.vector.tensor_tensor(x, x, w(gain).unsqueeze(1).broadcast_to([P, 2, D]), ALU.mult
                            ).then_inc(s_gain, 1)
    done(dve, s_gain, u)
    return nc.vector.tensor_tensor(out, x, w(bias).unsqueeze(1).broadcast_to([P, 2, D]), ALU.add
                                   ).then_inc(s_bias, 1)


def attention3_stage(net, cross):
    nc, X, Y, R, w = net.nc, net.X, net.Y, net.R, net.w
    SCALE = 8 ** -0.5
    i2 = "2" if cross else "1"
    with ExitStack() as ctx:
        sb, ps, sem = opener(net, ctx, "c3" if cross else "s3")
        xs = sb("xs", [P, 2, 2, D])
        xT = sb("xT", [P, 2, 2 * P])
        cT = sb("cT", [P, 2, 2, P]) if cross else None
        qk = sb("qk", [P, 2, 2, 2 * P])
        V = sb("V", [P, NT, D + 1])
        Se = sb("Se", [P, 2, 2, T])
        nz = sb("nz", [P, 2, 2, T])
        ln_ = sb("lengths", [P, 2, 2])
        pad = sb("pad", [P, 2, 2, T])
        mx = sb("mx", [P, 2, 2])
        Pr = sb("Pr", [P, 2, 2, P])
        PT = sb("PT", [P, 2, 2, P])
        rden = sb("rden", [P, 2, 2, 1])
        y = sb("y", [P, 2, 2, D])
        pX, pQ, pV, pS = [ps(n, [P, 512]) for n in ("pX", "pQ", "pV", "pS")]
        pL, pT, pO = [ps(n, [P, 512]) for n in ("pL", "pT", "pO")]
        s_zero, s_ones = sem("zero"), sem("ones")
        s_xs, s_xt, s_xts, s_qk, s_qks, s_v, s_vs = [sem(n) for n in (
            "xs", "xt", "xt_out", "qk", "qk_out", "v", "v_out")]
        s_S, s_Se, s_nz, s_L, s_len, s_pad, s_e1, s_e2, s_mx, s_sub, s_exp = [sem(n) for n in (
            "scores", "scores_out", "nonzero", "first_row", "lengths", "pad", "masked", "masked2",
            "max", "sub", "exp")]
        s_pt, s_pts, s_o, s_rd, s_y, s_g, s_b = [sem(n) for n in (
            "pt", "pt_out", "o", "rden", "y", "gain", "bias")]
        mark = sb("mark", [P, NU])
        combine = None if cross else Combine(net, net.routing, sem)
        n_in = None if cross else PairNorm(net, sb, sem, "nin", s_xt)
        n_out = PairNorm(net, sb, sem, "nout")
        s_in = s_xs if cross else n_in.s_out
        s_cT = [sem("cT_even"), sem("cT_odd")]
        block = ctx.enter_context(nc.Block())

        if cross:
            @block.sync
            def _(sp):
                clear_stale(net, sp)
                ctxT = net.dram["ctxT"].rearrange("n d t -> d n t")

                def load_context(u, p):
                    free(sp, s_v, u)
                    sp.dma_start(cT[:, p], ctxT[:, 2 * u:2 * u + 2, :] if isinstance(u, int)
                                 else ctxT[:, bass.ds(2 * u, 2), :]).then_inc(s_cT[p], 16)
                pipeline(sp, NU, [(0, load_context)])
        else:
            @block.sync
            def _(sp):
                clear_stale(net, sp)

        @block.gpsimd
        def _(pool):
            nc.gpsimd.memset(Pr[:, :, :, :], 0.0).then_inc(s_zero, 1)
            nc.gpsimd.memset(V[:, :, D:D + 1], 1.0).then_inc(s_ones, 1)
            n_out.setup(pool)
            if cross:
                pipeline(pool, NU, [(8, lambda u, p: n_out.pool_rstd(pool, u, p))])
            else:
                n_in.setup(pool)

                def gather(u, p):
                    for t in range(2):
                        combine.gather(2 * u + t)

                ahead = IN_FLIGHT // 2
                pipeline(pool, NU, [(ahead, lambda u, p: combine.report(pool, u, mark[:, u:u + 1])),
                                    (ahead + 1, lambda u, p: n_in.pool_rstd(pool, u, p)),
                                    (0, gather),
                                    (ahead + 9, lambda u, p: n_out.pool_rstd(pool, u, p))],
                         straight=True)

        @block.vector
        def _(dve):
            def copy_in(u, p):
                free(dve, s_xt, u)
                nc.vector.tensor_copy(xs[:, p], pair(Y, u)).then_inc(s_xs, 1)

            def moments_in(u, p):
                if isinstance(u, int):
                    done(dve, combine.s_x, u)
                n_in.vector_moments(dve, u, p, lambda t: tile_of(X, u, t))

            def apply_in(u, p):
                if not isinstance(u, int):
                    done(dve, combine.s_x, u + 1)
                n_in.vector_apply(dve, u, p, lambda t: tile_of(X, u, t),
                                  lambda t: (tile_of(R, u, t), xs[:, p, t]))

            def take_v(u, p):
                done(dve, s_v, u)
                nc.vector.tensor_copy(pair(V, u)[:, :, 0:D], pV[:, 0:2 * D].rearrange("p (a d) -> p a d", a=2)
                                      ).then_inc(s_vs, 1)

            def take_scores(u, p):
                done(dve, s_S, u)
                free(dve, s_e1, u)
                nc.vector.tensor_copy(Se[:, p], pS[:, 0:2 * T].rearrange("p (a k) -> p a k", a=2)
                                      ).then_inc(s_Se, 1)
                done(dve, s_Se, u)
                free(dve, s_L, u)
                nc.vector.tensor_scalar(nz[:, p], Se[:, p], 0.0, None, ALU.not_equal).then_inc(s_nz, 1)

            def softmax(u, p):
                done(dve, s_L, u)
                nc.vector.tensor_reduce(ln_[:, p], pL[:, 0:2 * T].rearrange("p (a k) -> p a k", a=2), AX,
                                        ALU.add).then_inc(s_len, 1)
                done(dve, s_len, u)
                free(dve, s_exp, u)
                nc.vector.tensor_tensor(pad[:, p], w("iota64").unsqueeze(1).broadcast_to([P, 2, T]),
                                        ln_[:, p].unsqueeze(2).broadcast_to([P, 2, T]), ALU.is_ge
                                        ).then_inc(s_pad, 1)
                done(dve, s_pad, u)
                nc.vector.scalar_tensor_tensor(pad[:, p], pad[:, p], NEG, Se[:, p], ALU.mult, ALU.add
                                               ).then_inc(s_e1, 1)
                done(dve, s_e1, u)
                if not cross:
                    nc.vector.tensor_tensor(pad[:, p], pad[:, p],
                                            w("causal").unsqueeze(1).broadcast_to([P, 2, T]), ALU.add
                                            ).then_inc(s_e2, 1)
                    done(dve, s_e2, u)
                nc.vector.tensor_reduce(mx[:, p], pad[:, p], AX, ALU.max).then_inc(s_mx, 1)
                done(dve, s_mx, u)
                nc.vector.tensor_tensor(pad[:, p], pad[:, p],
                                        mx[:, p].unsqueeze(2).broadcast_to([P, 2, T]), ALU.subtract
                                        ).then_inc(s_sub, 1)

            def add_z(u, p):
                done(dve, s_o, u)
                o = pO[:, 0:2 * (D + 1)].rearrange("p (a d) -> p a d", a=2)
                nc.vector.reciprocal(rden[:, p], o[:, :, D:D + 1]).then_inc(s_rd, 1)
                done(dve, s_rd, u)
                free(dve, s_b, u)
                for t in range(2):
                    i = nc.vector.scalar_tensor_tensor(y[:, p, t], o[:, t, 0:D], rden[:, p, t],
                                                       tile_of(Y if cross else R, u, t), ALU.mult, ALU.add)
                i.then_inc(s_y, 1)
                done(dve, s_y, u)
                n_out.vector_moments(dve, u, p, lambda t: y[:, p, t])

            def finish(u, p):
                n_out.vector_apply(dve, u, p, lambda t: y[:, p, t], lambda t: (y[:, p, t],))
                done(dve, n_out.s_out, u)
                affine(net, dve, u, y[:, p], "a3_g" + i2, "a3_c" + i2, s_g, s_b, pair(Y, u))

            if cross:
                pipeline(dve, NU, [(10, finish), (2, take_v), (8, add_z), (0, copy_in), (2, take_scores),
                                   (3, softmax)])
            else:
                pipeline(dve, NU, [(2, apply_in), (1, moments_in), (11, finish), (3, take_v), (9, add_z),
                                   (3, take_scores), (0, lambda u, p: combine.add_weighted(dve, u)),
                                   (4, softmax)])

        @block.scalar
        def _(act):
            act.wait_ge(s_zero, 1)

            def take_xt(u, p):
                done(act, s_xt, u)
                free(act, s_v, u)
                nc.scalar.activation(xT[:, p, :], pX[:, 0:2 * P], ACT.Copy).then_inc(s_xts, 1)

            def take_qk(u, p):
                done(act, s_qk, u)
                free(act, s_S, u)
                nc.scalar.activation(qk[:, p].rearrange("p a t -> p (a t)"), pQ[:, :], ACT.Copy
                                     ).then_inc(s_qks, 1)

            def exps(u, p):
                done(act, s_sub, u)
                free(act, s_pt, u)
                for b in range(2):
                    r = slice(64 * b, 64 * b + 64)
                    i = nc.scalar.activation(Pr[r, p, :, r], pad[r, p], ACT.Exp, scale=SCALE)
                i.then_inc(s_exp, 1)

            def take_pt(u, p):
                done(act, s_pt, u)
                free(act, s_o, u)
                nc.scalar.activation(PT[:, p].rearrange("p a t -> p (a t)"), pT[:, 0:2 * P], ACT.Copy
                                     ).then_inc(s_pts, 1)

            pipeline(act, NU, [(1, take_xt), (7, take_pt), (1, take_qk), (4, exps)])

        @block.tensor
        def _(pe):
            pe.wait_ge(s_ones, 1)

            def transpose_x(u, p):
                done(pe, s_in, u)
                free(pe, s_xts, u, bufs=1)
                for t in range(2):
                    i = nc.tensor.transpose(pX[:, P * t:P * t + P], xs[:, p, t], w("ident"))
                i.then_inc(s_xt, 1)

            def project(u, p):
                done(pe, s_xts, u)
                free(pe, s_qks, u, bufs=1)
                if cross:
                    landed(pe, s_cT, u, p)
                    other = cT[:, p].rearrange("p a t -> p (a t)")
                else:
                    other = xT[:, p, :]
                nc.tensor.matmul(pQ[:, 0:2 * P], w("a3_wq" + i2), xT[:, p, :], start=True, stop=True)
                nc.tensor.matmul(pQ[:, 2 * P:4 * P], w("a3_wk" + i2), other, start=True, stop=True
                                 ).then_inc(s_qk, 1)
                free(pe, s_vs, u, bufs=1)
                for t in range(2):
                    i = nc.tensor.matmul(pV[:, P * t:P * t + P], other[:, P * t:P * t + P],
                                         w("a3_wv" + i2), start=True, stop=True)
                i.then_inc(s_v, 1)

            def scores(u, p):
                done(pe, s_qks, u)
                free(pe, s_Se, u, bufs=1)
                for t in range(2):
                    for b in range(2):
                        c = slice(P * t + T * b, P * t + T * b + T)
                        i = nc.tensor.matmul(pS[T * b:T * b + T, T * t:T * t + T], qk[:, p, 0, c],
                                             qk[:, p, 1, c], start=True, stop=True)
                i.then_inc(s_S, 1)

            def first_rows(u, p):
                done(pe, s_nz, u)
                free(pe, s_len, u, bufs=1)
                nc.tensor.matmul(pL[:, 0:2 * T], w("sel0"), nz[:, p].rearrange("p a k -> p (a k)"),
                                 start=True, stop=True).then_inc(s_L, 1)

            def transpose_p(u, p):
                done(pe, s_exp, u)
                free(pe, s_pts, u, bufs=1)
                for t in range(2):
                    i = nc.tensor.transpose(pT[:, P * t:P * t + P], Pr[:, p, t], w("ident"))
                i.then_inc(s_pt, 1)

            def product_v(u, p):
                done(pe, s_pts, u)
                done(pe, s_vs, u)
                free(pe, s_y, u, bufs=1)
                for t in range(2):
                    i = nc.tensor.matmul(pO[:, (D + 1) * t:(D + 1) * (t + 1)], PT[:, p, t], tile_of(V, u, t),
                                         start=True, stop=True)
                i.then_inc(s_o, 1)

            pipeline(pe, NU, [(8, product_v), (7, transpose_p), (1, transpose_x), (2, scores),
                              (3, first_rows), (1, project)])


def mlp3_steps(net, sb, ps, sem):
    nc, X, Y, w = net.nc, net.X, net.Y, net.w
    xs, xT, h, y = sb("xs", [P, 2, 2, D]), sb("xT", [P, 2, 2 * P]), sb("h", [P, 2, 2 * P]), sb("y", [P, 2, 2, D])
    pX, pH, pO = ps("pX", [P, 512]), ps("pH", [P, 512]), ps("pO", [P, 512])
    s_xs, s_xt, s_xts, s_h, s_hs, s_o, s_y1, s_y, s_g, s_b, s_x = [sem(n) for n in (
        "xs", "xt", "xt_out", "h", "h_out", "o", "y1", "y", "gain", "bias", "x")]
    norm = PairNorm(net, sb, sem, "norm")

    def gpsimd_steps(pool):
        norm.setup(pool)
        return [(4, lambda u, p: norm.pool_rstd(pool, u, p))]

    def vector_steps(dve):
        def copy_in(u, p):
            free(dve, s_xt, u)
            nc.vector.tensor_copy(xs[:, p], pair(Y, u)).then_inc(s_xs, 1)

        def add_h(u, p):
            done(dve, s_o, u)
            free(dve, s_x, u)
            nc.vector.tensor_tensor(y[:, p], pO[:, 0:2 * D].rearrange("p (a d) -> p a d", a=2),
                                    pair(Y, u), ALU.add).then_inc(s_y1, 1)
            done(dve, s_y1, u)
            nc.vector.tensor_tensor(y[:, p], y[:, p], w("a3_b2").unsqueeze(1).broadcast_to([P, 2, D]),
                                    ALU.add).then_inc(s_y, 1)
            done(dve, s_y, u)
            norm.vector_moments(dve, u, p, lambda t: y[:, p, t])

        def finish(u, p):
            if not isinstance(u, int):
                done(dve, s_x, u - 1)
            norm.vector_apply(dve, u, p, lambda t: y[:, p, t], lambda t: (y[:, p, t],))
            done(dve, norm.s_out, u)
            affine(net, dve, u, y[:, p], "a3_g3", "a3_c3", s_g, s_b, y[:, p])
            done(dve, s_b, u)
            nc.vector.tensor_tensor(pair(X, u), pair(X, u), y[:, p], ALU.add).then_inc(s_x, 1)

        return [(0, copy_in), (4, add_h), (5, finish)]

    def scalar_steps(act):
        def take_xt(u, p):
            done(act, s_xt, u)
            free(act, s_h, u)
            nc.scalar.activation(xT[:, p, :], pX[:, 0:2 * P], ACT.Copy).then_inc(s_xts, 1)

        def relu(u, p):
            done(act, s_h, u)
            free(act, s_o, u)
            nc.scalar.activation(h[:, p, :], pH[:, 0:2 * P], ACT.Relu, bias=w("a3_b1")).then_inc(s_hs, 1)

        return [(2, relu), (1, take_xt)]

    def tensor_steps(pe):
        def transpose_x(u, p):
            done(pe, s_xs, u)
            free(pe, s_xts, u, bufs=1)
            for t in range(2):
                i = nc.tensor.transpose(pX[:, P * t:P * t + P], xs[:, p, t], w("ident"))
            i.then_inc(s_xt, 1)

        def hidden(u, p):
            done(pe, s_xts, u)
            free(pe, s_hs, u, bufs=1)
            nc.tensor.matmul(pH[:, 0:2 * P], w("a3_fc1"), xT[:, p, :], start=True, stop=True
                             ).then_inc(s_h, 1)

        def output(u, p):
            done(pe, s_hs, u)
            free(pe, s_y1, u, bufs=1)
            for t in range(2):
                i = nc.tensor.matmul(pO[:, D * t:D * t + D], h[:, p, P * t:P * t + P], w("a3_fc2"),
                                     start=True, stop=True)
            i.then_inc(s_o, 1)

        return [(3, output), (2, hidden), (1, transpose_x)]

    return (gpsimd_steps, vector_steps, scalar_steps, tensor_steps), s_x


def shift3_steps(net, sb, ps, sem, x_ready):
    nc, X, w = net.nc, net.X, net.w
    xs = sb("xs", [P, 2, 2, D])
    xT = sb("xT", [P, 2, 4, T + 1])
    mu = sb("mu", [P, 4])
    part = sb("part", [P, 2, 2, 4, T])
    mix = sb("mix", [P, 2, 2, 4, T])
    r, k1, k2, o = [sb(n, [P, 2, 2 * D]) for n in ("r", "k1", "k2", "o")]
    pX, pR, pK, pW = [ps(n, [P, 512]) for n in ("pX", "pR", "pK", "pW")]
    s_mu, s_zero, s_xt, s_xts, s_part, s_mix, s_r, s_rs, s_k, s_k1, s_k2, s_w, s_o, s_x = [
        sem(n) for n in ("mu", "zero", "xt", "xt_out", "part", "mix", "r", "r_out", "k", "k1", "k2",
                         "w", "o", "x")]
    norm = PairNorm(net, sb, sem, "norm", s_xt)

    def gpsimd_steps(pool):
        nc.gpsimd.memset(xT[:, :, :, 0:1], 0.0).then_inc(s_zero, 1)
        norm.setup(pool)
        return [(0, lambda u, p: norm.pool_rstd(pool, u, p))]

    def vector_steps(dve):
        for n, m in enumerate(("f3_mr", "f3_mk")):
            nc.vector.tensor_copy(mu[:, n:n + 1], w(m))
            nc.vector.tensor_scalar(mu[:, n + 2:n + 3], w(m), -1.0, 1.0, ALU.mult, ALU.add
                                    ).then_inc(s_mu, 1)
        dve.wait_ge(s_mu, 2)
        dve.wait_ge(s_zero, 1)

        def mixes(u, p):
            done(dve, s_xts, u)
            free(dve, s_k, u)
            for n in range(2):
                i = nc.vector.tensor_scalar(part[:, p, n], xT[:, p, :, 0:T], mu[:, n + 2:n + 3], None,
                                            ALU.mult)
            i.then_inc(s_part, 1)
            done(dve, s_part, u)
            for n in range(2):
                i = nc.vector.scalar_tensor_tensor(mix[:, p, n], xT[:, p, :, 1:T + 1], mu[:, n:n + 1],
                                                   part[:, p, n], ALU.mult, ALU.add)
            i.then_inc(s_mix, 1)

        def finish(u, p):
            done(dve, s_w, u)
            done(dve, s_rs, u)
            nc.vector.tensor_tensor(o[:, p, :], pW[:, 0:2 * D], r[:, p, :], ALU.mult).then_inc(s_o, 1)
            done(dve, s_o, u)
            nc.vector.tensor_tensor(pair(X, u), pair(X, u), o[:, p, :].rearrange("p (a d) -> p a d", a=2),
                                    ALU.add).then_inc(s_x, 1)

        def moments(u, p):
            if isinstance(u, int):
                done(dve, x_ready, u)
            norm.vector_moments(dve, u, p, lambda t: tile_of(X, u, t))

        def apply(u, p):
            norm.vector_apply(dve, u, p, lambda t: tile_of(X, u, t), lambda t: (xs[:, p, t],))

        return [(0, moments), (5, finish), (1, apply), (2, mixes)]

    def scalar_steps(act):
        def take_xt(u, p):
            done(act, s_xt, u)
            free(act, s_mix, u)
            nc.scalar.activation(xT[:, p, :, 1:T + 1], pX[:, 0:2 * P].rearrange("p (b t) -> p b t", t=T),
                                 ACT.Copy).then_inc(s_xts, 1)

        def gates(u, p):
            done(act, s_r, u)
            free(act, s_o, u)
            nc.scalar.activation(r[:, p, :], pR[:, 0:2 * D], ACT.Sigmoid).then_inc(s_rs, 1)
            done(act, s_k, u)
            free(act, s_w, u)
            nc.scalar.activation(k1[:, p, :], pK[:, 0:2 * D], ACT.Relu).then_inc(s_k1, 1)
            done(act, s_k1, u)
            nc.scalar.activation(k2[:, p, :], k1[:, p, :], ACT.Square).then_inc(s_k2, 1)

        return [(1, take_xt), (3, gates)]

    def tensor_steps(pe):
        def transpose_x(u, p):
            done(pe, norm.s_out, u)
            free(pe, s_xts, u, bufs=1)
            for t in range(2):
                i = nc.tensor.transpose(pX[:, P * t:P * t + P], xs[:, p, t], w("ident"))
            i.then_inc(s_xt, 1)

        def project(u, p):
            done(pe, s_mix, u)
            free(pe, s_rs, u, bufs=1)
            m = mix[:, p].rearrange("p n b t -> p n (b t)")
            for t in range(2):
                i = nc.tensor.matmul(pR[:, D * t:D * t + D], m[:, 0, P * t:P * t + P], w("f3_wr"),
                                     start=True, stop=True)
            i.then_inc(s_r, 1)
            free(pe, s_k1, u, bufs=1)
            nc.tensor.matmul(pK[:, 0:2 * P], w("f3_wk"), m[:, 1, :], start=True, stop=True
                             ).then_inc(s_k, 1)

        def output(u, p):
            done(pe, s_k2, u)
            free(pe, s_o, u, bufs=1)
            for t in range(2):
                i = nc.tensor.matmul(pW[:, D * t:D * t + D], k2[:, p, P * t:P * t + P], w("f3_wv"),
                                     start=True, stop=True)
            i.then_inc(s_w, 1)

        return [(1, transpose_x), (4, output), (3, project)]

    return gpsimd_steps, vector_steps, scalar_steps, tensor_steps


def mlp_shift3_stage(net):
    nc = net.nc
    BEHIND = 6
    with ExitStack() as ctx:
        sb, ps, sem = opener(net, ctx, "m3")

        def named(alloc, part):
            return lambda name, *more: alloc(part + "_" + name, *more)
        mlp, x_ready = mlp3_steps(net, *[named(a, "mlp") for a in (sb, ps, sem)])
        shift = shift3_steps(net, *[named(a, "shift") for a in (sb, ps, sem)], x_ready)
        block = ctx.enter_context(nc.Block())

        def both(engine, n):
            first = mlp[n](engine)
            return first + [(lag + BEHIND, fn) for lag, fn in shift[n](engine)]

        @block.sync
        def _(sp):
            clear_stale(net, sp)

        @block.gpsimd
        def _(pool):
            pipeline(pool, NU, both(pool, 0))

        @block.vector
        def _(dve):
            pipeline(dve, NU, both(dve, 1))

        @block.scalar
        def _(act):
            pipeline(act, NU, both(act, 2))

        @block.tensor
        def _(pe):
            pipeline(pe, NU, both(pe, 3))


class Routing:

    def __init__(self, net, first):
        nc, ctx = net.nc, net.ctx
        name = "r1" if first else "r2"

        def sb(n, shape, dt=F32):
            return ctx.enter_context(nc.sbuf_tensor(f"{name}_{n}", shape, dt))
        self.first = first

        self.s_put = net.software_sems.pop()
        self.s_got = [net.software_sems.pop() for _ in range(IN_FLIGHT)]
        self.logits = sb("logits", [P, NT, E])
        self.weight = sb("weight", [P, TOPK, NT])
        self.put = sb("put", [P, TOPK, NT], U32)
        self.get = self.put if first else sb("get", [P, TOPK, NT], U32)
        self.expert = sb("expert", [P, NCH1], I32) if first else None


def logits_stage(net, rt):
    nc, X, R, w = net.nc, net.X, net.R, net.w
    with ExitStack() as ctx:
        sb, ps, sem = opener(net, ctx, "g1" if rt.first else "g2")
        xn, xT = sb("xn", [P, 2, 2, D]), sb("xT", [P, 2, 2 * P])
        pX, pL = ps("pX", [P, 512]), ps("pL", [P, 512])
        s_xt, s_xts, s_l, s_ls, s_r = [sem(n) for n in ("xt", "xt_out", "logits", "logits_out", "kept")]
        norm = PairNorm(net, sb, sem, "norm", s_xt)
        block = ctx.enter_context(nc.Block())

        @block.sync
        def _(sp):
            clear_stale(net, sp)

        @block.gpsimd
        def _(pool):
            norm.setup(pool)
            pipeline(pool, NU, [(0, lambda u, p: norm.pool_rstd(pool, u, p))])

        @block.vector
        def _(dve):
            def moments(u, p):
                norm.vector_moments(dve, u, p, lambda t: tile_of(X, u, t))

            def apply(u, p):
                free(dve, s_r, u)
                norm.vector_apply(dve, u, p, lambda t: tile_of(X, u, t), lambda t: (xn[:, p, t],))

            def keep(u, p):
                done(dve, norm.s_out, u)
                nc.vector.tensor_copy(pair(R, u), xn[:, p]).then_inc(s_r, 1)

            def take_logits(u, p):
                done(dve, s_l, u)
                out, src = pair(rt.logits, u), pL[:, 0:2 * E].rearrange("p (a e) -> p a e", a=2)
                if rt.first:
                    i = nc.vector.tensor_copy(out, src)
                else:
                    i = nc.vector.tensor_tensor(out, src, w("f2_br").unsqueeze(1).broadcast_to([P, 2, E]),
                                                ALU.add)
                i.then_inc(s_ls, 1)

            pipeline(dve, NU, [(0, moments), (1, apply), (4, take_logits), (2, keep)])

        @block.scalar
        def _(act):
            def take_xt(u, p):
                done(act, s_xt, u)
                free(act, s_l, u)
                nc.scalar.activation(xT[:, p, :], pX[:, 0:2 * P], ACT.Copy).then_inc(s_xts, 1)
            pipeline(act, NU, [(2, take_xt)])

        @block.tensor
        def _(pe):
            def transpose_x(u, p):
                done(pe, norm.s_out, u)
                free(pe, s_xts, u, bufs=1)
                for t in range(2):
                    i = nc.tensor.transpose(pX[:, P * t:P * t + P], xn[:, p, t], w("ident"))
                i.then_inc(s_xt, 1)

            def gate(u, p):
                done(pe, s_xts, u)
                free(pe, s_ls, u, bufs=1)
                for t in range(2):
                    i = nc.tensor.matmul(pL[:, E * t:E * t + E], xT[:, p, P * t:P * t + P],
                                         w("f1_gate" if rt.first else "f2_wr"), start=True, stop=True)
                i.then_inc(s_l, 1)

            pipeline(pe, NU, [(3, gate), (2, transpose_x)])


def route_stage(net, rt):
    nc, R, Y, w = net.nc, net.R, net.Y, net.w
    first = rt.first
    xg = net.dram["slots_in"]
    NE = NT * E
    with ExitStack() as ctx:
        sb, ps, sem = opener(net, ctx, "t1" if first else "t2")
        L = rt.logits
        m = [sb(f"m{k}", [P, NT, 1]) for k in range(2)]
        pos, pm = sb("pos", [P, NT, E]), sb("pm", [P, NT, 1])
        sel = [sb(f"sel{k}", [P, NT, E]) for k in range(2)]
        both = sb("both", [P, NT, E])
        less = sb("less", [P, NT, E])
        scan = [sb(f"scan{k}", [P, NT, E]) for k in range(2)]
        tot = sb("tot", [P, NT, E])
        rank = sb("rank", [P, NT, E])
        keep = sb("keep", [P, NT, E])
        t3 = sb("t3", [P, NT, E])
        ex = sb("ex", [P, NT, E])
        den = sb("den", [P, NT, 1])
        inv = sb("inv", [P, NT, 1])
        gap = sb("gap", [P, NT, 1])
        egap = sb("egap", [P, NT, 1])
        slotf = sb("slotf", [P, TOPK, NT, 1])
        keptf = sb("keptf", [P, TOPK, NT, 1])
        dumpf = sb("dumpf", [P, TOPK, NT, 1])
        ends = [sb(f"ends{k}", [P, 1, E]) for k in range(2)]
        padded = sb("padded", [P, 1, E])
        base = sb("base", [P, 1, E])
        passed = sb("passed", [P, NCH1, E])
        expf = sb("expf", [P, NCH1, 1])
        pP, pT = ps("pP", [P, 512]), ps("pT", [P, 512])
        s_v = sem("vector")
        s_sel, s_cnt, s_arg, s_exp, s_idx, s_rows = [sem(n) for n in (
            "selected", "counted", "exp_args", "exps", "indices", "rows")]
        s_put = rt.s_put
        block = ctx.enter_context(nc.Block())

        @block.sync
        def _(sp):
            clear_stale(net, sp)
        wide = [P, NT, E]

        @block.vector
        def _(dve):
            count = [0]

            def then(i):
                i.then_inc(s_v, 1)
                count[0] += 1
                dve.wait_ge(s_v, count[0])

            v = nc.vector
            ranks8 = w("rank8").unsqueeze(1).broadcast_to(wide)
            src = L
            for k in range(2):
                then(v.tensor_reduce(m[k][:, :, 0], src[:, :, :], AX, ALU.max))
                then(v.tensor_tensor(pos[:, :, :], src[:, :, :], m[k][:, :, :].broadcast_to(wide), ALU.is_equal))
                then(v.tensor_tensor(pos[:, :, :], pos[:, :, :], ranks8, ALU.mult))
                then(v.tensor_reduce(pm[:, :, 0], pos[:, :, :], AX, ALU.max))
                then(v.tensor_tensor(sel[k][:, :, :], pos[:, :, :], pm[:, :, :].broadcast_to(wide), ALU.is_equal))
                if k == 0:
                    then(v.scalar_tensor_tensor(less[:, :, :], sel[0][:, :, :], -3e38, L[:, :, :],
                                                ALU.mult, ALU.add))
                    src = less
            v.tensor_tensor(both[:, :, :], sel[0][:, :, :], sel[1][:, :, :], ALU.add).then_inc(s_sel, 1)
            if first:
                then(v.tensor_tensor(ex[:, :, :], L[:, :, :], m[0][:, :, :].broadcast_to(wide), ALU.subtract))
            v.tensor_tensor(gap[:, :, :], m[1][:, :, :], m[0][:, :, :], ALU.subtract).then_inc(s_arg, 1)

            dve.wait_ge(s_cnt, 1)
            then(v.tensor_copy(tot[:, :, :], pT[:, 0:NE].rearrange("p (n e) -> p n e", e=E)))
            a = tot
            for n, d in enumerate((1, 2, 4, 8, 16)):
                b = scan[n % 2]
                v.tensor_copy(b[:, 0:d], a[:, 0:d])
                then(v.tensor_tensor(b[:, d:], a[:, d:], a[:, 0:NT - d], ALU.add))
                a = b
            then(v.tensor_tensor(t3[:, :, :], a[:, :, :], tot[:, :, :], ALU.subtract))
            then(v.tensor_tensor(rank[:, :, :], pP[:, 0:NE].rearrange("p (n e) -> p n e", e=E), t3[:, :, :],
                                 ALU.add))
            if first:
                counts = a[:, NT - 1:NT, :]
                then(v.tensor_scalar(padded[:, :, :], counts, 1.0 / CHUNK,
                                     (CHUNK - 1.0) / CHUNK - 0.5 + 0.5 / CHUNK, ALU.mult, ALU.add))
                then(v.tensor_scalar(padded[:, :, :], padded[:, :, :], 8388608.0, -8388608.0, ALU.add, ALU.add))
                then(v.tensor_scalar(padded[:, :, :], padded[:, :, :], float(CHUNK), None, ALU.mult))
                a = padded
                for n, d in enumerate((1, 2, 4)):
                    b = ends[n % 2]
                    v.tensor_copy(b[:, :, 0:d], a[:, :, 0:d])
                    then(v.tensor_tensor(b[:, :, d:], a[:, :, d:], a[:, :, 0:E - d], ALU.add))
                    a = b
                then(v.tensor_tensor(base[:, :, :], a[:, :, :], padded[:, :, :], ALU.subtract))
                then(v.tensor_tensor(passed[:, :, :], w("chunk0").unsqueeze(2).broadcast_to([P, NCH1, E]),
                                     a[:, :, :].broadcast_to([P, NCH1, E]), ALU.is_ge))
                then(v.tensor_reduce(expf[:, :, 0], passed[:, :, :], AX, ALU.add))
                then(v.tensor_scalar(rt.expert[:, :], expf[:, :, 0], float(E - 1), None, ALU.min))
                then(v.tensor_tensor(rank[:, :, :], rank[:, :, :], base[:, :, :].broadcast_to(wide), ALU.add))
            else:
                then(v.tensor_scalar(keep[:, :, :], rank[:, :, :], float(CAP), None, ALU.is_lt))
                then(v.tensor_scalar(base[:, 0, :], w("iota8"), float(CAP), None, ALU.mult))
                then(v.tensor_tensor(rank[:, :, :], rank[:, :, :], base[:, :, :].broadcast_to(wide), ALU.add))
            for k in range(2):
                then(v.tensor_tensor(t3[:, :, :], sel[k][:, :, :], rank[:, :, :], ALU.mult))
                then(v.tensor_reduce(slotf[:, k, :, 0], t3[:, :, :], AX, ALU.add))
                if not first:
                    then(v.tensor_tensor(t3[:, :, :], sel[k][:, :, :], keep[:, :, :], ALU.mult))
                    then(v.tensor_reduce(keptf[:, k, :, 0], t3[:, :, :], AX, ALU.add))
            if not first:
                then(v.tensor_tensor(slotf[:, :, :, :], slotf[:, :, :, :], keptf[:, :, :, :], ALU.mult))
                then(v.tensor_copy(rt.get[:, :, :], slotf[:, :, :, 0]))
                then(v.tensor_scalar(dumpf[:, :, :, :], keptf[:, :, :, :], -1.0, 1.0, ALU.mult, ALU.add))
                spare = w("spare").rearrange("p (k n) -> p k n", k=TOPK).unsqueeze(3)
                then(v.tensor_tensor(dumpf[:, :, :, :], dumpf[:, :, :, :], spare, ALU.mult))
                then(v.tensor_tensor(slotf[:, :, :, :], slotf[:, :, :, :], dumpf[:, :, :, :], ALU.add))
            v.tensor_copy(rt.put[:, :, :], slotf[:, :, :, 0]).then_inc(s_idx, 1)

            dve.wait_ge(s_exp, 1)
            if first:
                then(v.tensor_reduce(den[:, :, 0], ex[:, :, :], AX, ALU.add))
            else:
                then(v.tensor_scalar(den[:, :, :], egap[:, :, :], 1.0, None, ALU.add))
            then(v.reciprocal(inv[:, :, :], den[:, :, :]))
            wt = rt.weight
            v.tensor_copy(wt[:, 0, :], inv[:, :, 0])
            then(v.tensor_tensor(wt[:, 1, :], egap[:, :, 0], inv[:, :, 0], ALU.mult))
            if first:
                then(v.tensor_tensor(Y[:, :, :], R[:, :, :], wt[:, 0, :].unsqueeze(2).broadcast_to([P, NT, D]),
                                     ALU.mult))
                v.tensor_tensor(R[:, :, :], R[:, :, :], wt[:, 1, :].unsqueeze(2).broadcast_to([P, NT, D]),
                                ALU.mult).then_inc(s_rows, 1)
            else:
                v.tensor_tensor(wt[:, :, :], wt[:, :, :], keptf[:, :, :, 0], ALU.mult).then_inc(s_rows, 1)

        @block.scalar
        def _(act):
            act.wait_ge(s_arg, 1)
            if first:
                nc.scalar.activation(ex[:, :, :], ex[:, :, :], ACT.Exp)
            nc.scalar.activation(egap[:, :, :], gap[:, :, :], ACT.Exp).then_inc(s_exp, 1)

        @block.tensor
        def _(pe):
            pe.wait_ge(s_sel, 1)
            flat = both[:, :, :].rearrange("p n e -> p (n e)")
            nc.tensor.matmul(pP[:, 0:NE], w("tri"), flat, start=True, stop=True)
            nc.tensor.matmul(pT[:, 0:NE], w("ones"), flat, start=True, stop=True).then_inc(s_cnt, 1)

        @block.gpsimd
        def _(pool):
            pool.wait_ge(s_idx, 1)
            pool.wait_ge(s_rows, 1)
            for n in range(NT):
                for k in range(TOPK):
                    rows = (Y if k == 0 else R) if first else R
                    nc.gpsimd.indirect_dma_start(
                        xg[:, :], bass.IndirectOffsetOnAxis(ap=rt.put[:, k, n:n + 1], axis=0),
                        rows[:, n, :], None).then_inc(s_put, 16)
            pool.wait_ge(s_put, 16 * TOPK * NT)


def experts_stage(net, rt):
    nc, w = net.nc, net.w
    first = rt.first
    n = NCH1 if first else NCH2
    HC = (HID1P if first else HID2) // P
    UP = 2 * HID1P if first else HID2
    WB = UP + HC * D + (0 if first else HC + D)
    banks = HC if first else HC // 2
    xg, yg = net.dram["slots_in"], net.dram["slots_out"]
    weights = net.dram["f1" if first else "f2"]
    NSL = CHUNK // P
    with ExitStack() as ctx:
        sb, ps, sem = opener(net, ctx, "e1" if first else "e2")
        up = sb("w_up", [P, 2, UP])
        down = sb("w_down", [P, 2, WB - UP])
        rows = sb("rows", [P, 2, NSL, D])
        xT = sb("xT", [P, 2, CHUNK])
        act_out = sb("silu", [P, 2, HC, CHUNK]) if first else None
        h = sb("h", [P, 2, HC, CHUNK])
        y = sb("y", [P, 2, NSL, D])
        H = ps("H", [P, 2 * banks, 512])
        pX, pY = ps("pX", [P, 512]), ps("pY", [P, 512])
        s_up, s_down = [sem("up_even"), sem("up_odd")], [sem("down_even"), sem("down_odd")]
        s_r = [sem("rows_even"), sem("rows_odd")]
        s_out = [sem("out_even"), sem("out_odd")]
        s_xt, s_xts, s_h, s_a, s_hs, s_y, s_ys = [sem(m) for m in (
            "xt", "xt_out", "hidden", "silu", "hidden_out", "y", "y_out")]
        block = ctx.enter_context(nc.Block())

        @block.sync
        def _(sp):
            clear_stale(net, sp)
            def chunk_rows(t, u):
                r = t[0:n * CHUNK, :].rearrange("(c s p) d -> c p s d", s=NSL, p=P)
                return r[u]

            def load_rows(u, p):
                free(sp, s_xt, u)
                sp.dma_start(rows[:, p], chunk_rows(xg, u)).then_inc(s_r[p], 16)

            def expert_weights(u):
                if first:
                    col = rt.expert[0:1, u:u + 1] if isinstance(u, int) else rt.expert[0:1, bass.ds(u, 1)]
                    e = sp.value_load(col, min_val=0, max_val=E - 1)
                else:
                    e = u // (CAP // CHUNK)
                return weights[bass.ds(e, 1)].rearrange("a p n -> p (a n)")

            def load_up(u, p):
                src = expert_weights(u)
                free(sp, s_h, u, per=banks)
                sp.dma_start(up[:, p, :], src[:, 0:UP]).then_inc(s_up[p], 16)

            def load_down(u, p):
                src = expert_weights(u)
                free(sp, s_y if first else s_ys, u)
                sp.dma_start(down[:, p, :], src[:, UP:WB]).then_inc(s_down[p], 16)

            def store(u, p):
                done(sp, s_ys, u)
                sp.dma_start(chunk_rows(yg, u), y[:, p]).then_inc(s_out[p], 16)

            pipeline(sp, n, [(3, load_down), (0, load_rows), (1, load_up), (5, store)])
            for p in range(2):
                sp.wait_ge(s_out[p], 16 * (n // 2))

        @block.vector
        def _(dve):
            def take_xt(u, p):
                done(dve, s_xt, u)
                free(dve, s_h, u, per=banks)
                nc.vector.tensor_copy(xT[:, p, :], pX[:, 0:CHUNK]).then_inc(s_xts, 1)

            def gate(u, p):
                for b in range(banks):
                    dve.wait_ge(s_a, banks * u + (b + 1))
                    if b == 0:
                        free(dve, s_y, u)
                    nc.vector.tensor_tensor(h[:, p, b, :], act_out[:, p, b, :],
                                            H[:, banks * p + b, CHUNK:2 * CHUNK], ALU.mult
                                            ).then_inc(s_hs, 1)

            def take_y(u, p):
                done(dve, s_y, u)
                if not first:
                    landed(dve, s_down, u, p)
                stored = s_out[p]
                if not (isinstance(u, int) and u < 2):
                    dve.wait_ge(stored, 8 * u - 8 * p)
                src = pY[:, 0:NSL * D].rearrange("p (s d) -> p s d", d=D)
                if first:
                    i = nc.vector.tensor_copy(y[:, p], src)
                else:
                    b2 = down[:, p, HC * D + HC:].unsqueeze(1).broadcast_to([P, NSL, D])
                    i = nc.vector.tensor_tensor(y[:, p], src, b2, ALU.add)
                i.then_inc(s_ys, 1)

            if first:
                pipeline(dve, n, [(2, take_xt), (5, take_y), (3, gate)])
            else:
                pipeline(dve, n, [(5, take_y), (1, take_xt)])

        @block.scalar
        def _(act):
            def silu(u, p):
                for b in range(banks):
                    act.wait_ge(s_h, banks * u + (b + 1))
                    if b == 0:
                        free(act, s_hs, u, per=banks)
                    nc.scalar.activation(act_out[:, p, b, :], H[:, banks * p + b, 0:CHUNK], ACT.Silu
                                         ).then_inc(s_a, 1)

            def gelu(u, p):
                landed(act, s_down, u, p)
                for b in range(banks):
                    act.wait_ge(s_h, banks * u + (b + 1))
                    if b == 0:
                        free(act, s_y, u)
                    for c in range(2):
                        hc = 2 * b + c
                        i = nc.scalar.activation(h[:, p, hc, :], H[:, banks * p + b, CHUNK * c:CHUNK * (c + 1)],
                                                 ACT.Gelu, bias=down[:, p, HC * D + hc:HC * D + hc + 1])
                    i.then_inc(s_hs, 1)

            pipeline(act, n, [(3, silu if first else gelu)])

        @block.tensor
        def _(pe):
            def transpose_x(u, p):
                landed(pe, s_r, u, p)
                free(pe, s_xts, u, bufs=1)
                for s in range(NSL):
                    i = nc.tensor.transpose(pX[:, P * s:P * s + P], rows[:, p, s, :], w("ident"))
                i.then_inc(s_xt, 1)

            def hidden(u, p):
                done(pe, s_xts, u)
                landed(pe, s_up, u, p)
                free(pe, s_hs, u, per=banks)
                for b in range(banks):
                    for c in range(2):
                        at = HID1P * c + P * b if first else P * (2 * b + c)
                        i = nc.tensor.matmul(H[:, banks * p + b, CHUNK * c:CHUNK * (c + 1)],
                                             up[:, p, at:at + P], xT[:, p, :], start=True, stop=True)
                    i.then_inc(s_h, 1)

            def output(u, p):
                done(pe, s_hs, u, per=banks)
                landed(pe, s_down, u, p)
                free(pe, s_ys, u, bufs=1)
                for s in range(NSL):
                    for c in range(HC):
                        i = nc.tensor.matmul(pY[:, D * s:D * s + D], h[:, p, c, P * s:P * s + P],
                                             down[:, p, D * c:D * (c + 1)],
                                             start=(c == 0), stop=(c == HC - 1))
                i.then_inc(s_y, 1)

            pipeline(pe, n, [(5, output), (2, transpose_x), (3, hidden)])


class Combine:

    def __init__(self, net, rt, sem):
        self.net, self.rt = net, rt
        self.s_here, self.s_weighted, self.s_first, self.s_x = [sem(n) for n in (
            "rows_here", "rows_weighted", "first_row_added", "rows_added")]

    def gather(self, u):
        rt, net = self.rt, self.net
        rows = net.dram["slots_out"][0:(NCH1 if rt.first else NCH2) * CHUNK, :]
        for k, t in enumerate((net.Y, net.R)):
            net.nc.gpsimd.indirect_dma_start(
                t[:, u, :], None, rows, bass.IndirectOffsetOnAxis(ap=rt.get[:, k, u:u + 1], axis=0)
            ).then_inc(rt.s_got[u % IN_FLIGHT], 16)

    def arrive(self, pool, u):
        pool.wait_ge(self.rt.s_got[u % IN_FLIGHT], 16 * TOPK * (u // IN_FLIGHT + 1))

    def report(self, pool, u, mark):
        for t in (2 * u, 2 * u + 1):
            self.arrive(pool, t)
        self.net.nc.gpsimd.memset(mark, 0.0).then_inc(self.s_here, 1)

    def add_weighted(self, dve, u):
        net, v = self.net, self.net.nc.vector
        rows = (pair(net.Y, u), pair(net.R, u))
        done(dve, self.s_here, u)
        for k, t in enumerate(rows):
            wt = self.rt.weight[:, k, 2 * u:2 * u + 2] if isinstance(u, int) else \
                self.rt.weight[:, k, bass.ds(2 * u, 2)]
            v.tensor_tensor(t, t, wt.unsqueeze(2).broadcast_to([P, 2, D]), ALU.mult
                            ).then_inc(self.s_weighted, 1)
        done(dve, self.s_weighted, u, per=2)
        v.tensor_tensor(pair(net.X, u), pair(net.X, u), rows[0], ALU.add).then_inc(self.s_first, 1)
        done(dve, self.s_first, u)
        v.tensor_tensor(pair(net.X, u), pair(net.X, u), rows[1], ALU.add).then_inc(self.s_x, 1)

    def add(self, pool, u):
        net = self.net
        self.arrive(pool, u)
        x, rows = net.X[:, u, :], (net.Y[:, u, :], net.R[:, u, :])
        net.nc.gpsimd.tensor_tensor(x, x, rows[0], ALU.add).then_inc(self.s_first, 1)
        done(pool, self.s_first, u)
        net.nc.gpsimd.tensor_tensor(x, x, rows[1], ALU.add).then_inc(self.s_x, 1)


def mixture(net, first):
    rt = Routing(net, first)
    logits_stage(net, rt)
    route_stage(net, rt)
    experts_stage(net, rt)
    net.routing = rt


def store_stage(net):
    nc = net.nc
    with ExitStack() as ctx:
        _, _, sem = opener(net, ctx, "out")
        s_out = sem("stored")
        block = ctx.enter_context(nc.Block())

        @block.sync
        def _(sp):
            clear_stale(net, sp)
            sp.dma_start(net.dram["out"].rearrange("(i b) t d -> (b t) i d", b=2), net.X[:, :, :]
                         ).then_inc(s_out, 16)
            sp.wait_ge(s_out, 16)


def feed_forward0(net):
    key_attention0_stage(net)
    norm_gelu_stage(net)


def feed_forward1(net):
    mixture(net, first=True)


def feed_forward2(net):
    mixture(net, first=False)


def attention3(net):
    attention3_stage(net, cross=False)
    attention3_stage(net, cross=True)
LAYERS = (attention0_stage, feed_forward0, attention1_stage, feed_forward1, attention2_stage, feed_forward2,
          attention3, mlp_shift3_stage)


def build(nc, dram):
    with ExitStack() as ctx:
        W = ctx.enter_context(nc.sbuf_tensor("W", [P, PACKW], F32))
        X = ctx.enter_context(nc.sbuf_tensor("X", [P, NT, D], F32))
        net = Net(nc, dram, W, X)
        net.ctx = ctx
        net.software_sems = [ctx.enter_context(nc.semaphore(f"software_dma{k}"))
                             for k in range(2 * (1 + IN_FLIGHT))]
        net.Y = ctx.enter_context(nc.sbuf_tensor("Y", [P, NT, D], F32))
        net.R = ctx.enter_context(nc.sbuf_tensor("R", [P, NT, D], F32))
        net.norms = ctx.enter_context(nc.sbuf_tensor("norms", [P, 2, NT], F32))
        net.s_rest = ctx.enter_context(nc.semaphore("weights_loaded"))
        net.s_fill = ctx.enter_context(nc.semaphore("slots_zeroed"))
        load_stage(net)
        for layer in LAYERS:
            layer(net)
        store_stage(net)


def constants():
    p = np.arange(P)
    one = np.float32
    c = {"ident": np.eye(P, dtype=one), "ones": np.ones((P, P), one)}
    c["maskA"] = (p[:, None] // 8 == np.arange(16)).astype(one)
    c["maskB"] = ((p[:, None] % 64) // 8 == np.arange(8)).astype(one)
    d = p % 8
    theta = (one(1.0) / one(1250) ** (np.arange(0, 4, 2, dtype=one) / one(4))).astype(one)
    ang = np.arange(D, dtype=one)[None, :] * theta[d % 2][:, None]
    rotates = (d < 4)[:, None]
    c["cos"] = np.where(rotates, np.cos(ang), 1).astype(one)
    c["sin"] = np.where(rotates, np.where((d < 2)[:, None], -np.sin(ang), np.sin(ang)), 0).astype(one)
    c["tri"] = (p[:, None] < p[None, :]).astype(one)
    c["sel0"] = (p[:, None] == 64 * (p[None, :] // 64)).astype(one)
    k = np.arange(64)
    c["iota64"] = np.broadcast_to(k, (P, 64)).astype(one)
    q = (p % 64)[:, None]
    c["causal"] = np.where(k[None, :] > q, one(NEG), one(0)).astype(one)
    c["allow1"] = np.where(k[None, :] // 4 <= q, one(0), one(NEG)).astype(one)
    c["rank8"] = np.broadcast_to(8 - np.arange(8), (P, 8)).astype(one)
    c["iota8"] = np.broadcast_to(np.arange(8), (P, 8)).astype(one)
    c["chunk0"] = np.broadcast_to(np.arange(NCH1) * CHUNK, (P, NCH1)).astype(one)
    n = np.arange(TOPK * NT)
    c["spare"] = (NTOK * TOPK + P * n[None, :] + p[:, None]).astype(one)
    return c


def lay_out(inp):
    c = constants()

    def bd(w):
        z = np.zeros((P, P), np.float32)
        z[:64, :64] = w
        z[64:, 64:] = w
        return z

    def rows(v):
        return np.broadcast_to(v[None, :], (P, v.size))

    def col(v):
        return v.reshape(-1, 1)

    turn = np.arange(64).reshape(8, 8)[:, [2, 3, 0, 1, 4, 5, 6, 7]].reshape(-1)
    g = {k: np.asarray(v) for k, v in inp.items()}
    wq, wk = g["L0_xattn_Wq"], g["L0_xattn_Wk"]
    c["a0_wq"], c["a0_wqr"] = bd(wq.T), bd(wq[turn].T)
    c["a0_wk"], c["a0_wkr"] = bd(wk.T), bd(wk[turn].T)
    c["a0_wv"], c["a0_wo"] = bd(g["L0_xattn_Wv"].T), bd(g["L0_xattn_Wo"].T)
    b = [g["L0_xattn_bq"], g["L0_xattn_bq"][turn], g["L0_xattn_bk"], g["L0_xattn_bk"][turn],
         g["L0_xattn_bv"], g["L0_xattn_bo"]]
    c["a0_bias"] = np.stack([np.concatenate([v, v]) for v in b], 1)
    c["f0_wq"], c["f0_wk"], c["f0_wv"] = g["L0_ffn_Wq"], g["L0_ffn_Wk"], g["L0_ffn_Wv"]
    groups = [np.concatenate([g["L0_ffn_Wo"][64 * n:64 * n + 64]] * 2, 0) for n in range(2)]
    c["f0_wo2"], c["f0_woT2"] = np.concatenate(groups, 1), np.concatenate([m.T for m in groups], 1)
    c["f0_wff"] = g["L0_ffn_Wff"]
    for n, m in (("a1_wq", "Wq"), ("a1_wk", "Wk"), ("a1_wv", "Wv"), ("a1_wo", "Wo")):
        c[n] = g["L1_xattn_" + m].T
    for n, m in (("a1_bq", "bq"), ("a1_bk", "bk")):
        v = g["L1_xattn_" + m].reshape(2, 64).T
        c[n] = np.concatenate([v, v], 0)
    c["a1_bv"], c["a1_bo"] = col(g["L1_xattn_bv"]), rows(g["L1_xattn_bo"])
    c["f1_gate"] = g["L1_ffn_gate_w"].T
    c["a2_wq"], c["a2_wk"], c["a2_wv"] = g["L2_xattn_Wq"], g["L2_xattn_Wk"], g["L2_xattn_Wv"]
    c["a2_wo"] = g["L2_xattn_Wo"].reshape(4, P, D).transpose(1, 0, 2).reshape(P, 512)
    c["a2_bo"] = rows(g["L2_xattn_bo"])
    c["f2_wr"], c["f2_br"] = g["L2_ffn_Wr"], rows(g["L2_ffn_br"])
    for m in ("Wq1", "Wk1", "Wv1", "Wq2", "Wk2", "Wv2"):
        c["a3_" + m.lower()] = g["L3_xattn_" + m]
    c["a3_fc1"], c["a3_fc2"] = g["L3_xattn_fc1_w"], g["L3_xattn_fc2_w"]
    c["a3_b1"], c["a3_b2"] = col(g["L3_xattn_fc1_b"]), rows(g["L3_xattn_fc2_b"])
    for i in "123":
        c["a3_g" + i], c["a3_c" + i] = rows(g[f"L3_xattn_ln{i}_g"]), rows(g[f"L3_xattn_ln{i}_b"])
    c["f3_wr"], c["f3_wk"], c["f3_wv"] = g["L3_ffn_W_r"].T, g["L3_ffn_W_k"].T, g["L3_ffn_W_v"].T
    c["f3_mr"], c["f3_mk"] = col(g["L3_ffn_mu_r"]), col(g["L3_ffn_mu_k"])
    wpack = np.ascontiguousarray(np.concatenate([c[n] for n, _ in PACK], 1))
    assert wpack.shape == (P, PACKW), wpack.shape

    ctx = np.ascontiguousarray(g["ctx_1024"])
    f1w = np.zeros((E, P, 2, HID1P), np.float32)
    f1w[:, :, 0, :HID1], f1w[:, :, 1, :HID1] = g["L1_ffn_w1"], g["L1_ffn_w3"]
    f1d = np.zeros((E, HID1P, D), np.float32)
    f1d[:, :HID1] = g["L1_ffn_w2"]
    f1d = f1d.reshape(E, HID1P // P, P, D).transpose(0, 2, 1, 3)
    f2d = g["L2_ffn_W2"].reshape(E, HID2 // P, P, D).transpose(0, 2, 1, 3)
    f1 = np.concatenate([f1w.reshape(E, P, -1), f1d.reshape(E, P, -1)], 2)
    b1 = g["L2_ffn_b1"].reshape(E, HID2 // P, P).transpose(0, 2, 1)
    b2 = np.broadcast_to(g["L2_ffn_b2"][:, None, :], (E, P, D))
    f2 = np.concatenate([g["L2_ffn_W1"], f2d.reshape(E, P, -1), b1, b2], 2)
    return {
        "x": np.ascontiguousarray(g["x"]), "ctx": ctx, "wpack": wpack,
        "ctxT": np.ascontiguousarray(ctx.reshape(NT, P, D).transpose(0, 2, 1)),
        "f1": np.ascontiguousarray(f1), "f2": np.ascontiguousarray(f2),
    }


def kernel(**inputs):
    import concourse.bacc as bacc
    from concourse.bass_utils import run_bass_kernel_spmd

    nc = bacc.Bacc("TRN2", target_bir_lowering=False, num_devices=1)
    arrays = {f"in_{n}_dram": a for n, a in lay_out(inputs).items()}
    dram = {n[3:-5]: nc.dram_tensor(n, a.shape, mybir.dt.from_np(a.dtype), kind="ExternalInput").ap()
            for n, a in arrays.items()}
    dram["out"] = nc.dram_tensor("out_0_dram", (B, T, D), F32, kind="ExternalOutput").ap()
    dram["slots_in"] = nc.dram_tensor("slots_in", (2 * NTOK * TOPK, D), F32).ap()
    dram["slots_out"] = nc.dram_tensor("slots_out", (NCH1 * CHUNK, D), F32).ap()
    build(nc, dram)
    r = run_bass_kernel_spmd(nc, [arrays], core_ids=[0])
    return r.results[0]["out_0_dram"]
```
